# Optimizing a Trainium2 kernel written in Bass

```python
import numpy as np
import jax
import jax.numpy as jnp

def _softmax(x, axis=-1):
    return jax.nn.softmax(x, axis=axis)

def _gelu(x):
    return jax.nn.gelu(x, approximate=True)

def _silu(x):
    return jax.nn.silu(x)

def _sigmoid(x):
    return jax.nn.sigmoid(x)

def _layernorm(x, axis=-1, eps=1e-05):
    m = jnp.mean(x, axis=axis, keepdims=True)
    v = jnp.var(x, axis=axis, keepdims=True)
    return (x - m) / jnp.sqrt(v + eps)

def _scatter_add(tgt, idx, src, axis=0):
    return tgt.at[idx].add(src)

def _segment_sum(src, seg, n):
    return jax.ops.segment_sum(src, seg, n)
kernel_name = 'mk_xattn_ffn_d4_seqx_r8_ebc1c0'

def setup_inputs(seed: int=0):
    np.random.seed(seed)
    _w = jnp.asarray

    def _rec_inputs():
        import jax
        import jax.numpy as jnp
        _rk = jax.random.key(seed)
        x = -0.0002928 + 1 * jax.random.normal(jax.random.fold_in(_rk, 1), (8, 128, 128), jnp.float32)
        _lenS = 128 - jax.random.randint(jax.random.fold_in(_rk, 7), (8,), 0, max(1, 128 // 4) + 1, jnp.int32)
        _lenS2 = 128 - jax.random.randint(jax.random.fold_in(_rk, 8), (8,), 0, max(1, 128 // 4) + 1, jnp.int32)
        _ctx_1024P = jax.random.normal(jax.random.fold_in(_rk, 11), (8, 16, 128), jnp.float32)
        _ctx_1024c = jax.random.dirichlet(jax.random.fold_in(_rk, 511), 0.3 * jnp.ones((16,), jnp.float32), (8, 128))
        _ctx_1024t = jnp.einsum('bsk,bkd->bsd', _ctx_1024c, _ctx_1024P)
        _ctx_1024t = _ctx_1024t * jax.lax.rsqrt(jnp.mean(jnp.square(_ctx_1024t)) + 1e-12) * 0.953939
        ctx_1024 = -1.39393e-06 + 0.999914 * (_ctx_1024t + 0.3 * jax.random.normal(jax.random.fold_in(_rk, 611), (8, 128, 128), jnp.float32))
        return (x, ctx_1024)
    x, ctx_1024 = _rec_inputs()

    def _L0_xattn_setup():
        import jax, jax.numpy as jnp
        import numpy as np
        D_MODEL = 128
        N_HEADS = 16
        D_K = D_MODEL // N_HEADS
        key = jax.random.key(seed)
        kq, kk, kv = jax.random.split(key, 3)
        shape = (2, 256, D_MODEL)
        return {'Q': jax.random.normal(kq, shape, dtype=jnp.float32), 'K': jax.random.normal(kk, shape, dtype=jnp.float32), 'V': jax.random.normal(kv, shape, dtype=jnp.float32)}
    _L0_xattn_all = _L0_xattn_setup()
    _L0_xattn_in = {k: v for k, v in _L0_xattn_all.items() if k in ()}
    del _L0_xattn_all

    def _L0_ffn_setup():
        import jax, jax.numpy as jnp
        import numpy as np
        HIDDEN = 128
        INNER = 512

        def _weight_quant(w):
            scale = 1.0 / jnp.clip(jnp.mean(jnp.abs(w)), 1e-05)
            wq = jnp.clip(jnp.round(w * scale), -1.0, 1.0) / scale
            return w + jax.lax.stop_gradient(wq - w)

        def _act_quant(x):
            scale = 127.0 / jnp.clip(jnp.max(jnp.abs(x), axis=-1, keepdims=True), 1e-05)
            xq = jnp.clip(jnp.round(x * scale), -128.0, 127.0) / scale
            return x + jax.lax.stop_gradient(xq - x)

        def _bitlinear(x, w):
            return jnp.einsum('bsi,oi->bso', _act_quant(x), _weight_quant(w))
        key = jax.random.key(seed)
        k0, k1, k2, k3 = jax.random.split(key, 4)
        x = jax.random.normal(k0, (4, 256, HIDDEN), dtype=jnp.float32)
        w_gate = jax.random.normal(k1, (INNER, HIDDEN), dtype=jnp.float32) / np.sqrt(HIDDEN)
        w_up = jax.random.normal(k2, (INNER, HIDDEN), dtype=jnp.float32) / np.sqrt(HIDDEN)
        w_down = jax.random.normal(k3, (HIDDEN, INNER), dtype=jnp.float32) / np.sqrt(INNER)
        return {'x': x, 'w_gate': w_gate, 'w_up': w_up, 'w_down': w_down}
    _L0_ffn_all = _L0_ffn_setup()
    _L0_ffn_in = {k: v for k, v in _L0_ffn_all.items() if k in ('w_gate', 'w_up', 'w_down')}
    del _L0_ffn_all

    def _L1_xattn_setup():
        import jax, jax.numpy as jnp
        import numpy as np
        D_MODEL = 128
        NUM_HEADS = 16
        DEPTH = D_MODEL // NUM_HEADS
        B, S = (4, 256)

        def _split_heads(x):
            b, s, _ = x.shape
            return x.reshape(b, s, NUM_HEADS, DEPTH).transpose(0, 2, 1, 3)
        key = jax.random.key(seed)
        ks = jax.random.split(key, 11)
        scale = 1.0 / np.sqrt(D_MODEL)
        inp = {'q': jax.random.normal(ks[0], (B, S, D_MODEL), dtype=jnp.float32), 'k': jax.random.normal(ks[1], (B, S, D_MODEL), dtype=jnp.float32), 'v': jax.random.normal(ks[2], (B, S, D_MODEL), dtype=jnp.float32), 'wq_w': jax.random.normal(ks[3], (D_MODEL, D_MODEL), dtype=jnp.float32) * scale, 'wq_b': jax.random.normal(ks[4], (D_MODEL,), dtype=jnp.float32) * scale, 'wk_w': jax.random.normal(ks[5], (D_MODEL, D_MODEL), dtype=jnp.float32) * scale, 'wk_b': jax.random.normal(ks[6], (D_MODEL,), dtype=jnp.float32) * scale, 'wv_w': jax.random.normal(ks[7], (D_MODEL, D_MODEL), dtype=jnp.float32) * scale, 'wv_b': jax.random.normal(ks[8], (D_MODEL,), dtype=jnp.float32) * scale, 'proj_w': jax.random.normal(ks[9], (D_MODEL, D_MODEL), dtype=jnp.float32) * scale, 'proj_b': jax.random.normal(ks[10], (D_MODEL,), dtype=jnp.float32) * scale}
        return inp
    _L1_xattn_all = _L1_xattn_setup()
    _L1_xattn_in = {k: v for k, v in _L1_xattn_all.items() if k in ('wq_w', 'wq_b', 'wk_w', 'wk_b', 'wv_w', 'wv_b', 'proj_w', 'proj_b')}
    del _L1_xattn_all

    def _L1_ffn_setup():
        import jax, jax.numpy as jnp
        import numpy as np
        TOP_K = 2
        CAPACITY_FACTOR = 1.0
        key = jax.random.key(seed)
        ks = jax.random.split(key, 4)
        sl, bs, hs, ffn, E = (256, 8, 128, 512, 8)
        x = jax.random.normal(ks[0], (sl, bs, hs), dtype=jnp.float32)
        w_router = jax.random.normal(ks[1], (hs, E), dtype=jnp.float32) * 0.02
        w1 = jax.random.normal(ks[2], (E, hs, ffn), dtype=jnp.float32) * 0.02
        w2 = jax.random.normal(ks[3], (E, ffn, hs), dtype=jnp.float32) * 0.02
        bias = jnp.zeros((1, 1, hs), dtype=jnp.float32)
        return {'x': x, 'w_router': w_router, 'w1': w1, 'w2': w2, 'bias': bias}
    _L1_ffn_all = _L1_ffn_setup()
    _L1_ffn_in = {k: v for k, v in _L1_ffn_all.items() if k in ('w_router', 'w1', 'w2', 'bias')}
    del _L1_ffn_all

    def _L2_xattn_setup():
        import jax, jax.numpy as jnp
        import numpy as np
        import math
        D_MODEL = 128
        N_HEADS = 16
        HEAD_DIM = D_MODEL // N_HEADS
        TOP_K = 32
        SCALE = math.sqrt(HEAD_DIM)

        def _split_heads(t, n):
            B, L, _ = t.shape
            return t.reshape(B, L, N_HEADS, HEAD_DIM).transpose(0, 2, 1, 3)
        key = jax.random.key(seed)
        ks = jax.random.split(key, 12)
        B, S, N = (2, 256, 256)
        std = 1.0 / math.sqrt(D_MODEL)
        inp = {'x': jax.random.normal(ks[0], (B, S, D_MODEL), dtype=jnp.float32), 'knowledge_embeddings': jax.random.normal(ks[1], (B, N, D_MODEL), dtype=jnp.float32), 'Wq': jax.random.normal(ks[2], (D_MODEL, D_MODEL), dtype=jnp.float32) * std, 'bq': jnp.zeros((D_MODEL,), dtype=jnp.float32), 'Wk': jax.random.normal(ks[3], (D_MODEL, D_MODEL), dtype=jnp.float32) * std, 'bk': jnp.zeros((D_MODEL,), dtype=jnp.float32), 'Wv': jax.random.normal(ks[4], (D_MODEL, D_MODEL), dtype=jnp.float32) * std, 'bv': jnp.zeros((D_MODEL,), dtype=jnp.float32), 'Wo': jax.random.normal(ks[5], (D_MODEL, D_MODEL), dtype=jnp.float32) * std, 'bo': jnp.zeros((D_MODEL,), dtype=jnp.float32)}
        return inp
    _L2_xattn_all = _L2_xattn_setup()
    _L2_xattn_in = {k: v for k, v in _L2_xattn_all.items() if k in ('Wq', 'bq', 'Wk', 'bk', 'Wv', 'bv', 'Wo', 'bo')}
    del _L2_xattn_all

    def _L2_ffn_setup():
        import jax, jax.numpy as jnp
        import numpy as np
        B, S, H = (4, 256, 128)
        E = 8
        GS = 2
        NG = E // GS
        F = int(H * 4 * (2.0 / 3.0))
        key = jax.random.key(seed)
        ks = jax.random.split(key, 7)
        sc_h = 1.0 / np.sqrt(H)
        sc_f = 1.0 / np.sqrt(F)
        return {'x': jax.random.normal(ks[0], (B, S, H), dtype=jnp.float32), 'Wr': jax.random.normal(ks[1], (H, E), dtype=jnp.float32) * sc_h, 'br': jnp.zeros((E,), dtype=jnp.float32), 'W_up': jax.random.normal(ks[2], (NG, H, F), dtype=jnp.float32) * sc_h, 'b_up': jax.random.normal(ks[3], (NG, F), dtype=jnp.float32) * 0.01, 'W_down': jax.random.normal(ks[4], (E, F, H), dtype=jnp.float32) * sc_f, 'b_down': jax.random.normal(ks[5], (E, H), dtype=jnp.float32) * 0.01}
    _L2_ffn_all = _L2_ffn_setup()
    _L2_ffn_in = {k: v for k, v in _L2_ffn_all.items() if k in ('Wr', 'br', 'W_up', 'b_up', 'W_down', 'b_down')}
    del _L2_ffn_all

    def _L3_xattn_setup():
        import jax, jax.numpy as jnp
        import numpy as np
        EMBED_DIM = 128
        NUM_HEADS = 16
        HEAD_DIM = EMBED_DIM // NUM_HEADS
        SCALE = HEAD_DIM ** (-0.5)
        key = jax.random.key(seed)
        ks = jax.random.split(key, 8)
        B, Nq, Nkv, C = (2, 128, 256, EMBED_DIM)
        xavier = (6.0 / (C + C)) ** 0.5

        def w(k):
            return jax.random.uniform(k, (C, C), jnp.float32, -xavier, xavier)
        return {'query': jax.random.normal(ks[0], (B, Nq, C), jnp.float32), 'key': jax.random.normal(ks[1], (B, Nkv, C), jnp.float32), 'value': jax.random.normal(ks[2], (B, Nkv, C), jnp.float32), 'Wq': w(ks[3]), 'bq': jnp.zeros((C,), jnp.float32), 'Wk': w(ks[4]), 'bk': jnp.zeros((C,), jnp.float32), 'Wv': w(ks[5]), 'bv': jnp.zeros((C,), jnp.float32), 'Wo': w(ks[6]), 'bo': jnp.zeros((C,), jnp.float32), 'temperature': jnp.ones((NUM_HEADS, 1, 1), jnp.float32)}
    _L3_xattn_all = _L3_xattn_setup()
    _L3_xattn_in = {k: v for k, v in _L3_xattn_all.items() if k in ('Wq', 'bq', 'Wk', 'bk', 'Wv', 'bv', 'Wo', 'bo', 'temperature')}
    del _L3_xattn_all

    def _L3_ffn_setup():
        import jax, jax.numpy as jnp
        import numpy as np
        B, S, D = (4, 256, 128)
        F = 512
        E = 8
        K = 2
        EPS = 1e-09
        key = jax.random.key(seed)
        ks = jax.random.split(key, 6)
        scale = 0.02
        return {'x': jax.random.normal(ks[0], (B, S, D), dtype=jnp.float32), 'Wg': jax.random.normal(ks[1], (D, E), dtype=jnp.float32) * scale, 'W1': jax.random.normal(ks[2], (E, D, F), dtype=jnp.float32) * scale, 'b1': jnp.zeros((E, F), dtype=jnp.float32), 'W2': jax.random.normal(ks[3], (E, F, D), dtype=jnp.float32) * scale, 'b2': jnp.zeros((E, D), dtype=jnp.float32)}
    _L3_ffn_all = _L3_ffn_setup()
    _L3_ffn_in = {k: v for k, v in _L3_ffn_all.items() if k in ('Wg', 'W1', 'b1', 'W2', 'b2')}
    del _L3_ffn_all
    return {'x': x, 'ctx_1024': ctx_1024, 'L0_ffn_w_gate': _L0_ffn_in['w_gate'], 'L0_ffn_w_up': _L0_ffn_in['w_up'], 'L0_ffn_w_down': _L0_ffn_in['w_down'], 'L1_xattn_wq_w': _L1_xattn_in['wq_w'], 'L1_xattn_wq_b': _L1_xattn_in['wq_b'], 'L1_xattn_wk_w': _L1_xattn_in['wk_w'], 'L1_xattn_wk_b': _L1_xattn_in['wk_b'], 'L1_xattn_wv_w': _L1_xattn_in['wv_w'], 'L1_xattn_wv_b': _L1_xattn_in['wv_b'], 'L1_xattn_proj_w': _L1_xattn_in['proj_w'], 'L1_xattn_proj_b': _L1_xattn_in['proj_b'], 'L1_ffn_w_router': _L1_ffn_in['w_router'], 'L1_ffn_w1': _L1_ffn_in['w1'], 'L1_ffn_w2': _L1_ffn_in['w2'], 'L1_ffn_bias': _L1_ffn_in['bias'], 'L2_xattn_Wq': _L2_xattn_in['Wq'], 'L2_xattn_bq': _L2_xattn_in['bq'], 'L2_xattn_Wk': _L2_xattn_in['Wk'], 'L2_xattn_bk': _L2_xattn_in['bk'], 'L2_xattn_Wv': _L2_xattn_in['Wv'], 'L2_xattn_bv': _L2_xattn_in['bv'], 'L2_xattn_Wo': _L2_xattn_in['Wo'], 'L2_xattn_bo': _L2_xattn_in['bo'], 'L2_ffn_Wr': _L2_ffn_in['Wr'], 'L2_ffn_br': _L2_ffn_in['br'], 'L2_ffn_W_up': _L2_ffn_in['W_up'], 'L2_ffn_b_up': _L2_ffn_in['b_up'], 'L2_ffn_W_down': _L2_ffn_in['W_down'], 'L2_ffn_b_down': _L2_ffn_in['b_down'], 'L3_xattn_Wq': _L3_xattn_in['Wq'], 'L3_xattn_bq': _L3_xattn_in['bq'], 'L3_xattn_Wk': _L3_xattn_in['Wk'], 'L3_xattn_bk': _L3_xattn_in['bk'], 'L3_xattn_Wv': _L3_xattn_in['Wv'], 'L3_xattn_bv': _L3_xattn_in['bv'], 'L3_xattn_Wo': _L3_xattn_in['Wo'], 'L3_xattn_bo': _L3_xattn_in['bo'], 'L3_xattn_temperature': _L3_xattn_in['temperature'], 'L3_ffn_Wg': _L3_ffn_in['Wg'], 'L3_ffn_W1': _L3_ffn_in['W1'], 'L3_ffn_b1': _L3_ffn_in['b1'], 'L3_ffn_W2': _L3_ffn_in['W2'], 'L3_ffn_b2': _L3_ffn_in['b2']}

def reference(x, ctx_1024, L0_ffn_w_gate, L0_ffn_w_up, L0_ffn_w_down, L1_xattn_wq_w, L1_xattn_wq_b, L1_xattn_wk_w, L1_xattn_wk_b, L1_xattn_wv_w, L1_xattn_wv_b, L1_xattn_proj_w, L1_xattn_proj_b, L1_ffn_w_router, L1_ffn_w1, L1_ffn_w2, L1_ffn_bias, L2_xattn_Wq, L2_xattn_bq, L2_xattn_Wk, L2_xattn_bk, L2_xattn_Wv, L2_xattn_bv, L2_xattn_Wo, L2_xattn_bo, L2_ffn_Wr, L2_ffn_br, L2_ffn_W_up, L2_ffn_b_up, L2_ffn_W_down, L2_ffn_b_down, L3_xattn_Wq, L3_xattn_bq, L3_xattn_Wk, L3_xattn_bk, L3_xattn_Wv, L3_xattn_bv, L3_xattn_Wo, L3_xattn_bo, L3_xattn_temperature, L3_ffn_Wg, L3_ffn_W1, L3_ffn_b1, L3_ffn_W2, L3_ffn_b2):
    import jax
    import jax.numpy as jnp

    def _L0_xattn_ref(Q, K, V):
        import jax, jax.numpy as jnp
        import numpy as np
        D_MODEL = 128
        N_HEADS = 16
        D_K = D_MODEL // N_HEADS
        B, S, _ = Q.shape
        q = Q.reshape(B, S, N_HEADS, D_K).transpose(0, 2, 1, 3)
        k = K.reshape(B, S, N_HEADS, D_K).transpose(0, 2, 1, 3)
        v = V.reshape(B, S, N_HEADS, D_K).transpose(0, 2, 1, 3)
        scale = 1.0 / np.sqrt(D_K).astype(np.float32)
        scores = jnp.einsum('bhqd,bhkd->bhqk', q, k) * scale
        attn = jax.nn.softmax(scores, axis=-1)
        out = jnp.einsum('bhqk,bhkd->bhqd', attn, v)
        return out.transpose(0, 2, 1, 3).reshape(B, S, D_MODEL)

    def _L0_ffn_ref(x, w_gate, w_up, w_down):
        import jax, jax.numpy as jnp
        import numpy as np
        HIDDEN = 128
        INNER = 512

        def _weight_quant(w):
            scale = 1.0 / jnp.clip(jnp.mean(jnp.abs(w)), 1e-05)
            wq = jnp.clip(jnp.round(w * scale), -1.0, 1.0) / scale
            return w + jax.lax.stop_gradient(wq - w)

        def _act_quant(x):
            scale = 127.0 / jnp.clip(jnp.max(jnp.abs(x), axis=-1, keepdims=True), 1e-05)
            xq = jnp.clip(jnp.round(x * scale), -128.0, 127.0) / scale
            return x + jax.lax.stop_gradient(xq - x)

        def _bitlinear(x, w):
            return jnp.einsum('bsi,oi->bso', _act_quant(x), _weight_quant(w))
        gate = jax.nn.silu(_bitlinear(x, w_gate))
        up = _bitlinear(x, w_up)
        return _bitlinear(gate * up, w_down)

    def _L1_xattn_ref(q, k, v, wq_w, wq_b, wk_w, wk_b, wv_w, wv_b, proj_w, proj_b):
        import jax, jax.numpy as jnp
        import numpy as np
        D_MODEL = 128
        NUM_HEADS = 16
        DEPTH = D_MODEL // NUM_HEADS
        B, S = (4, 256)

        def _split_heads(x):
            b, s, _ = x.shape
            return x.reshape(b, s, NUM_HEADS, DEPTH).transpose(0, 2, 1, 3)
        qh = _split_heads(q @ wq_w.T + wq_b)
        kh = _split_heads(k @ wk_w.T + wk_b)
        vh = _split_heads(v @ wv_w.T + wv_b)
        scores = jnp.einsum('bhqd,bhkd->bhqk', qh, kh) / jnp.sqrt(jnp.float32(DEPTH))
        attn = jax.nn.softmax(scores, axis=-1)
        ctx = jnp.einsum('bhqk,bhkd->bhqd', attn, vh)
        ctx = ctx.transpose(0, 2, 1, 3).reshape(q.shape[0], q.shape[1], D_MODEL)
        return ctx @ proj_w.T + proj_b

    def _L1_ffn_ref(x, w_router, w1, w2, bias):
        import jax, jax.numpy as jnp
        import numpy as np
        TOP_K = 2
        CAPACITY_FACTOR = 1.0
        sl, bs, hs = x.shape
        E = w_router.shape[1]
        xf = x.reshape(-1, hs)
        T = xf.shape[0]
        capacity = int(CAPACITY_FACTOR * TOP_K * T / E)
        scores = jax.nn.softmax(xf @ w_router, axis=-1)
        expert_weights, top_experts = jax.lax.top_k(scores, TOP_K)
        flat_e = top_experts.reshape(-1)
        flat_w = expert_weights.reshape(-1)
        N = flat_e.shape[0]
        order = jnp.argsort(flat_e, stable=True)
        bin_ids = flat_e[order]
        tpe = jnp.zeros((E,), jnp.int32).at[flat_e].add(1)
        starts = jnp.cumsum(tpe) - tpe
        offsets = jnp.arange(N) - starts[bin_ids]
        valid = offsets < capacity
        slot = jnp.where(valid, bin_ids * capacity + offsets, E * capacity)
        src = order // TOP_K
        xb = jnp.zeros((E * capacity + 1, hs), x.dtype).at[slot].set(xf[src])
        xb = xb[:-1].reshape(E, capacity, hs)
        h = jax.nn.gelu(jnp.einsum('ech,ehf->ecf', xb, w1))
        y = jnp.einsum('ecf,efh->ech', h, w2).reshape(E * capacity, hs)
        yv = jnp.where(valid[:, None], y[jnp.minimum(slot, E * capacity - 1)], 0.0)
        out = jnp.zeros((T, hs), x.dtype).at[src].add(flat_w[order][:, None] * yv)
        return out.reshape(sl, bs, hs) + bias

    def _L2_xattn_ref(x, knowledge_embeddings, Wq, bq, Wk, bk, Wv, bv, Wo, bo):
        import jax, jax.numpy as jnp
        import numpy as np
        import math
        D_MODEL = 128
        N_HEADS = 16
        HEAD_DIM = D_MODEL // N_HEADS
        TOP_K = 32
        SCALE = math.sqrt(HEAD_DIM)

        def _split_heads(t, n):
            B, L, _ = t.shape
            return t.reshape(B, L, N_HEADS, HEAD_DIM).transpose(0, 2, 1, 3)
        B, S, _ = x.shape
        N = knowledge_embeddings.shape[1]
        Q = _split_heads(x @ Wq.T + bq, N_HEADS)
        K = _split_heads(knowledge_embeddings @ Wk.T + bk, N_HEADS)
        V = _split_heads(knowledge_embeddings @ Wv.T + bv, N_HEADS)
        scores = jnp.einsum('bhsd,bhnd->bhsn', Q, K) / SCALE
        k = min(TOP_K, N)
        topk_scores, topk_indices = jax.lax.top_k(scores, k)
        sparse_weights = jax.nn.softmax(topk_scores, axis=-1)
        sel_V = jnp.take_along_axis(V[:, :, None, :, :], topk_indices[..., None], axis=3)
        context = jnp.einsum('bhsk,bhskd->bhsd', sparse_weights, sel_V)
        context = context.transpose(0, 2, 1, 3).reshape(B, S, D_MODEL)
        return context @ Wo.T + bo

    def _L2_ffn_ref(x, Wr, br, W_up, b_up, W_down, b_down):
        import jax, jax.numpy as jnp
        import numpy as np
        B, S, H = (4, 256, 128)
        E = 8
        GS = 2
        NG = E // GS
        F = int(H * 4 * (2.0 / 3.0))
        b, s, h = x.shape
        n_tok = b * s
        k = n_tok // E
        xf = x.reshape(n_tok, h)
        logits = xf @ Wr + br
        Sm = jax.nn.softmax(logits, axis=-1)
        G_t, idx_t = jax.lax.top_k(Sm.T, k)
        G = G_t.T
        idx = idx_t.T
        tokens = xf[idx]
        group = jnp.arange(E) // GS
        Wu = W_up[group]
        bu = b_up[group]
        mid = jax.nn.silu(jnp.einsum('keh,ehf->kef', tokens, Wu) + bu)
        out = jnp.einsum('kef,efh->keh', mid, W_down) + b_down
        y = jnp.zeros_like(xf).at[idx].add(G[..., None] * out)
        return y.reshape(b, s, h)

    def _L3_xattn_ref(query, key, value, Wq, bq, Wk, bk, Wv, bv, Wo, bo, temperature):
        import jax, jax.numpy as jnp
        import numpy as np
        EMBED_DIM = 128
        NUM_HEADS = 16
        HEAD_DIM = EMBED_DIM // NUM_HEADS
        SCALE = HEAD_DIM ** (-0.5)
        B, Nq, C = query.shape
        Nkv = key.shape[1]
        H, D = (NUM_HEADS, HEAD_DIM)
        Q = (query @ Wq.T + bq).reshape(B, Nq, H, D).transpose(0, 2, 1, 3)
        K = (key @ Wk.T + bk).reshape(B, Nkv, H, D).transpose(0, 2, 1, 3)
        V = (value @ Wv.T + bv).reshape(B, Nkv, H, D).transpose(0, 2, 1, 3)
        scores = jnp.einsum('bhqd,bhkd->bhqk', Q, K) * SCALE
        scores = scores / temperature
        attn = jax.nn.softmax(scores, axis=-1)
        out = jnp.einsum('bhqk,bhkd->bhqd', attn, V)
        out = out.transpose(0, 2, 1, 3).reshape(B, Nq, C)
        return out @ Wo.T + bo

    def _L3_ffn_ref(x, Wg, W1, b1, W2, b2):
        import jax, jax.numpy as jnp
        import numpy as np
        B, S, D = (4, 256, 128)
        F = 512
        E = 8
        K = 2
        EPS = 1e-09
        logits = jnp.einsum('bsd,de->bse', x, Wg)
        P = jax.nn.softmax(logits, axis=-1)
        _, topk_idx = jax.lax.top_k(P, K)
        mask = jax.nn.one_hot(topk_idx, E, dtype=x.dtype).sum(-2)
        P_topk = P * mask
        P_norm = P_topk / (P_topk.sum(axis=-1, keepdims=True) + EPS)
        h = jax.nn.gelu(jnp.einsum('bsd,edf->ebsf', x, W1) + b1[:, None, None, :], approximate=False)
        y_e = jnp.einsum('ebsf,efd->ebsd', h, W2) + b2[:, None, None, :]
        y = jnp.einsum('ebsd,bse->bsd', y_e, P_norm)
        return y
    x = x + _L0_xattn_ref(_layernorm(x, axis=-1), ctx_1024, ctx_1024)
    x = x + _L0_ffn_ref(_layernorm(x, axis=-1), L0_ffn_w_gate, L0_ffn_w_up, L0_ffn_w_down)
    x = x + _L1_xattn_ref(_layernorm(x, axis=-1), ctx_1024, ctx_1024, L1_xattn_wq_w, L1_xattn_wq_b, L1_xattn_wk_w, L1_xattn_wk_b, L1_xattn_wv_w, L1_xattn_wv_b, L1_xattn_proj_w, L1_xattn_proj_b)
    x = x + _L1_ffn_ref(_layernorm(x, axis=-1), L1_ffn_w_router, L1_ffn_w1, L1_ffn_w2, L1_ffn_bias)
    x = x + _L2_xattn_ref(_layernorm(x, axis=-1), ctx_1024, L2_xattn_Wq, L2_xattn_bq, L2_xattn_Wk, L2_xattn_bk, L2_xattn_Wv, L2_xattn_bv, L2_xattn_Wo, L2_xattn_bo)
    x = x + _L2_ffn_ref(_layernorm(x, axis=-1), L2_ffn_Wr, L2_ffn_br, L2_ffn_W_up, L2_ffn_b_up, L2_ffn_W_down, L2_ffn_b_down)
    x = x + _L3_xattn_ref(_layernorm(x, axis=-1), ctx_1024, ctx_1024, L3_xattn_Wq, L3_xattn_bq, L3_xattn_Wk, L3_xattn_bk, L3_xattn_Wv, L3_xattn_bv, L3_xattn_Wo, L3_xattn_bo, L3_xattn_temperature)
    x = x + _L3_ffn_ref(_layernorm(x, axis=-1), L3_ffn_Wg, L3_ffn_W1, L3_ffn_b1, L3_ffn_W2, L3_ffn_b2)
    return x

_drawn_inputs = setup_inputs


def setup_inputs(seed=0):
    import zlib

    import numpy as np

    out = dict(_drawn_inputs(seed))
    spreads = {'L1_ffn_bias': (0.0, 0.1),
     'L2_xattn_bq': (0.0, 0.1),
     'L2_xattn_bk': (0.0, 2.0),
     'L2_xattn_bv': (0.0, 0.1),
     'L2_xattn_bo': (0.0, 0.1),
     'L2_ffn_br': (0.0, 0.469),
     'L3_xattn_bq': (0.0, 0.391),
     'L3_xattn_bk': (0.0, 2.0),
     'L3_xattn_bv': (0.0, 0.1),
     'L3_xattn_bo': (0.0, 0.1),
     'L3_xattn_temperature': (1.0, 0.2),
     'L3_ffn_b1': (0.0, 0.779),
     'L3_ffn_b2': (0.0, 0.1)}
    factors = {'L1_xattn_wq_b': 3.141,
     'L1_xattn_wk_b': 64.0,
     'L1_ffn_w_router': 4.354,
     'L1_ffn_w1': 4.612,
     'L1_ffn_w2': 4.729,
     'L2_ffn_b_up': 35.601,
     'L2_ffn_b_down': 22.6}
    for name, (base, spread) in spreads.items():
        noise = np.random.default_rng([zlib.crc32(name.encode()), seed]).standard_normal(out[name].shape)
        drawn = base * np.exp(spread * noise) if base else spread * noise
        out[name] = jnp.asarray(drawn.astype(out[name].dtype))
    for name, factor in factors.items():
        out[name] = (out[name] * factor).astype(out[name].dtype)
    return out
```

```python
from contextlib import ExitStack

import concourse.bass as bass
from concourse import mybir

B = 8
P = 128
D = 128
NH = 16
DK = D // NH
NG = 4
GH = NH // NG
GW = GH * DK
NPART = P // GW
VW = DK + 1
F = 512
NC = F // P
E = 8
TOPK_E = 2
T = B * P
CAPACITY = TOPK_E * T // E
EC_K = T // E
EGRP = 2
NEG = E // EGRP
F2 = int(D * 4 * (2.0 / 3.0))
NC2 = -(-F2 // P)
FC2 = -(-F2 // NC2)
FROWS2 = [min(FC2, F2 - c * FC2) for c in range(NC2)]
TOP_ATTN = 32
ROUNDS = TOP_ATTN // 8
U = 4
HALF = T // 2
HB = B // 2
LN_EPS = 1e-5
QMIN = 1e-5
NORM_EPS = 1e-9
ROUND = 12582912.0
TAKEN = -3.0e38
PAD = -2.0e38
C = DK ** -0.5

F32 = mybir.dt.float32
F32R = mybir.dt.float32r
BF16 = mybir.dt.bfloat16
U32 = mybir.dt.uint32
ALU = mybir.AluOpType
ACT = mybir.ActivationFunctionType
AX = mybir.AxisListType.X

ATTN = dict(var=1, rstd=1, xn=1, xnT_ps=1, xnT=1, q_ps=1, qb=1, qst=1, s_ps=NG, sx=NG, p=NG, pt_ps=NG,
            pt=NG, pv=NG, on=1, onT_ps=1, onT=1, o_ps=1, x=1)
ATTN0 = {k: n for k, n in ATTN.items() if k not in ("onT_ps", "onT", "o_ps")}
TOPK = {**{k: n for k, n in ATTN.items() if k not in ("sx", "p")}, "ss": NG, "topk": NG, "ex": NG, "psel": NG}
BIT = dict(var=1, rstd=1, xn=1, xnT_ps=1, xnT=1, gu_ps=1, gate=1, h=1, hqT_ps=1, hqT=1, dn_ps=1, x=1)
MOE = dict(var=1, rstd=1, xn=1, xnT_ps=1, xnT=1, lg_ps=1, lmax=1, lexp=1, gates=1, h_ps=E, hT=E, y_ps=E, acc=E, x=1)
MOE1 = dict(MOE, cnt_ps=1)
MOE3 = dict(MOE, gT_ps=1, gT=1, b2_ps=1)
ECR = dict(var=1, rstd=1, xn=1, xnT_ps=1, xnT=1, lg_ps=1)
EC = dict(h_ps=NEG, hT=NEG, y_ps=NEG, acc=NEG, gT=1, b2_ps=1, x=1)
PHASES = [("attn0", ATTN0), ("bit0", BIT), ("attn1", ATTN), ("moe1", MOE1), ("attn2", TOPK),
          ("ecr2", ECR), ("ec2", EC), ("attn3", ATTN), ("moe3", MOE3)]
FREE = dict(sx=NG, ss=NG, pt_ps=4, pt=2, pv=2, on=1, ex=2, psel=2, qst=1, hT=2, y_ps=2, acc=2)
LAYER = {"attn1": 0, "attn2": 1, "attn3": 2}


class Counts:

    def __init__(self):
        self.before, self.each, total = {}, {}, {}
        for _, each in PHASES:
            for what in each:
                total.setdefault(what, FREE.get(what, 0))
        for name, each in PHASES:
            self.before[name] = dict(total)
            self.each[name] = each
            for what, n in each.items():
                total[what] += n * B
        self.names = list(total)

    def of(self, phase, what, b, n=1):
        return b * self.each[phase][what] + (self.before[phase][what] + n)


class Chain:

    def __init__(self, eng, sem):
        self.eng, self.sem, self.n, self.it, self.per = eng, sem, 0, None, 0

    def mark(self, ins):
        ins.then_inc(self.sem, 1)
        self.n += 1
        return self.n

    def value(self, n):
        return n if self.it is None else self.it * self.per + n

    def turn(self, it, per):
        self.it, self.per, self.at0 = it, per, self.n

    def done(self, turns):
        assert self.n - self.at0 == self.per, f"{self.n - self.at0} marked in a turn, not {self.per}"
        self.n, self.it = self.at0 + self.per * turns, None


def build(nc, a, out):
    with ExitStack() as ctx:
        def sb(name, shape, dt=F32):
            return ctx.enter_context(nc.sbuf_tensor("sb_" + name, shape, dt))

        def sem(name):
            return ctx.enter_context(nc.semaphore(name))

        bank = [ctx.enter_context(nc.psum_tensor(f"bank{i}", [P, 512], F32)) for i in range(8)]
        S_BANK = bank[0:4]
        PT_BANK = bank[4:6]
        A_BANK, O_BANK = bank[6], bank[7]
        H_BANK, Y_BANK = bank[0:2], bank[4:6]

        def halfword(bk):
            return bk[:, 0:256].bitcast(BF16)

        x_res = sb("x_res", [P, B, D])
        ctx_tok = sb("ctx_tok", [P, B, D])
        xnT_all = ctx_tok
        ctxT = sb("ctxT", [P, T])
        k_st = sb("k_st", [P, GH, NG, B, P], F32R)
        k_raw = sb("k_raw", [P, 2 * NG, 512])
        k_part = sb("k_part", [P, NG, 512], F32R)
        v_aug = sb("v_aug", [P, B, NH, VW])
        id_rep = sb("id_rep", [P, NG, NPART, GW])
        wq_rep = sb("wq_rep", [P, 3, NG, NPART, GW])
        wk_rep = sb("wk_rep", [P, 3, NG, NPART, GW])
        wv_T = sb("wv_T", [P, 3, D])
        wo_T = sb("wo_T", [P, 3, D])
        bq_rep = sb("bq_rep", [P, 3, NG])
        bk_rep = sb("bk_rep", [P, 3, NG])
        bv_row = sb("bv_row", [P, 3, D])
        bo_row = sb("bo_row", [P, 3, D])
        temp_row = sb("temp_row", [P, NH])
        itemp_row = sb("itemp_row", [P, NH])
        temp_rep = sb("temp_rep", [P, NG])
        itemp_rep = sb("itemp_rep", [P, NG])
        ident = sb("ident", [P, P])
        ident_b = sb("ident_b", [P, P], BF16)
        ones = sb("ones", [P, P])
        ones_b = sb("ones_b", [P, P], BF16)
        before_b = sb("before_b", [P, P], BF16)
        stats = sb("stats", [P, 2, 6])
        mv = sb("mv", [P, 2, 2])
        ve = sb("ve", [P, 2, 1])
        rstd = sb("rstd", [P, 2, 1])
        minus_half = sb("minus_half", [P, 1])
        xn = sb("xn", [P, 2, D])
        xnT = sb("xnT", [P, 2, D])
        qb = sb("qb", [P, 512])
        q_st = sb("q_st", [P, 2, 512], F32R)
        mx = sb("mx", [P, NG, GH])
        p_sb = sb("p_sb", [P, NG, GH, P])
        pt_sb = sb("pt_sb", [P, 2, GH, P])
        rden = sb("rden", [P, 2, NH])
        on = sb("on", [P, 2, D])
        onT = sb("onT", [P, 2, D])
        t_row = sb("t_row", [P, 2, D])
        v8 = sb("v8", [P, 2, GH, ROUNDS, 8])
        negm = sb("negm", [P, 2, GH])
        shared = sb("shared", [P, 4, 512])
        gate, h0 = shared[:, 0:2, :], shared[:, 2:4, :]
        ss = shared[:, 0:2, :].rearrange("p r (j k) -> p r j k", k=P)
        sel = shared[:, 2:4, :].rearrange("p r (j k) -> p r j k", k=P)
        probT = shared[0:E, 0:2, :].rearrange("p r k -> p (r k)")
        takenT = shared[0:E, 2:4, :].rearrange("p r k -> p (r k)")
        wstat = sb("wstat", [P, 3, 3])
        amax = sb("amax", [P, 2, 2])
        aclip = sb("aclip", [P, 2, 2])
        qscale = sb("qscale", [P, 2, 2])
        deq = sb("deq", [P, 2, 3])
        xr = sb("xr", [P, 2, D])
        xq = sb("xq", [P, 2, D], BF16)
        xqT = sb("xqT", [P, 2, D], BF16)
        idle = pt_sb[:, :, :, :].rearrange("p a j k -> p (a j k)").bitcast(BF16)
        hq = idle[:, 0:2 * F].rearrange("p (a f) -> p a f", a=2)
        hqT = idle[:, 2 * F:4 * F].rearrange("p (a f) -> p a f", a=2)
        w1 = sb("w1", [P, E, F])
        w2 = sb("w2", [P, E, NC, D])
        hT = sb("hT", [P, 2, NC, P])
        wbT = hT[:, :, :, :].rearrange("p a c k -> p (a c k)").bitcast(BF16)[:, 0:3 * 512]\
            .rearrange("p (m n) -> p m n", m=3)
        wb_q = w1[:, 0:2, :].rearrange("p e f -> p (e f)").bitcast(BF16)[:, 0:3 * 512]\
            .rearrange("p (m n) -> p m n", m=3)
        early = w2[:, :, :, :].rearrange("p e c d -> p (e c d)")
        w_raw = early[:, 0:12 * D].rearrange("p (m i) -> p m i", m=12)
        wb_raw = early[:, 12 * D:12 * D + 3 * 512].rearrange("p (m i) -> p m i", m=3)
        wr = sb("wr", [P, 3, E])
        b1_col = sb("b1_col", [P, E, NC])
        b2_sb = sb("b2_sb", [E, 2, D])
        br_row = sb("br_row", [P, E])
        bias_row = sb("bias_row", [P, D])
        lrow = sb("lrow", [P, 2, E + 6])
        top8 = sb("top8", [P, 2, 8])
        pick8 = sb("pick8", [P, 2, 8])
        lmark = sb("lmark", [P, 2, E + 6])
        nlm = sb("nlm", [P, 2, 1])
        el = sb("el", [P, 2, E])
        esum = sb("esum", [P, 2, 1])
        rsum = sb("rsum", [P, 2, 1])
        pr = sb("pr", [P, 2, E])
        maskf = sb("maskf", [P, 2, E])
        mask_b = sb("mask_b", [P, 2, E], BF16)
        seen = sb("seen", [P, E])
        seen_b = sb("seen_b", [P, 2, E], BF16)
        fits = sb("fits", [P, 2, E])
        gates = sb("gates", [P, 2, E])
        gsum = sb("gsum", [P, 2, 3])
        gT = sb("gT", [E, 2, P])
        wu2 = sb("wu2", [P, NEG, F2])
        wd2 = k_raw[0:FC2, :, :].rearrange("p a k -> p (a k)")[:, 0:NC2 * E * D]\
            .rearrange("p (c e d) -> p c e d", c=NC2, e=E)
        bu2 = sb("bu2", [P, NEG, NC2])
        lg_all = sb("lg_all", [P, B, E])
        lmax_all = sb("lmax_all", [P, B])
        lsum_all = sb("lsum_all", [P, B])
        rsum_all = sb("rsum_all", [P, B])
        prob = sb("prob", [P, B, E])
        gates_all = sb("gates_all", [P, B, E])
        ec8 = sb("ec8", [E, 2, 8])

        counts = Counts()
        s = {name: sem("s_" + name) for name in counts.names}
        of = counts.of
        ld_x, ld_ctx, ld_w, ld_bit = sem("ld_x"), sem("ld_ctx"), sem("ld_w"), sem("ld_bit")
        ld_small, ld_moe1, ld_moe3, ld_ec = sem("ld_small"), sem("ld_moe1"), sem("ld_moe3"), sem("ld_ec")
        const_ready = sem("const_ready")
        v_ones = sem("v_ones")
        zero_ready = sem("zero_ready")
        tr_ps = sem("tr_ps")
        ctxT_ready = sem("ctxT_ready")
        w_ready = sem("w_ready")
        v0_ready = sem("v0_ready")
        wsum_ready = sem("wsum_ready")
        wtot_ps = sem("wtot_ps")
        wb_ready = sem("wb_ready")
        wbT_ps = sem("wbT_ps")
        wbT_ready = sem("wbT_ready")
        k_ps = sem("k_ps")
        k_evac = sem("k_evac")
        k_upper = sem("k_upper")
        k_lower = sem("k_lower")
        k_split = sem("k_split")
        k_placed = sem("k_placed")
        v_ps = sem("v_ps")
        v_ready = sem("v_ready")
        lg_all_ready = sem("lg_all_ready")
        lexp_all = sem("lexp_all")
        prob_ready = sem("prob_ready")
        probT_ps = sem("probT_ps")
        probT_ready = sem("probT_ready")
        taken_ready = sem("taken_ready")
        taken_ps = sem("taken_ps")
        gT_all_ready = sem("gT_all_ready")
        ec_gates = sem("ec_gates")
        dve_own, act_own, pool_own = sem("dve_own"), sem("act_own"), sem("pool_own")
        xnT_two = sem("xnT_two")
        held = sem("held")
        stored = sem("stored")

        def hold(eng, what, value):
            eng.wait_ge(what, value)
            eng.sem_inc(held, 1)

        KEY_PHASES = ["attn0", "attn1", "attn2", "attn3"]
        PLACES = NPART * GH
        block = ctx.enter_context(nc.Block())
        n_small = [0]

        @block.sync
        def _(sp):
            sp.dma_start(ctx_tok[:, :, :], a["ctx_1024"].rearrange("b p d -> p b d")).then_inc(ld_ctx, 16)
            sp.dma_start(x_res[:, :, :], a["x"].rearrange("b p d -> p b d")).then_inc(ld_x, 16)
            mats = ["L1_xattn_wq_w", "L1_xattn_wk_w", "L1_xattn_wv_w", "L1_xattn_proj_w",
                    "L2_xattn_Wq", "L2_xattn_Wk", "L2_xattn_Wv", "L2_xattn_Wo",
                    "L3_xattn_Wq", "L3_xattn_Wk", "L3_xattn_Wv", "L3_xattn_Wo"]
            for i, name in enumerate(mats):
                sp.dma_start(w_raw[:, i, :], a[name]).then_inc(ld_w, 16)
            for i, name in enumerate(("L0_ffn_w_gate", "L0_ffn_w_up")):
                sp.dma_start(wb_raw[:, i, :].rearrange("p (c i) -> p c i", c=NC),
                             a[name].rearrange("(c p) i -> p c i", p=P)).then_inc(ld_bit, 16)
            sp.dma_start(wb_raw[:, 2, :], a["L0_ffn_w_down"]).then_inc(ld_bit, 16)

            def small(dst, src):
                sp.dma_start(dst, src, allow_slow_non_contiguous=True).then_inc(ld_small, 16)
                n_small[0] += 1

            names = [("L1_xattn_wq_b", "L1_xattn_wk_b", "L1_xattn_wv_b", "L1_xattn_proj_b"),
                     ("L2_xattn_bq", "L2_xattn_bk", "L2_xattn_bv", "L2_xattn_bo"),
                     ("L3_xattn_bq", "L3_xattn_bk", "L3_xattn_bv", "L3_xattn_bo")]
            for i, (q, k, v, o) in enumerate(names):
                for part in range(NPART):
                    rows = slice(GW * part, GW * (part + 1))
                    small(bq_rep[rows, i, :], a[q].rearrange("(g h) -> h g", h=GW))
                    small(bk_rep[rows, i, :], a[k].rearrange("(g h) -> h g", h=GW))
                small(bv_row[:, i, :], a[v].partition_broadcast(P))
                small(bo_row[:, i, :], a[o].partition_broadcast(P))
            temp = a["L3_xattn_temperature"].rearrange("h a b -> (h a b)")
            small(temp_row[:, :], temp.partition_broadcast(P))
            for part in range(NPART):
                for j in range(GH):
                    lo = GW * part + DK * j
                    small(temp_rep[lo:lo + DK, :], temp.rearrange("(g j) -> j g", j=GH)[j].partition_broadcast(DK))
            small(wr[:, 0, :], a["L1_ffn_w_router"])
            small(wr[:, 1, :], a["L2_ffn_Wr"])
            small(wr[:, 2, :], a["L3_ffn_Wg"])
            small(bias_row[:, :], a["L1_ffn_bias"].rearrange("a b d -> (a b d)").partition_broadcast(P))
            small(br_row[:, :], a["L2_ffn_br"].partition_broadcast(P))
            small(b2_sb[:, 0, :], a["L2_ffn_b_down"])
            small(b2_sb[:, 1, :], a["L3_ffn_b2"])
            for e in range(E):
                small(b1_col[:, e, :], a["L3_ffn_b1"][e].rearrange("(c p) -> p c", p=P))
            for g in range(NEG):
                for c, n in enumerate(FROWS2):
                    small(bu2[0:n, g, c:c + 1],
                          a["L2_ffn_b_up"][g, c * FC2:c * FC2 + n].rearrange("(f o) -> f o", o=1))
            sp.dma_start(wu2[:, :, :], a["L2_ffn_W_up"].rearrange("g d f -> d g f")).then_inc(ld_ec, 16)

            def place_keys(i):
                for half in range(2):
                    sp.wait_ge(k_split, NG * (2 * i + half + 1))
                    if i == 0:
                        sp.wait_ge(zero_ready, B)
                    else:
                        sp.wait_ge(s["s_ps"], of(KEY_PHASES[i - 1], "s_ps", B - 1, NG))
                    for part in range(NPART):
                        for j in range(GH):
                            lo = GW * part + DK * j
                            sp.dma_start(
                                k_st[lo:lo + DK, j, :, HB * half:HB * (half + 1), :]
                                .rearrange("p g b k -> p g (b k)").bitcast(F32),
                                k_part[lo:lo + DK, :, :].bitcast(F32)).then_inc(k_placed, 16)

            place_keys(0)
            sp.wait_ge(ctxT_ready, 2)
            sp.wait_ge(w_ready, 3)
            sp.wait_ge(wb_ready, 1)
            for e in range(E):
                if e == 0:
                    sp.wait_ge(wbT_ps, 1)
                sp.dma_start(w1[:, e, :], a["L1_ffn_w1"][e]).then_inc(ld_moe1, 16)
                sp.dma_start(w2[:, e, :, :], a["L1_ffn_w2"][e].rearrange("(c p) d -> p c d", p=P)).then_inc(ld_moe1, 16)
            place_keys(1)
            place_keys(2)
            sp.wait_ge(s["y_ps"], of("moe1", "y_ps", B - 1, E))
            for e in range(E):
                sp.dma_start(w1[:, e, :], a["L3_ffn_W1"][e]).then_inc(ld_moe3, 16)
                sp.dma_start(w2[:, e, :, :], a["L3_ffn_W2"][e].rearrange("(c p) d -> p c d", p=P)).then_inc(ld_moe3, 16)
            place_keys(3)
            for c, n in enumerate(FROWS2):
                sp.dma_start(wd2[0:n, c, :, :],
                             a["L2_ffn_W_down"][:, c * FC2:c * FC2 + n, :].rearrange("e f d -> f e d")).then_inc(ld_ec, 16)
            for b in range(B):
                sp.wait_ge(s["x"], of("moe3", "x", b))
                sp.dma_start(out[b], x_res[:, b, :]).then_inc(stored, 16)
            sp.wait_ge(stored, 16 * B)

        SMALL = 16 * n_small[0]

        @block.gpsimd
        def _(pool):
            own = Chain(pool, pool_own)

            def step(ins):
                pool.wait_ge(pool_own, own.mark(ins))

            step(pool.memset(ident[:, :], 0.0))
            step(pool.affine_select(out=ident[:, :], in_=ident[:, :], compare_op=ALU.not_equal, fill=1.0,
                                    base=0, pattern=[[-1, P]], channel_multiplier=1))
            pool.tensor_copy(ident_b[:, :], ident[:, :]).then_inc(const_ready, 1)
            for part in range(NPART):
                step(pool.tensor_copy(id_rep[:, :, part, :], ident[:, :].rearrange("p (g f) -> p g f", g=NG)))
            pool.memset(ones[:, :], 1.0).then_inc(const_ready, 1)
            pool.memset(ones_b[:, :], 1.0).then_inc(const_ready, 1)
            step(pool.memset(before_b[:, :], 1.0))
            pool.affine_select(out=before_b[:, :], in_=before_b[:, :], compare_op=ALU.is_gt, fill=0.0,
                               base=0, pattern=[[1, P]], channel_multiplier=-1).then_inc(const_ready, 1)
            pool.memset(minus_half[:, :], -0.5)
            pool.memset(v_aug[:, :, :, DK:VW], 1.0).then_inc(v_ones, 1)
            for j in range(GH):
                for g in range(0, NG, 2):
                    pool.memset(k_st[:, j, g:g + 2, :, :].bitcast(U32), 0).then_inc(zero_ready, 1)

            def split_keys(i, half, g, first=True):
                done = half * NG + (2 * NG * i + g)
                raw = k_raw[:, bass.ds(half * NG + g, 1), :].rearrange("p u k -> p (u k)")
                pool.wait_ge(k_evac, done + 1)
                if first:
                    pool.wait_ge(k_split, done)
                pool.tensor_copy(k_part[:, g, :], raw).then_inc(k_upper, 1)
                pool.wait_ge(k_upper, done + 1)
                rows = slice(GW, 2 * GW)
                pool.tensor_tensor(k_part[rows, g, :], raw[rows, :], k_part[rows, g, :], ALU.subtract).then_inc(k_lower, 1)
                pool.wait_ge(k_lower, done + 1)
                rows = slice(3 * GW, 4 * GW)
                pool.tensor_tensor(k_part[rows, g, :], raw[rows, :], k_part[rows, g, :], ALU.subtract).then_inc(k_split, 1)

            def scale_of(ph, b, p):
                pool.wait_ge(s["var"], of(ph, "var", b))
                pool.tensor_tensor(rstd[:, p, :], ve[:, p, :], minus_half[:, :], ALU.pow).then_inc(s["rstd"], 1)

            def norms(ph, keys=None):
                with pool.Fori(0, B // U) as it:
                    for u in range(U):
                        scale_of(ph, it * U + u, u % 2)
                        if keys is not None:
                            if u == 0:
                                pool.wait_ge(k_placed, it * (16 * PLACES) + 16 * PLACES * 2 * keys)
                            split_keys(keys, it, u)
                            pool.wait_ge(k_split, it * NG + (2 * NG * keys + u + 1))

            for half in range(2):
                if half == 1:
                    pool.wait_ge(k_placed, 16 * PLACES)
                for g in range(NG):
                    split_keys(0, half, g, half + g > 0)
            pool.wait_ge(k_split, 2 * NG)
            norms("attn0")
            norms("bit0", 1)
            norms("attn1")
            norms("moe1", 2)
            with pool.Fori(0, B // U) as it:
                scale_of("attn2", it * U, 0)
                for u in range(U):
                    b = it * U + u
                    if u + 1 < U:
                        scale_of("attn2", b + 1, (u + 1) % 2)
                    for g in range(NG):
                        pool.wait_ge(s["ex"], of("attn2", "ex", b, g + 1))
                        pool.tensor_tensor(p_sb[:, g, :, :], p_sb[:, g, :, :], sel[:, g % 2, :, :],
                                           ALU.subtract).then_inc(s["psel"], 1)
            norms("ecr2", 3)
            norms("attn3")
            norms("moe3")

        @block.tensor
        def _(pe):
            for what, n in FREE.items():
                pe.sem_inc(s[what], n)

            pe.wait_ge(const_ready, 1)
            pe.wait_ge(ld_ctx, 16)
            for half in range(2):
                for i in range(4):
                    ins = pe.transpose(bank[half][:, P * i:P * (i + 1)], ctx_tok[:, 4 * half + i, :], ident[:, :])
                ins.then_inc(tr_ps, 1)
            pe.wait_ge(ld_w, 16 * 12)
            for layer in range(3):
                for i in range(4):
                    ins = pe.transpose(bank[2 + layer][:, P * i:P * (i + 1)], w_raw[:, 4 * layer + i, :], ident[:, :])
                ins.then_inc(tr_ps, 1)

            def project_keys(i):
                if i == 0:
                    pe.wait_ge(ctxT_ready, 2)
                    pe.wait_ge(const_ready, 2)
                else:
                    pe.wait_ge(ctxT_ready, 2)
                    pe.wait_ge(w_ready, 3)
                    pe.wait_ge(s["x"], of(KEY_PHASES[i - 1], "x", B - 1))
                for unit in range(2 * NG):
                    half, g = unit // NG, unit % NG
                    if unit >= 2:
                        pe.wait_ge(k_evac, 2 * NG * i + unit - 1)
                    w = id_rep[:, g, :, :] if i == 0 else wk_rep[:, i - 1, g, :, :]
                    pe.matmul(bank[6 + unit % 2][:, :], w.rearrange("p a f -> p (a f)"),
                              ctxT[:, HALF * half:HALF * (half + 1)], start=True, stop=True).then_inc(k_ps, 1)
                if i > 0:
                    for half in range(2):
                        for j in range(HB):
                            b = HB * half + j
                            ins = pe.matmul(PT_BANK[half][:, P * j:P * (j + 1)], ctxT[:, P * b:P * (b + 1)],
                                            wv_T[:, i - 1, :], start=True, stop=True)
                        ins.then_inc(v_ps, 1)
                    pe.wait_ge(k_evac, 2 * NG * (i + 1))
                    pe.wait_ge(v_ready, 2 * i)

            def attention(ph):
                layer = LAYER.get(ph)
                topk = ph == "attn2"
                used, weights = ("ss", "psel") if topk else ("sx", "p")

                def front_t(b, p):
                    pe.wait_ge(s["xn"], of(ph, "xn", b))
                    pe.transpose(A_BANK[:, 0:P], xn[:, p, :], ident[:, :]).then_inc(s["xnT_ps"], 1)

                def front_q(b, p):
                    pe.wait_ge(s["xnT"], of(ph, "xnT", b))
                    for g in range(NG):
                        w = id_rep[:, g, :, :] if layer is None else wq_rep[:, layer, g, :, :]
                        ins = pe.matmul(A_BANK[:, P * g:P * (g + 1)], w.rearrange("p a f -> p (a f)"),
                                        xnT[:, p, :], start=True, stop=True)
                    ins.then_inc(s["q_ps"], 1)

                pe.wait_ge(k_placed, 16 * PLACES * 2 * (KEY_PHASES.index(ph) + 1))
                if layer is None:
                    pe.wait_ge(v0_ready, 1)
                else:
                    pe.wait_ge(v_ready, 2 * (layer + 1))
                with pe.Fori(0, B // U) as it:
                    front_t(it * U, 0)
                    front_q(it * U, 0)
                    for t in range(NG * U + 5):
                        u, g = t // NG, t % NG
                        b, p = it * U + u, u % 2
                        if g == 1 and u + 1 < U:
                            if u >= 2 and layer is not None:
                                pe.wait_ge(s["x"], of(ph, "x", b - 2))
                            front_t(b + 1, (u + 1) % 2)
                        if g == 2 and u + 1 < U:
                            front_q(b + 1, (u + 1) % 2)
                        if u < U:
                            if g == 0:
                                pe.wait_ge(s["qst"], of(ph, "qst", b))
                            pe.wait_ge(s[used], of(ph, used, b, g + 1 - NG))
                            pe.matmul(S_BANK[g][:, :], q_st[:, p, P * g:P * (g + 1)],
                                      k_st[:, :, g, bass.ds(b, 1), :].rearrange("p j b k -> p j (b k)"),
                                      start=True, stop=True).then_inc(s["s_ps"], 1)
                        t2 = t - 2
                        if 0 <= t2 < NG * U:
                            b2, g2 = it * U + t2 // NG, t2 % NG
                            pe.wait_ge(s[weights], of(ph, weights, b2, g2 + 1))
                            pe.wait_ge(s["pt"], of(ph, "pt", b2, g2 + 1 - 2))
                            for j in range(GH):
                                ins = pe.transpose(PT_BANK[g2 % 2][:, P * j:P * (j + 1)], p_sb[:, g2, j, :], ident[:, :])
                            ins.then_inc(s["pt_ps"], 1)
                        t3 = t - 3
                        if 0 <= t3 < NG * U:
                            b3, g3 = it * U + t3 // NG, t3 % NG
                            pe.wait_ge(s["pt"], of(ph, "pt", b3, g3 + 1))
                            if g3 == 0:
                                pe.wait_ge(s["on"], of(ph, "on", b3, 0))
                            for j in range(GH):
                                h = GH * g3 + j
                                ins = pe.matmul(O_BANK[:, VW * h:VW * (h + 1)], pt_sb[:, g3 % 2, j, :],
                                                v_aug[:, bass.ds(b3, 1), h, :].rearrange("p b v -> p (b v)"),
                                                start=True, stop=True)
                            ins.then_inc(s["pv"], 1)
                        if layer is not None and g == 3 and 1 <= u <= U:
                            pe.wait_ge(s["on"], of(ph, "on", b - 1))
                            if u + 1 < U:
                                pe.wait_ge(s["qb"], of(ph, "qb", b + 1))
                            elif u >= 2:
                                pe.wait_ge(s["x"], of(ph, "x", b - 2))
                            pe.transpose(A_BANK[:, 0:P], on[:, (u - 1) % 2, :], ident[:, :]).then_inc(s["onT_ps"], 1)
                        if layer is not None and g == 0 and 2 <= u <= U + 1:
                            pe.wait_ge(s["onT"], of(ph, "onT", b - 2))
                            pe.matmul(A_BANK[:, 0:D], onT[:, u % 2, :], wo_T[:, layer, :],
                                      start=True, stop=True).then_inc(s["o_ps"], 1)

            def bitffn(ph):
                def front(b, p):
                    pe.wait_ge(s["xn"], of(ph, "xn", b))
                    pe.transpose(halfword(A_BANK)[:, 0:P], xq[:, p, :], ident_b[:, :]).then_inc(s["xnT_ps"], 1)
                    pe.wait_ge(s["xnT"], of(ph, "xnT", b))
                    for m in range(2):
                        ins = pe.matmul(S_BANK[2 * p + m][:, :], xqT[:, p, :], wbT[:, m, :], start=True, stop=True)
                    ins.then_inc(s["gu_ps"], 1)

                pe.wait_ge(wbT_ready, 1)
                with pe.Fori(0, B // U) as it:
                    front(it * U, 0)
                    for u in range(U):
                        b, p = it * U + u, u % 2
                        if u + 1 < U:
                            if u >= 1:
                                pe.wait_ge(s["h"], of(ph, "h", b - 1))
                            front(b + 1, (u + 1) % 2)
                        pe.wait_ge(s["h"], of(ph, "h", b))
                        for c in range(NC):
                            ins = pe.transpose(halfword(PT_BANK[p])[:, P * c:P * (c + 1)], hq[:, p, P * c:P * (c + 1)],
                                               ident_b[:, :])
                        ins.then_inc(s["hqT_ps"], 1)
                        pe.wait_ge(s["hqT"], of(ph, "hqT", b))
                        if u >= 1:
                            pe.wait_ge(s["x"], of(ph, "x", b - 1))
                        for c in range(NC):
                            ins = pe.matmul(O_BANK[:, 0:D], hqT[:, p, P * c:P * (c + 1)], wbT[:, 2, P * c:P * (c + 1)],
                                            start=(c == 0), stop=(c == NC - 1))
                        ins.then_inc(s["dn_ps"], 1)

            def moe(ph):
                third = ph == "moe3"
                router = 2 if third else 0

                def front_t(b, p):
                    pe.wait_ge(s["xn"], of(ph, "xn", b))
                    pe.transpose(A_BANK[:, 0:P], xn[:, p, :], ident[:, :]).then_inc(s["xnT_ps"], 1)

                def front_l(b, p):
                    pe.wait_ge(s["xnT"], of(ph, "xnT", b))
                    pe.matmul(O_BANK[:, 0:E], xnT[:, p, :], wr[:, router, :], start=True, stop=True).then_inc(s["lg_ps"], 1)

                def front_c(b, p):
                    pe.wait_ge(s["lmax"], of(ph, "lmax", b))
                    pe.matmul(O_BANK[:, 64:64 + E], before_b[:, :], mask_b[:, p, :], start=True, stop=False)
                    pe.matmul(O_BANK[:, 64:64 + E], ones_b[:, :], seen_b[:, p, :], start=False,
                              stop=True).then_inc(s["cnt_ps"], 1)

                def front_g(b, p):
                    pe.wait_ge(s["gates"], of(ph, "gates", b))
                    pe.transpose(A_BANK[0:E, 0:P], gates[:, p, :], ident[:, :]).then_inc(s["gT_ps"], 1)

                def front_b(b, p):
                    pe.wait_ge(s["gT"], of(ph, "gT", b))
                    pe.matmul(O_BANK[:, 0:D], gT[:, p, :], b2_sb[:, 1, :], start=True, stop=True).then_inc(s["b2_ps"], 1)

                pe.wait_ge(ld_small, SMALL)
                pe.wait_ge(*((ld_moe3, 32 * E) if third else (ld_moe1, 32 * E)))
                with pe.Fori(0, B // U) as it:
                    front_t(it * U, 0)
                    front_l(it * U, 0)
                    if third:
                        front_g(it * U, 0)
                        front_b(it * U, 0)
                    else:
                        front_c(it * U, 0)
                    for i in range(E * U + 1):
                        u, e = i // E, i % E
                        b, p = it * U + u, u % 2
                        if u < U:
                            pe.wait_ge(s["hT"], of(ph, "hT", b, e + 1 - 2))
                            for c in range(NC):
                                ins = pe.matmul(H_BANK[e % 2][:, P * c:P * (c + 1)], w1[:, e, P * c:P * (c + 1)],
                                                xnT[:, p, :], start=True, stop=True)
                            ins.then_inc(s["h_ps"], 1)
                        if i >= 1:
                            b1, e1 = it * U + (i - 1) // E, (i - 1) % E
                            pe.wait_ge(s["hT"], of(ph, "hT", b1, e1 + 1))
                            pe.wait_ge(s["acc"], of(ph, "acc", b1, e1 + 1 - 2))
                            for c in range(NC):
                                ins = pe.matmul(Y_BANK[e1 % 2][:, 0:D], hT[:, e1 % 2, c, :], w2[:, e1, c, :],
                                                start=(c == 0), stop=(c == NC - 1))
                            ins.then_inc(s["y_ps"], 1)
                        if u + 1 < U:
                            q = (u + 1) % 2
                            if e == 1:
                                front_t(b + 1, q)
                            if e == 2:
                                front_l(b + 1, q)
                            if e == 4 and not third:
                                front_c(b + 1, q)
                            if e == 6 and third:
                                front_g(b + 1, q)
                            if e == 7 and third:
                                front_b(b + 1, q)

            def choose_tokens(ph):
                with pe.Fori(0, B // 2) as it:
                    for p in range(2):
                        b = it * 2 + p
                        pe.wait_ge(s["xn"], of(ph, "xn", b))
                        pe.transpose(PT_BANK[p][:, 0:P], xn[:, p, :], ident[:, :]).then_inc(s["xnT_ps"], 1)
                        pe.wait_ge(s["xnT"], of(ph, "xnT", b))
                        pe.matmul(bank[0][:, bass.ds(b * E, E)], xnT[:, p, :], wr[:, 1, :],
                                  start=True, stop=True).then_inc(s["lg_ps"], 1)
                pe.wait_ge(prob_ready, 1)
                for b in range(B):
                    ins = pe.transpose(bank[1 + b // HB][0:E, P * (b % HB):P * (b % HB + 1)], prob[:, b, :], ident[:, :])
                ins.then_inc(probT_ps, 1)
                pe.wait_ge(taken_ready, 1)
                for b in range(B):
                    ins = pe.transpose(bank[3][:, E * b:E * (b + 1)], takenT[:, P * b:P * (b + 1)], ident[0:E, 0:E])
                ins.then_inc(taken_ps, 1)

            def expert_choice(ph):
                pe.wait_ge(ld_ec, 16 * (1 + NC2))
                with pe.Fori(0, B // U) as it:
                    for i in range(NEG * U + 1):
                        u, g = i // NEG, i % NEG
                        b, p = it * U + u, u % 2
                        if u < U:
                            if g == 0:
                                pe.wait_ge(s["gT"], of(ph, "gT", b))
                                if u >= 1:
                                    pe.wait_ge(s["acc"], of(ph, "acc", b - 1, 1))
                                pe.matmul(O_BANK[:, 0:D], gT[:, p, :], b2_sb[:, 0, :], start=True,
                                          stop=True).then_inc(s["b2_ps"], 1)
                            pe.wait_ge(s["hT"], of(ph, "hT", b, g + 1 - 2))
                            for c, n in enumerate(FROWS2):
                                ins = pe.matmul(H_BANK[g % 2][0:n, P * c:P * (c + 1)], wu2[:, g, FC2 * c:FC2 * c + n],
                                                xnT_all[:, bass.ds(b, 1), :].rearrange("p b t -> p (b t)"),
                                                start=True, stop=True)
                            ins.then_inc(s["h_ps"], 1)
                        if i >= 1:
                            b1, g1 = it * U + (i - 1) // NEG, (i - 1) % NEG
                            pe.wait_ge(s["hT"], of(ph, "hT", b1, g1 + 1))
                            pe.wait_ge(s["acc"], of(ph, "acc", b1, g1 + 1 - 2))
                            for c, n in enumerate(FROWS2):
                                ins = pe.matmul(Y_BANK[g1 % 2][:, 0:EGRP * D], hT[0:n, g1 % 2, c, :],
                                                wd2[0:n, c, EGRP * g1:EGRP * (g1 + 1), :],
                                                start=(c == 0), stop=(c == NC2 - 1))
                            ins.then_inc(s["y_ps"], 1)

            project_keys(0)
            pe.wait_ge(wsum_ready, 3)
            pe.wait_ge(const_ready, 4)
            pe.matmul(bank[5][:, 0:3], ones[:, :], wstat[:, 0, :], start=True, stop=True).then_inc(wtot_ps, 1)
            pe.wait_ge(wb_ready, 1)
            pe.wait_ge(ctxT_ready, 2)
            pe.wait_ge(w_ready, 3)
            for m in range(3):
                for c in range(NC):
                    ins = pe.transpose(halfword(bank[m])[:, P * c:P * (c + 1)], wb_q[:, m, P * c:P * (c + 1)], ident_b[:, :])
            ins.then_inc(wbT_ps, 1)
            pe.wait_ge(wbT_ready, 1)
            pe.wait_ge(k_evac, 2 * NG)
            attention("attn0")
            project_keys(1)
            bitffn("bit0")
            attention("attn1")
            project_keys(2)
            moe("moe1")
            attention("attn2")
            project_keys(3)
            choose_tokens("ecr2")
            expert_choice("ec2")
            attention("attn3")
            moe("moe3")

        @block.scalar
        def _(act):
            own = Chain(act, act_own)
            act.wait_ge(tr_ps, 1)
            act.copy(ctxT[:, 0:HALF], bank[0][:, :]).then_inc(ctxT_ready, 1)
            act.wait_ge(tr_ps, 2)
            act.copy(ctxT[:, HALF:T], bank[1][:, :]).then_inc(ctxT_ready, 1)

            def evacuate_keys(i):
                for unit in range(2 * NG):
                    act.wait_ge(k_ps, 2 * NG * i + unit + 1)
                    if i > 0 and unit == 0:
                        act.wait_ge(k_split, 2 * NG * i)
                        act.wait_ge(ld_small, SMALL)
                    if i == 0:
                        act.copy(k_raw[:, unit, :], bank[6 + unit % 2][:, :]).then_inc(k_evac, 1)
                    else:
                        act.activation(k_raw[:, unit, :], bank[6 + unit % 2][:, :], ACT.Identity,
                                       bias=bk_rep[:, i - 1, unit % NG:unit % NG + 1]).then_inc(k_evac, 1)

            evacuate_keys(0)
            act.wait_ge(ld_bit, 48)
            for m in range(3):
                act.activation(shared[:, m, :], wb_raw[:, m, :], ACT.Abs, accum_out=wstat[:, 0, m:m + 1]).then_inc(wsum_ready, 1)
            act.wait_ge(wbT_ps, 1)
            for m in range(3):
                ins = act.copy(wbT[:, m, :], halfword(bank[m]))
            ins.then_inc(wbT_ready, 1)

            def attention(ph):
                layer = LAYER.get(ph)
                topk = ph == "attn2"

                def front_t(b, p):
                    act.wait_ge(s["xnT_ps"], of(ph, "xnT_ps", b))
                    act.copy(xnT[:, p, :], A_BANK[:, 0:P]).then_inc(s["xnT"], 1)

                def front_q(b, p):
                    act.wait_ge(s["q_ps"], of(ph, "q_ps", b))
                    hold(act, s["qst"], of(ph, "qst", b, 0))
                    if layer is None:
                        act.copy(qb[:, :], A_BANK[:, :]).then_inc(s["qb"], 1)
                    else:
                        for g in range(NG):
                            ins = act.activation(qb[:, P * g:P * (g + 1)], A_BANK[:, P * g:P * (g + 1)], ACT.Identity,
                                                 bias=bq_rep[:, layer, g:g + 1])
                        ins.then_inc(s["qb"], 1)

                with act.Fori(0, B // U) as it:
                    front_t(it * U, 0)
                    front_q(it * U, 0)
                    for t in range(NG * U + 5):
                        u, g = t // NG, t % NG
                        b, p = it * U + u, u % 2
                        if g == 1 and u + 1 < U:
                            front_t(b + 1, (u + 1) % 2)
                        if g == 2 and u + 1 < U:
                            front_q(b + 1, (u + 1) % 2)
                        if topk and u < U:
                            act.wait_ge(s["s_ps"], of(ph, "s_ps", b, g + 1))
                            hold(act, s["ex"], of(ph, "ex", b, g + 1 - 2))
                            act.copy(ss[:, g % 2, :, :].rearrange("p j k -> p (j k)"), S_BANK[g][:, :]).then_inc(s["ss"], 1)
                        t2 = t - (3 if topk else 2)
                        if 0 <= t2 < NG * U:
                            b2, g2 = it * U + t2 // NG, t2 % NG
                            act.wait_ge(s["pt_ps"], of(ph, "pt_ps", b2, g2 + 1))
                            hold(act, s["pv"], of(ph, "pv", b2, g2 + 1 - 2))
                            act.copy(pt_sb[:, g2 % 2, :, :].rearrange("p j k -> p (j k)"),
                                     PT_BANK[g2 % 2][:, :]).then_inc(s["pt"], 1)
                        if topk and 1 <= t <= NG * U:
                            b1, g1 = it * U + (t - 1) // NG, (t - 1) % NG
                            r = g1 % 2
                            act.wait_ge(s["topk"], of(ph, "topk", b1, g1 + 1))
                            hold(act, s["pt_ps"], of(ph, "pt_ps", b1, g1 + 1 - 4))
                            for j in range(GH):
                                act.activation(p_sb[:, g1, j, :], ss[:, r, j, :], ACT.Exp, bias=negm[:, r, j:j + 1], scale=C)
                                ins = act.activation(sel[:, r, j, :], sel[:, r, j, :], ACT.Exp,
                                                     bias=negm[:, r, j:j + 1], scale=C)
                            ins.then_inc(s["ex"], 1)
                        if not topk and u < U:
                            act.wait_ge(s["sx"], of(ph, "sx", b, g + 1))
                            flat = p_sb[:, g, :, :].rearrange("p j k -> p (j k)")
                            act.activation(flat, flat, ACT.Exp, scale=C).then_inc(s["p"], 1)
                        if layer is not None and g == 3 and 1 <= u <= U:
                            act.wait_ge(s["onT_ps"], of(ph, "onT_ps", b - 1))
                            act.copy(onT[:, (u - 1) % 2, :], A_BANK[:, 0:P]).then_inc(s["onT"], 1)

            def bitffn(ph):
                def front(b, p):
                    act.wait_ge(s["xnT_ps"], of(ph, "xnT_ps", b))
                    act.copy(xqT[:, p, :], halfword(A_BANK)[:, 0:P]).then_inc(s["xnT"], 1)
                    act.wait_ge(s["gu_ps"], of(ph, "gu_ps", b))
                    act.activation(gate[:, p, :], S_BANK[2 * p][:, :], ACT.Silu, scale=deq[:, p, 0:1]).then_inc(s["gate"], 1)

                with act.Fori(0, B // U) as it:
                    front(it * U, 0)
                    for u in range(U):
                        b, p = it * U + u, u % 2
                        if u + 1 < U:
                            front(b + 1, (u + 1) % 2)
                        act.wait_ge(s["hqT_ps"], of(ph, "hqT_ps", b))
                        act.copy(hqT[:, p, :], halfword(PT_BANK[p])).then_inc(s["hqT"], 1)

            def moe(ph):
                third = ph == "moe3"

                def front_t(b, p):
                    act.wait_ge(s["xnT_ps"], of(ph, "xnT_ps", b))
                    act.copy(xnT[:, p, :], A_BANK[:, 0:P]).then_inc(s["xnT"], 1)

                def front_e(b, p):
                    act.wait_ge(s["lmax"], of(ph, "lmax", b))
                    act.activation(el[:, p, :], lrow[:, p, 0:E], ACT.Exp, bias=nlm[:, p, :],
                                   accum_out=esum[:, p, :]).then_inc(s["lexp"], 1)

                def front_g(b, p):
                    act.wait_ge(s["gT_ps"], of(ph, "gT_ps", b))
                    act.copy(gT[:, p, :], A_BANK[0:E, 0:P]).then_inc(s["gT"], 1)

                with act.Fori(0, B // U) as it:
                    front_t(it * U, 0)
                    front_e(it * U, 0)
                    if third:
                        front_g(it * U, 0)
                    for i in range(E * U):
                        u, e = i // E, i % E
                        b = it * U + u
                        act.wait_ge(s["h_ps"], of(ph, "h_ps", b, e + 1))
                        hold(act, s["y_ps"], of(ph, "y_ps", b, e + 1 - 2))
                        if third:
                            for c in range(NC):
                                ins = act.activation(hT[:, e % 2, c, :], H_BANK[e % 2][:, P * c:P * (c + 1)], ACT.Gelu,
                                                     bias=b1_col[:, e, c:c + 1])
                        else:
                            ins = act.activation(hT[:, e % 2, :, :].rearrange("p c k -> p (c k)"), H_BANK[e % 2][:, :],
                                                 ACT.Gelu_apprx_tanh)
                        ins.then_inc(s["hT"], 1)
                        if u + 1 < U:
                            q = (u + 1) % 2
                            if e == 1:
                                front_t(b + 1, q)
                            if e == 4:
                                front_e(b + 1, q)
                            if e == 6 and third:
                                front_g(b + 1, q)

            def choose_tokens(ph):
                with act.Fori(0, B // 2) as it:
                    for p in range(2):
                        b = it * 2 + p
                        act.wait_ge(s["xnT_ps"], of(ph, "xnT_ps", b))
                        hold(act, s["lg_ps"], of(ph, "lg_ps", b, -1))
                        act.copy(xnT[:, p, :], PT_BANK[p][:, 0:P]).then_inc(xnT_two, 1)
                        act.copy(xnT_all[:, bass.ds(b, 1), :].rearrange("p b t -> p (b t)"),
                                 PT_BANK[p][:, 0:P]).then_inc(s["xnT"], 1)
                act.wait_ge(lg_all_ready, 1)
                act.activation(prob[:, :, :], lg_all[:, :, :], ACT.Exp).then_inc(lexp_all, 1)
                act.wait_ge(probT_ps, 1)
                for half in range(2):
                    ins = act.copy(probT[:, HALF * half:HALF * (half + 1)], bank[1 + half][0:E, :])
                ins.then_inc(probT_ready, 1)

            def expert_choice(ph):
                act.wait_ge(gT_all_ready, 1)
                with act.Fori(0, B // U) as it:
                    for i in range(NEG * U):
                        u, g = i // NEG, i % NEG
                        b, p = it * U + u, u % 2
                        if g == 0:
                            if u >= 2:
                                hold(act, s["b2_ps"], of(ph, "b2_ps", b - 2))
                            act.copy(gT[:, p, :], probT[:, bass.ds(b * P, P)]).then_inc(s["gT"], 1)
                        act.wait_ge(s["h_ps"], of(ph, "h_ps", b, g + 1))
                        hold(act, s["y_ps"], of(ph, "y_ps", b, g + 1 - 2))
                        for c, n in enumerate(FROWS2):
                            ins = act.activation(hT[0:n, g % 2, c, :], H_BANK[g % 2][0:n, P * c:P * (c + 1)], ACT.Silu,
                                                 bias=bu2[0:n, g, c:c + 1])
                        ins.then_inc(s["hT"], 1)

            attention("attn0")
            evacuate_keys(1)
            bitffn("bit0")
            attention("attn1")
            evacuate_keys(2)
            moe("moe1")
            attention("attn2")
            evacuate_keys(3)
            choose_tokens("ecr2")
            expert_choice("ec2")
            attention("attn3")
            moe("moe3")

        @block.vector
        def _(dve):
            own = Chain(dve, dve_own)

            def need(n):
                dve.wait_ge(dve_own, own.value(n))

            def need_alone(n):
                hold(dve, dve_own, own.value(n))

            def layernorm(ph, b, p, x_ready=None):
                if x_ready is not None:
                    hold(dve, *x_ready)
                xb = x_res[:, bass.ds(b, 1), :].rearrange("p b d -> p (b d)")
                n = own.mark(dve.bn_stats(stats[:, p, :], xb))
                need_alone(n)
                n = own.mark(dve.bn_aggr(mv[:, p, :], stats[:, p, :]))
                need(n)
                dve.tensor_scalar(ve[:, p, :], mv[:, p, 1:2], LN_EPS, None, ALU.add).then_inc(s["var"], 1)
                dve.wait_ge(s["rstd"], of(ph, "rstd", b))
                return dve.tensor_scalar(xn[:, p, :], xb, mv[:, p, 0:1], rstd[:, p, :], ALU.subtract, ALU.mult)

            def xb_of(b):
                return x_res[:, bass.ds(b, 1), :].rearrange("p b d -> p (b d)")

            dve.wait_ge(ld_ctx, 16)
            dve.wait_ge(v_ones, 1)
            dve.tensor_copy(v_aug[:, :, :, 0:DK], ctx_tok[:, :, :].rearrange("p b (h d) -> p b h d", h=NH))\
               .then_inc(v0_ready, 1)
            dve.wait_ge(ld_small, SMALL)
            n = own.mark(dve.reciprocal(itemp_row[:, :], temp_row[:, :]))
            n = own.mark(dve.reciprocal(itemp_rep[:, :], temp_rep[:, :]))
            need(n)
            n = own.mark(dve.tensor_tensor(bq_rep[:, 2, :], bq_rep[:, 2, :], itemp_rep[:, :], ALU.mult))
            for layer in range(3):
                dve.wait_ge(tr_ps, 3 + layer)
                wt = bank[2 + layer][:, :].rearrange("p (m g f) -> p m g f", m=4, g=NG)
                for part in range(NPART):
                    if layer == 2:
                        scale = itemp_row[:, :].rearrange("p (g j o) -> p g j o", g=NG, o=1).to_broadcast([P, NG, GH, DK])
                        dve.tensor_tensor(wq_rep[:, layer, :, part, :].rearrange("p g (j d) -> p g j d", d=DK),
                                          wt[:, 0, :, :].rearrange("p g (j d) -> p g j d", d=DK), scale, ALU.mult)
                    else:
                        dve.tensor_copy(wq_rep[:, layer, :, part, :], wt[:, 0, :, :])
                    dve.tensor_copy(wk_rep[:, layer, :, part, :], wt[:, 1, :, :])
                dve.tensor_copy(wv_T[:, layer, :], bank[2 + layer][:, 2 * D:3 * D])
                dve.tensor_copy(wo_T[:, layer, :], bank[2 + layer][:, 3 * D:4 * D]).then_inc(w_ready, 1)
            dve.wait_ge(wtot_ps, 1)
            n = own.mark(dve.tensor_scalar(wstat[:, 1, :], bank[5][:, 0:3], 1.0 / (F * D), QMIN, ALU.mult, ALU.max))
            need(n)
            n = own.mark(dve.reciprocal(wstat[:, 2, :], wstat[:, 1, :]))
            need(n)
            for m in range(3):
                n = own.mark(dve.tensor_scalar(wb_raw[:, m, :], wb_raw[:, m, :], wstat[:, 2, m:m + 1], ROUND,
                                               ALU.mult, ALU.add))
            need(n)
            for m in range(3):
                n = own.mark(dve.tensor_scalar(wb_raw[:, m, :], wb_raw[:, m, :], ROUND, 1.0, ALU.subtract, ALU.min))
            need(n)
            for m in range(3):
                ins = dve.tensor_scalar(wb_q[:, m, :], wb_raw[:, m, :], -1.0, None, ALU.max)
            ins.then_inc(wb_ready, 1)

            def values(i):
                for half in range(2):
                    dve.wait_ge(v_ps, 2 * (i - 1) + half + 1)
                    bias = bv_row[:, i - 1, :].rearrange("p (o h d) -> p o h d", o=1, h=NH)
                    for j in range(HB):
                        ins = dve.tensor_tensor(v_aug[:, HB * half + j, :, 0:DK],
                                                PT_BANK[half][:, P * j:P * (j + 1)].rearrange("p (h d) -> p h d", h=NH),
                                                bias[:, 0, :, :], ALU.add)
                    ins.then_inc(v_ready, 1)

            def attention(ph, before, marks):
                layer = LAYER.get(ph)
                topk = ph == "attn2"

                def front_x(b, p, first=False):
                    layernorm(ph, b, p, (s["x"], of(before, "x", b)) if before else None).then_inc(s["xn"], 1)

                def front_q(b, p):
                    dve.wait_ge(s["qb"], of(ph, "qb", b))
                    n = own.mark(dve.tensor_copy(q_st[:, p, :], qb[:, :]))
                    need(n)
                    dve.tensor_tensor(q_st[P // 2:P, p, :], qb[P // 2:P, :], q_st[P // 2:P, p, :],
                                      ALU.subtract).then_inc(s["qst"], 1)

                def shift(b, g):
                    dve.wait_ge(s["s_ps"], of(ph, "s_ps", b, g + 1))
                    scores = S_BANK[g][:, :].rearrange("p (j k) -> p j k", j=GH)
                    n = own.mark(dve.tensor_reduce(mx[:, g, :], scores, AX, ALU.max))
                    need(n)
                    hold(dve, s["pt_ps"], of(ph, "pt_ps", b, g + 1 - 4))
                    dve.tensor_tensor(p_sb[:, g, :, :], scores, mx[:, g, :].unsqueeze(2).to_broadcast([P, GH, P]),
                                      ALU.subtract).then_inc(s["sx"], 1)

                def search(b, g):
                    r = g % 2
                    hold(dve, s["ss"], of(ph, "ss", b, g + 1))
                    hold(dve, s["psel"], of(ph, "psel", b, g + 1 - 2))
                    taken = [None] * GH
                    for rnd in range(ROUNDS):
                        src = ss if rnd == 0 else sel
                        found = [None] * GH
                        for j in range(GH):
                            if rnd > 0 and j % 2 == 0:
                                need_alone(taken[j + 1])
                            found[j] = own.mark(dve.max(v8[:, r, j, rnd, :], src[:, r, j, :]))
                        for j in range(GH):
                            if j % 2 == 0:
                                need_alone(found[j + 1])
                            taken[j] = own.mark(dve.match_replace(sel[:, r, j, :], v8[:, r, j, rnd, :], src[:, r, j, :],
                                                                  TAKEN))
                        if rnd == 0:
                            own.mark(dve.tensor_scalar(negm[:, r, :], v8[:, r, :, 0, 0], -C, None, ALU.mult))
                    need(taken[-1])
                    dve.sem_inc(s["topk"], 1)

                def normalize(b, p):
                    dve.wait_ge(s["pv"], of(ph, "pv", b, NG))
                    o = O_BANK[:, 0:NH * VW].rearrange("p (h v) -> p h v", v=VW)
                    n = own.mark(dve.reciprocal(rden[:, p, :], o[:, :, DK]))
                    need(n)
                    dve.tensor_tensor(on[:, p, :].rearrange("p (h d) -> p h d", h=NH), o[:, :, 0:DK],
                                      rden[:, p, :].unsqueeze(2).to_broadcast([P, NH, DK]), ALU.mult).then_inc(s["on"], 1)

                def add(b, p):
                    if layer is None:
                        dve.wait_ge(s["on"], of(ph, "on", b))
                        dve.tensor_tensor(xb_of(b), xb_of(b), on[:, p, :], ALU.add).then_inc(s["x"], 1)
                    else:
                        dve.wait_ge(s["o_ps"], of(ph, "o_ps", b))
                        n = own.mark(dve.tensor_tensor(t_row[:, p, :], A_BANK[:, 0:D], bo_row[:, layer, :], ALU.add))
                        need(n)
                        dve.tensor_tensor(xb_of(b), xb_of(b), t_row[:, p, :], ALU.add).then_inc(s["x"], 1)

                with dve.Fori(0, B // U) as it:
                    own.turn(it, marks)
                    front_x(it * U, 0)
                    front_q(it * U, 0)
                    for t in range(NG * U + 5):
                        u, g = t // NG, t % NG
                        b, p = it * U + u, u % 2
                        if u < U:
                            (search if topk else shift)(b, g)
                        if g == 0 and u + 1 < U:
                            front_x(b + 1, (u + 1) % 2)
                        if g == 0 and layer is not None and 2 <= u <= U + 1:
                            add(b - 2, u % 2)
                        if g == 3:
                            if u + 1 < U:
                                front_q(b + 1, (u + 1) % 2)
                            if 1 <= u <= U:
                                normalize(b - 1, (u - 1) % 2)
                                if layer is None:
                                    add(b - 1, (u - 1) % 2)
                own.done(B // U)

            def bitffn(ph, before, marks):
                def quantize(src, p, which, width, tmp, dst):
                    n = own.mark(dve.tensor_reduce(amax[:, p, which:which + 1], src, AX, ALU.max, apply_absolute_value=True))
                    need(n)
                    n = own.mark(dve.tensor_scalar(aclip[:, p, which:which + 1], amax[:, p, which:which + 1], QMIN,
                                                   1.0 / 127.0, ALU.max, ALU.mult))
                    need(n)
                    n = own.mark(dve.reciprocal(qscale[:, p, which:which + 1], aclip[:, p, which:which + 1]))
                    need(n)
                    n = own.mark(dve.tensor_scalar(tmp, src, qscale[:, p, which:which + 1], ROUND, ALU.mult, ALU.add))
                    if which == 0:
                        for m in range(2):
                            own.mark(dve.tensor_scalar(deq[:, p, m:m + 1], aclip[:, p, 0:1], wstat[:, 1, m:m + 1],
                                                       None, ALU.mult))
                    else:
                        own.mark(dve.tensor_scalar(deq[:, p, 2:3], aclip[:, p, 1:2], wstat[:, 1, 2:3],
                                                   None, ALU.mult))
                    need(n)
                    return dve.tensor_scalar(dst, tmp, ROUND, None, ALU.subtract)

                def front(b, p):
                    n = own.mark(layernorm(ph, b, p, (s["x"], of(before, "x", b))))
                    need(n)
                    quantize(xn[:, p, :], p, 0, D, xr[:, p, :], xq[:, p, :]).then_inc(s["xn"], 1)

                def inner(b, p):
                    dve.wait_ge(s["gate"], of(ph, "gate", b))
                    n = own.mark(dve.scalar_tensor_tensor(h0[:, p, :], S_BANK[2 * p + 1][:, :], deq[:, p, 1:2],
                                                          gate[:, p, :], ALU.mult, ALU.mult))
                    need(n)
                    quantize(h0[:, p, :], p, 1, F, gate[:, p, :], hq[:, p, :]).then_inc(s["h"], 1)

                def add(b, p):
                    dve.wait_ge(s["dn_ps"], of(ph, "dn_ps", b))
                    dve.scalar_tensor_tensor(xb_of(b), O_BANK[:, 0:D], deq[:, p, 2:3], xb_of(b), ALU.mult,
                                             ALU.add).then_inc(s["x"], 1)

                with dve.Fori(0, B // U) as it:
                    own.turn(it, marks)
                    front(it * U, 0)
                    for u in range(U):
                        b, p = it * U + u, u % 2
                        inner(b, p)
                        if u >= 1:
                            add(b - 1, 1 - p)
                        if u + 1 < U:
                            front(b + 1, 1 - p)
                    add(it * U + (U - 1), (U - 1) % 2)
                own.done(B // U)

            def moe(ph, before, marks):
                third = ph == "moe3"

                def front_x(b, p):
                    layernorm(ph, b, p, (s["x"], of(before, "x", b))).then_inc(s["xn"], 1)

                def front_m(b, p):
                    dve.wait_ge(s["lg_ps"], of(ph, "lg_ps", b))
                    n = own.mark(dve.tensor_copy(lrow[:, p, 0:E], O_BANK[:, 0:E]))
                    need_alone(n)
                    n = own.mark(dve.max(top8[:, p, :], lrow[:, p, :]))
                    need(n)
                    n1 = own.mark(dve.tensor_copy(pick8[:, p, 0:TOPK_E], top8[:, p, 0:TOPK_E]))
                    own.mark(dve.tensor_scalar(nlm[:, p, :], top8[:, p, 0:1], -1.0, None, ALU.mult))
                    need_alone(n1)
                    n = own.mark(dve.match_replace(lmark[:, p, :], pick8[:, p, :], lrow[:, p, :], TAKEN))
                    need(n)
                    n = own.mark(dve.tensor_scalar(maskf[:, p, :], lmark[:, p, 0:E], TAKEN, None, ALU.is_equal))
                    need(n)
                    if not third:
                        own.mark(dve.tensor_copy(seen_b[:, p, :], seen[:, :]))
                        own.mark(dve.tensor_copy(mask_b[:, p, :], maskf[:, p, :]))
                        n = own.mark(dve.tensor_tensor(seen[:, :], seen[:, :], maskf[:, p, :], ALU.add))
                    need(own.n)
                    dve.sem_inc(s["lmax"], 1)

                def front_g(b, p):
                    dve.wait_ge(s["lexp"], of(ph, "lexp", b))
                    n = own.mark(dve.reciprocal(rsum[:, p, :], esum[:, p, :]))
                    need(n)
                    n = own.mark(dve.scalar_tensor_tensor(pr[:, p, :], el[:, p, :], rsum[:, p, :], maskf[:, p, :],
                                                          ALU.mult, ALU.mult))
                    if third:
                        need(n)
                        n = own.mark(dve.tensor_reduce(gsum[:, p, 0:1], pr[:, p, :], AX, ALU.add))
                        need(n)
                        n = own.mark(dve.tensor_scalar(gsum[:, p, 1:2], gsum[:, p, 0:1], NORM_EPS, None, ALU.add))
                        need(n)
                        n = own.mark(dve.reciprocal(gsum[:, p, 2:3], gsum[:, p, 1:2]))
                        need(n)
                        n = own.mark(dve.tensor_scalar(gates[:, p, :], pr[:, p, :], gsum[:, p, 2:3], None, ALU.mult))
                    else:
                        hold(dve, s["cnt_ps"], of(ph, "cnt_ps", b))
                        need(n)
                        n = own.mark(dve.scalar_tensor_tensor(gates[:, p, :], O_BANK[:, 64:64 + E], float(CAPACITY),
                                                              pr[:, p, :], ALU.is_lt, ALU.mult))
                    need(n)
                    dve.sem_inc(s["gates"], 1)

                def front_b(b, p):
                    if third:
                        dve.wait_ge(s["b2_ps"], of(ph, "b2_ps", b))
                        return own.mark(dve.tensor_tensor(xb_of(b), xb_of(b), O_BANK[:, 0:D], ALU.add))
                    return own.mark(dve.tensor_tensor(xb_of(b), xb_of(b), bias_row[:, :], ALU.add))

                n = own.mark(dve.memset(lrow[:, :, E:E + 6], PAD))
                n = own.mark(dve.memset(pick8[:, :, TOPK_E:8], PAD))
                n = own.mark(dve.memset(seen[:, :], 0.0))
                need(n)
                with dve.Fori(0, B // U) as it:
                    own.turn(it, marks)
                    front_x(it * U, 0)
                    front_m(it * U, 0)
                    front_g(it * U, 0)
                    n = front_b(it * U, 0)
                    for i in range(E * U):
                        u, e = i // E, i % E
                        b, p = it * U + u, u % 2
                        dve.wait_ge(s["y_ps"], of(ph, "y_ps", b, e + 1))
                        if e == 0:
                            need_alone(n)
                        else:
                            hold(dve, s["acc"], of(ph, "acc", b, e))
                        dve.scalar_tensor_tensor(xb_of(b), Y_BANK[e % 2][:, 0:D], gates[:, p, e:e + 1], xb_of(b),
                                                 ALU.mult, ALU.add).then_inc(s["acc"], 1)
                        if e == E - 1:
                            dve.wait_ge(s["acc"], of(ph, "acc", b, E))
                            dve.sem_inc(s["x"], 1)
                        if u + 1 < U:
                            if e == 0:
                                front_x(b + 1, 1 - p)
                            if e == 3:
                                front_m(b + 1, 1 - p)
                            if e == 5:
                                front_g(b + 1, 1 - p)
                            if e == 7:
                                n = front_b(b + 1, 1 - p)
                own.done(B // U)

            def choose_tokens(ph, before, marks):
                with dve.Fori(0, B // 2) as it:
                    own.turn(it, marks)
                    for p in range(2):
                        b = it * 2 + p
                        hold(dve, s["xnT_ps"], of(ph, "xnT_ps", b, -1))
                        layernorm(ph, b, p, (s["x"], of(before, "x", b))).then_inc(s["xn"], 1)
                own.done(B // 2)
                dve.wait_ge(s["lg_ps"], of(ph, "lg_ps", B - 1))
                n = own.mark(dve.tensor_tensor(lg_all[:, :, :], bank[0][:, 0:B * E].rearrange("p (b e) -> p b e", e=E),
                                               br_row[:, :].unsqueeze(1).to_broadcast([P, B, E]), ALU.add))
                need(n)
                n = own.mark(dve.tensor_reduce(lmax_all[:, :], lg_all[:, :, :], AX, ALU.max))
                need(n)
                dve.tensor_tensor(lg_all[:, :, :], lg_all[:, :, :], lmax_all[:, :].unsqueeze(2).to_broadcast([P, B, E]),
                                  ALU.subtract).then_inc(lg_all_ready, 1)
                dve.wait_ge(lexp_all, 1)
                n = own.mark(dve.tensor_reduce(lsum_all[:, :], prob[:, :, :], AX, ALU.add))
                need(n)
                n = own.mark(dve.reciprocal(rsum_all[:, :], lsum_all[:, :]))
                need(n)
                dve.tensor_tensor(prob[:, :, :], prob[:, :, :], rsum_all[:, :].unsqueeze(2).to_broadcast([P, B, E]),
                                  ALU.mult).then_inc(prob_ready, 1)
                dve.wait_ge(probT_ready, 1)
                for rnd in range(EC_K // 8):
                    src = probT if rnd == 0 else takenT
                    n = own.mark(dve.max(ec8[:, rnd % 2, :], src))
                    need(n)
                    n = own.mark(dve.match_replace(takenT, ec8[:, rnd % 2, :], src, TAKEN))
                    need(n)
                n = own.mark(dve.tensor_scalar(takenT, takenT, TAKEN, None, ALU.is_equal))
                need(n)
                dve.sem_inc(taken_ready, 1)
                dve.wait_ge(taken_ready, 1)
                dve.tensor_tensor(probT, probT, takenT, ALU.mult).then_inc(gT_all_ready, 1)
                dve.wait_ge(taken_ps, 1)
                dve.tensor_tensor(gates_all[:, :, :], prob[:, :, :], bank[3][:, 0:B * E].rearrange("p (b e) -> p b e", e=E),
                                  ALU.mult).then_inc(ec_gates, 1)

            def expert_choice(ph):
                dve.wait_ge(ec_gates, 1)
                with dve.Fori(0, B // U) as it:
                    own.turn(it, U * (1 + NEG))
                    for i in range(NEG * U):
                        u, g = i // NEG, i % NEG
                        b, p = it * U + u, u % 2
                        if g == 0:
                            dve.wait_ge(s["b2_ps"], of(ph, "b2_ps", b))
                            n = own.mark(dve.tensor_tensor(xb_of(b), xb_of(b), O_BANK[:, 0:D], ALU.add))
                        dve.wait_ge(s["y_ps"], of(ph, "y_ps", b, g + 1))
                        for e in range(EGRP):
                            if e == 0 and g > 0:
                                hold(dve, s["acc"], of(ph, "acc", b, g))
                            else:
                                need_alone(n)
                            gcol = gates_all[:, bass.ds(b, 1), EGRP * g + e:EGRP * g + e + 1].rearrange("p b e -> p (b e)")
                            ins = dve.scalar_tensor_tensor(xb_of(b), Y_BANK[g % 2][:, D * e:D * (e + 1)], gcol, xb_of(b),
                                                           ALU.mult, ALU.add)
                            if e == 0:
                                n = own.mark(ins)
                            else:
                                ins.then_inc(s["acc"], 1)
                        if g == NEG - 1:
                            dve.wait_ge(s["acc"], of(ph, "acc", b, NEG))
                            dve.sem_inc(s["x"], 1)
                own.done(B // U)

            dve.wait_ge(ld_x, 16)
            attention("attn0", None, MARKS["attn0"])
            values(1)
            bitffn("bit0", "attn0", MARKS["bit0"])
            attention("attn1", "bit0", MARKS["attn1"])
            values(2)
            moe("moe1", "attn1", MARKS["moe1"])
            attention("attn2", "moe1", MARKS["attn2"])
            values(3)
            choose_tokens("ecr2", "attn2", 2 * NORM)
            expert_choice("ec2")
            attention("attn3", "ec2", MARKS["attn3"])
            moe("moe3", "attn3", MARKS["moe3"])


NORM, SPLIT, SHIFT, ROWS = 2, 1, NG, 1
MARKS = {
    "attn0": U * (NORM + SPLIT + SHIFT + ROWS),
    "attn1": U * (NORM + SPLIT + SHIFT + ROWS + 1),
    "attn3": U * (NORM + SPLIT + SHIFT + ROWS + 1),
    "attn2": U * (NORM + SPLIT + ROWS + 1 + NG * (ROUNDS * GH * 2 + 1)),
    "bit0": U * (NORM + 1 + 4 + 2 + 1 + 4 + 1),
    "moe1": U * (NORM + 6 + 3 + 3 + 1),
    "moe3": U * (NORM + 6 + 6 + 1),
}

_OUT_SHAPE = (B, P, D)


def kernel(**inputs):
    import numpy as _np
    import concourse.bacc as _bacc
    from concourse import mybir as _mybir
    from concourse.bass_utils import run_bass_kernel_spmd as _run

    nc = _bacc.Bacc("TRN2", target_bir_lowering=False, num_devices=1)
    arrays, aps = {}, {}
    for name, value in inputs.items():
        arr = _np.ascontiguousarray(value)
        arrays["in_" + name] = arr
        aps[name] = nc.dram_tensor("in_" + name, arr.shape, _mybir.dt.from_np(arr.dtype), kind="ExternalInput").ap()
    out = nc.dram_tensor("out_0", _OUT_SHAPE, _mybir.dt.float32, kind="ExternalOutput").ap()
    build(nc, aps, out)
    r = _run(nc, [arrays], core_ids=[0])
    return r.results[0]["out_0"]
```

```python
from contextlib import ExitStack

import concourse.bass as bass
from concourse import mybir

B = 8
P = 128
D = 128
NH = 16
DK = D // NH
NG = 4
GH = NH // NG
GW = GH * DK
NPART = P // GW
VW = DK + 1
F = 512
NC = F // P
E = 8
TOPK_E = 2
T = B * P
CAPACITY = TOPK_E * T // E
EC_K = T // E
EGRP = 2
NEG = E // EGRP
F2 = int(D * 4 * (2.0 / 3.0))
NC2 = -(-F2 // P)
FC2 = -(-F2 // NC2)
FROWS2 = [min(FC2, F2 - c * FC2) for c in range(NC2)]
TOP_ATTN = 32
ROUNDS = TOP_ATTN // 8
U = 4
LAG = 2
LEAD = 3
HALF = T // 2
HB = B // 2
LN_EPS = 1e-5
QMIN = 1e-5
NORM_EPS = 1e-9
ROUND = 12582912.0
TAKEN = -3.0e38
PAD = -2.0e38
C = DK ** -0.5

F32 = mybir.dt.float32
F32R = mybir.dt.float32r
BF16 = mybir.dt.bfloat16
U32 = mybir.dt.uint32
ALU = mybir.AluOpType
ACT = mybir.ActivationFunctionType
AX = mybir.AxisListType.X

ATTN = dict(var=1, rstd=1, xn=1, xnT_ps=1, xnT=1, q_ps=1, qb=1, q_up=1, qst=1, vc=1, s_ps=NG, sx=NG, p=NG, pt_ps=NG,
            pt=NG, pv=NG, oT=1, oq_ps=1, on=1, onT_ps=1, onT=1, o_ps=1, x=1)
ATTN0 = {k: n for k, n in ATTN.items() if k not in ("onT_ps", "onT", "o_ps")}
TOPK = {**{k: n for k, n in ATTN.items() if k not in ("sx", "p")}, "ss": NG, "topk": NG, "sd": 2 * NG, "ex": 2 * NG, "psel": NG}
BIT = dict(var=1, rstd=1, xn=1, xnT_ps=1, xnT=1, gu_ps=1, gate=1, h=1, hqT_ps=1, hqT=1, dn_ps=1, x=1)
MOE = dict(var=1, rstd=1, xn=1, xnT_ps=1, xnT=1, lg_ps=1, lmax=1, lexp=1, gates=1, h_ps=E, hT=E, y_ps=E, acc=E, x=1)
MOE1 = dict(m_var=1, m_rstd=1, m_xn=1, m_xnT_ps=1, m_xnT=1, lg_ps=1, lg=1, lmax=1, lexp=1, cnt_ps=1, cnt=1, gates=1,
            h_ps=E, hT=E, y_ps=E, ym=E, xm=E + 1)
MOE3 = dict(MOE, gT_ps=1, gT=1, b2_ps=1)
ECR = dict(var=1, rstd=1, xn=1, xnT_ps=1, xnT=1, lg_ps=1)
EC = dict(h_ps=NEG, hT=NEG, y_ps=NEG, acc=NEG, gT=1, b2_ps=1, x=1)
PHASES = [("attn0", ATTN0), ("bit0", BIT), ("attn1", ATTN), ("moe1", MOE1), ("attn2", TOPK),
          ("ecr2", ECR), ("ec2", EC), ("attn3", ATTN), ("moe3", MOE3)]
FREE = dict(oT=1, oq_ps=1, qb=1, sx=2, ss=1, pt_ps=4, pt=2, pv=2, on=1, psel=2, qst=1, hT=2, y_ps=2, acc=2, ym=1, xm=2)
LAYER = {"attn1": 0, "attn2": 1, "attn3": 2}


class Counts:

    def __init__(self):
        self.before, self.each, total = {}, {}, {}
        for _, each in PHASES:
            for what in each:
                total.setdefault(what, FREE.get(what, 0))
        for name, each in PHASES:
            self.before[name] = dict(total)
            self.each[name] = each
            for what, n in each.items():
                total[what] += n * B
        self.names = list(total)

    def of(self, phase, what, b, n=1):
        return b * self.each[phase][what] + (self.before[phase][what] + n)


class Chain:

    def __init__(self, eng, sem):
        self.eng, self.sem, self.n, self.it, self.per = eng, sem, 0, None, 0

    def mark(self, ins):
        ins.then_inc(self.sem, 1)
        self.n += 1
        return self.n

    def value(self, n):
        return n if self.it is None else self.it * self.per + n

    def turn(self, it, per):
        self.it, self.per, self.at0 = it, per, self.n

    def done(self, turns):
        assert self.n - self.at0 == self.per, f"{self.n - self.at0} marked in a turn, not {self.per}"
        self.n, self.it = self.at0 + self.per * turns, None


def build(nc, a, out):
    with ExitStack() as ctx:
        def sb(name, shape, dt=F32):
            return ctx.enter_context(nc.sbuf_tensor("sb_" + name, shape, dt))

        def sem(name):
            return ctx.enter_context(nc.semaphore(name))

        bank = [ctx.enter_context(nc.psum_tensor(f"bank{i}", [P, 512], F32)) for i in range(8)]
        S_BANK = bank[0:4]
        W_BANK, R_BANK = bank[2], bank[3]
        PT_BANK = bank[4:6]
        A_BANK, O_BANK = bank[6], bank[7]
        H_BANK, Y_BANK = bank[0:2], bank[4:6]
        W2_BANK, H2_BANK = bank[1], bank[2:4]

        def halfword(bk):
            return bk[:, 0:256].bitcast(BF16)

        x_res = sb("x_res", [P, B, D])
        ctx_tok = sb("ctx_tok", [P, B, D])
        xnT_all = ctx_tok
        ctxT = sb("ctxT", [P, T])
        k_st = sb("k_st", [P, GH, NG, B, P], F32R)
        k_raw = sb("k_raw", [P, 2 * NG, 512])
        k_part = sb("k_part", [P, NG, 512], F32R)
        v_aug = sb("v_aug", [P, B, NH, VW])
        id_rep = sb("id_rep", [P, NG, NPART, GW])
        wq_rep = sb("wq_rep", [P, 3, NG, NPART, GW])
        wk_rep = sb("wk_rep", [P, 3, NG, NPART, GW])
        wv_T = sb("wv_T", [P, 3, D])
        wo_T = sb("wo_T", [P, 3, D])
        bq_rep = sb("bq_rep", [P, 3, NG])
        bk_rep = sb("bk_rep", [P, 3, NG])
        bv_row = sb("bv_row", [P, 3, D])
        bo_row = sb("bo_row", [P, 3, D])
        temp_row = sb("temp_row", [P, NH])
        itemp_row = sb("itemp_row", [P, NH])
        temp_rep = sb("temp_rep", [P, NG])
        itemp_rep = sb("itemp_rep", [P, NG])
        ident = sb("ident", [P, P])
        head_mask = sb("head_mask", [P, GH])
        ident_b = sb("ident_b", [P, P], BF16)
        ones = sb("ones", [P, P])
        ones_b = sb("ones_b", [P, P], BF16)
        before_b = sb("before_b", [P, P], BF16)
        stats = sb("stats", [P, 2, 6])
        mv = sb("mv", [P, 2, 2])
        ve = sb("ve", [P, 2, 1])
        rstd = sb("rstd", [P, 2, 1])
        minus_half = sb("minus_half", [P, 1])
        one = sb("one", [P, 1])
        xn = sb("xn", [P, 2, D])
        xnT = sb("xnT", [P, 2, D])
        qb = sb("qb", [P, 512])
        m_stats = sb("m_stats", [P, 6])
        m_mv = sb("m_mv", [P, 2])
        m_ve = sb("m_ve", [P, 1])
        m_rstd = sb("m_rstd", [P, 1])
        cnt_sb = sb("cnt_sb", [P, E])
        v_cur = sb("v_cur", [P, 2, NH, GW])
        oT_sb = sb("oT_sb", [P, NG, P])
        q_st = sb("q_st", [P, 2, 512], F32R)
        mx = sb("mx", [P, NG, GH])
        p_sb = sb("p_sb", [P, NG, GH, P])
        pt_sb = sb("pt_sb", [P, 2, GH, P])
        rden = sb("rden", [P, 2, NH])
        on = sb("on", [P, 2, D])
        onT = sb("onT", [P, 2, D])
        t_row = sb("t_row", [P, 2, D])
        v8 = sb("v8", [P, 2, GH, ROUNDS, 8])
        shared = sb("shared", [P, 4, 512])
        gate, h0 = shared[:, 0:2, :], shared[:, 2:4, :]
        ss = shared[:, 0:2, :].rearrange("p r (j k) -> p r j k", k=P)
        sel = shared[:, 2:4, :].rearrange("p r (j k) -> p r j k", k=P)
        probT = shared[0:E, 0:2, :].rearrange("p r k -> p (r k)")
        takenT = shared[0:E, 2:4, :].rearrange("p r k -> p (r k)")
        wstat = sb("wstat", [P, 3, 3])
        amax = sb("amax", [P, 2, 2])
        aclip = sb("aclip", [P, 2, 2])
        qscale = sb("qscale", [P, 2, 2])
        deq = sb("deq", [P, 2, 3])
        xr = sb("xr", [P, 2, D])
        xq = sb("xq", [P, 2, D], BF16)
        xqT = sb("xqT", [P, 2, D], BF16)
        idle = pt_sb[:, :, :, :].rearrange("p a j k -> p (a j k)").bitcast(BF16)
        hq = idle[:, 0:2 * F].rearrange("p (a f) -> p a f", a=2)
        hqT = idle[:, 2 * F:4 * F].rearrange("p (a f) -> p a f", a=2)
        m_xn, m_xnT = ones, xr
        ys = id_rep[:, 0:2, :, :].rearrange("p g a f -> p g (a f)")
        w1 = sb("w1", [P, E, F])
        w2 = sb("w2", [P, E, NC, D])
        hT = sb("hT", [P, 2, NC, P])
        wbT = hT[:, :, :, :].rearrange("p a c k -> p (a c k)").bitcast(BF16)[:, 0:3 * 512]\
            .rearrange("p (m n) -> p m n", m=3)
        wb_q = w1[:, 0:2, :].rearrange("p e f -> p (e f)").bitcast(BF16)[:, 0:3 * 512]\
            .rearrange("p (m n) -> p m n", m=3)
        early = w2[:, :, :, :].rearrange("p e c d -> p (e c d)")
        w_raw = early[:, 0:12 * D].rearrange("p (m i) -> p m i", m=12)
        wb_raw = early[:, 12 * D:12 * D + 3 * 512].rearrange("p (m i) -> p m i", m=3)
        wr = sb("wr", [P, 3, E])
        b1_col = sb("b1_col", [P, E, NC])
        b2_sb = sb("b2_sb", [E, 2, D])
        br_row = sb("br_row", [P, E])
        bias_row = sb("bias_row", [P, D])
        lrow = sb("lrow", [P, 2, E + 6])
        top8 = sb("top8", [P, 2, 8])
        pick8 = sb("pick8", [P, 2, 8])
        lmark = sb("lmark", [P, 2, E + 6])
        nlm = sb("nlm", [P, 2, 1])
        el = sb("el", [P, 2, E])
        esum = sb("esum", [P, 2, 1])
        rsum = sb("rsum", [P, 2, 1])
        pr = sb("pr", [P, 2, E])
        maskf = sb("maskf", [P, 2, E])
        mask_b = sb("mask_b", [P, 2, E], BF16)
        seen = sb("seen", [P, E])
        seen_b = sb("seen_b", [P, 2, E], BF16)
        fits = sb("fits", [P, 2, E])
        gates = sb("gates", [P, 2, E])
        gsum = sb("gsum", [P, 2, 3])
        gT = sb("gT", [E, 2, P])
        wu2 = early[:, 0:NEG * F2].rearrange("p (g f) -> p g f", g=NEG)
        wd2 = w1[0:FC2, :, :].rearrange("p e f -> p (e f)")[:, 0:NC2 * E * D]\
            .rearrange("p (c e d) -> p c e d", c=NC2, e=E)
        bu2 = sb("bu2", [P, NEG, NC2])
        lg_all = sb("lg_all", [P, B, E])
        lmax_all = sb("lmax_all", [P, B])
        lsum_all = sb("lsum_all", [P, B])
        rsum_all = sb("rsum_all", [P, B])
        prob = sb("prob", [P, B, E])
        gates_all = lg_all
        ec8 = sb("ec8", [E, 2, 8])

        counts = Counts()
        s = {name: sem("s_" + name) for name in counts.names}
        of = counts.of
        ld_x, ld_ctx, ld_w, ld_bit = sem("ld_x"), sem("ld_ctx"), sem("ld_w"), sem("ld_bit")
        ld_small, ld_moe1, ld_moe3, ld_ec = sem("ld_small"), sem("ld_moe1"), sem("ld_moe3"), sem("ld_ec")
        const_ready = sem("const_ready")
        v_ones = sem("v_ones")
        tr_ps = sem("tr_ps")
        ctxT_ready = sem("ctxT_ready")
        w_ready = sem("w_ready")
        v0_ready = sem("v0_ready")
        wsum_ready = sem("wsum_ready")
        wtot_ps = sem("wtot_ps")
        wb_ready = sem("wb_ready")
        wbT_ps = sem("wbT_ps")
        wbT_ready = sem("wbT_ready")
        k0_split = sem("k0_split")
        k0_masked = sem("k0_masked")
        k0_scaled = sem("k0_scaled")
        k_ps = sem("k_ps")
        k_evac = sem("k_evac")
        k_upper = sem("k_upper")
        k_lower = sem("k_lower")
        k_split = sem("k_split")
        k_placed = sem("k_placed")
        v_ps = sem("v_ps")
        v_ready = sem("v_ready")
        lg_all_ready = sem("lg_all_ready")
        lexp_all = sem("lexp_all")
        prob_ready = sem("prob_ready")
        probT_ps = sem("probT_ps")
        probT_ready = sem("probT_ready")
        taken_ready = sem("taken_ready")
        taken_ps = sem("taken_ps")
        gT_all_ready = sem("gT_all_ready")
        ec_gates = sem("ec_gates")
        dve_own, act_own, pool_own = sem("dve_own"), sem("act_own"), sem("pool_own")
        xnT_two = sem("xnT_two")
        held = sem("held")
        stored = sem("stored")

        def hold(eng, what, value):
            eng.wait_ge(what, value)
            if not isinstance(value, int):
                eng.sem_inc(held, 1)

        def batches(eng, step, lead, lag, own=None, marks=0):
            first, middle = (0 if lead == LAG else -lead), (B - lead - lag) // 2
            for b in range(first, lag):
                step(b, b % 2, lambda k: 0 <= b + k < B)
            with eng.Fori(0, middle) as it:
                if own:
                    own.turn(it, marks)
                for u in range(2):
                    step(it * 2 + (lag + u), (lag + u) % 2, lambda k: True)
            if own:
                own.done(middle)
            for b in range(lag + 2 * middle, B + lag):
                step(b, b % 2, lambda k: 0 <= b + k < B)

        def xb_of(b):
            return x_res[:, bass.ds(b, 1), :].rearrange("p b d -> p (b d)")

        def slot(b, g, back):
            k = g - back
            return (b + k // NG if k // NG else b), k % NG, k // NG

        KEY_PHASES = ["attn0", "attn1", "attn2", "attn3"]
        PLACES = NPART * GH
        block = ctx.enter_context(nc.Block())
        n_small = [0]

        @block.sync
        def _(sp):
            sp.dma_start(ctx_tok[:, :, :], a["ctx_1024"].rearrange("b p d -> p b d")).then_inc(ld_ctx, 16)
            sp.dma_start(x_res[:, :, :], a["x"].rearrange("b p d -> p b d")).then_inc(ld_x, 16)
            for i, name in enumerate(("L0_ffn_w_gate", "L0_ffn_w_up")):
                sp.dma_start(wb_raw[:, i, :].rearrange("p (c i) -> p c i", c=NC),
                             a[name].rearrange("(c p) i -> p c i", p=P)).then_inc(ld_bit, 16)
            sp.dma_start(wb_raw[:, 2, :], a["L0_ffn_w_down"]).then_inc(ld_bit, 16)
            mats = ["L1_xattn_wq_w", "L1_xattn_wk_w", "L1_xattn_wv_w", "L1_xattn_proj_w",
                    "L2_xattn_Wq", "L2_xattn_Wk", "L2_xattn_Wv", "L2_xattn_Wo",
                    "L3_xattn_Wq", "L3_xattn_Wk", "L3_xattn_Wv", "L3_xattn_Wo"]
            for i, name in enumerate(mats):
                sp.dma_start(w_raw[:, i, :], a[name]).then_inc(ld_w, 16)
            temp = a["L3_xattn_temperature"].rearrange("h a b -> (h a b)")
            sp.dma_start(temp_row[:, :], temp.partition_broadcast(P)).then_inc(ld_w, 16)

            def small(dst, src):
                sp.dma_start(dst, src, allow_slow_non_contiguous=True).then_inc(ld_small, 16)
                n_small[0] += 1

            names = [("L1_xattn_wq_b", "L1_xattn_wk_b", "L1_xattn_wv_b", "L1_xattn_proj_b"),
                     ("L2_xattn_bq", "L2_xattn_bk", "L2_xattn_bv", "L2_xattn_bo"),
                     ("L3_xattn_bq", "L3_xattn_bk", "L3_xattn_bv", "L3_xattn_bo")]
            for i, (q, k, v, o) in enumerate(names):
                for part in range(NPART):
                    rows = slice(GW * part, GW * (part + 1))
                    small(bq_rep[rows, i, :], a[q].rearrange("(g h) -> h g", h=GW))
                    small(bk_rep[rows, i, :], a[k].rearrange("(g h) -> h g", h=GW))
                small(bv_row[:, i, :], a[v].partition_broadcast(P))
                small(bo_row[:, i, :], a[o].partition_broadcast(P))
            for part in range(NPART):
                for j in range(GH):
                    lo = GW * part + DK * j
                    small(temp_rep[lo:lo + DK, :], temp.rearrange("(g j) -> j g", j=GH)[j].partition_broadcast(DK))
            small(wr[:, 0, :], a["L1_ffn_w_router"])
            small(wr[:, 1, :], a["L2_ffn_Wr"])
            small(wr[:, 2, :], a["L3_ffn_Wg"])
            small(bias_row[:, :], a["L1_ffn_bias"].rearrange("a b d -> (a b d)").partition_broadcast(P))
            small(br_row[:, :], a["L2_ffn_br"].partition_broadcast(P))
            small(b2_sb[:, 0, :], a["L2_ffn_b_down"])
            small(b2_sb[:, 1, :], a["L3_ffn_b2"])
            for e in range(E):
                small(b1_col[:, e, :], a["L3_ffn_b1"][e].rearrange("(c p) -> p c", p=P))
            for g in range(NEG):
                for c, n in enumerate(FROWS2):
                    small(bu2[0:n, g, c:c + 1],
                          a["L2_ffn_b_up"][g, c * FC2:c * FC2 + n].rearrange("(f o) -> f o", o=1))

            def place_keys(i):
                for half in range(2):
                    sp.wait_ge(k_split, NG * (2 * (i - 1) + half + 1))
                    sp.wait_ge(s["s_ps"], of(KEY_PHASES[i - 1], "s_ps", B - 1, NG))
                    for part in range(NPART):
                        for j in range(GH):
                            lo = GW * part + DK * j
                            sp.dma_start(
                                k_st[lo:lo + DK, j, :, HB * half:HB * (half + 1), :]
                                .rearrange("p g b k -> p g (b k)").bitcast(F32),
                                k_part[lo:lo + DK, :, :].bitcast(F32)).then_inc(k_placed, 16)

            sp.wait_ge(ctxT_ready, 2)
            sp.wait_ge(w_ready, 3)
            sp.wait_ge(wb_ready, 1)
            for e in range(E):
                if e == 0:
                    sp.wait_ge(wbT_ps, 1)
                sp.dma_start(w1[:, e, :], a["L1_ffn_w1"][e]).then_inc(ld_moe1, 16)
                sp.dma_start(w2[:, e, :, :], a["L1_ffn_w2"][e].rearrange("(c p) d -> p c d", p=P)).then_inc(ld_moe1, 16)
            place_keys(1)
            place_keys(2)
            sp.wait_ge(s["y_ps"], of("moe1", "y_ps", B - 1, E))
            sp.dma_start(wu2, a["L2_ffn_W_up"].rearrange("g d f -> d g f")).then_inc(ld_ec, 16)
            for c, n in enumerate(FROWS2):
                sp.dma_start(wd2[0:n, c, :, :],
                             a["L2_ffn_W_down"][:, c * FC2:c * FC2 + n, :].rearrange("e f d -> f e d")).then_inc(ld_ec, 16)
            place_keys(3)
            sp.wait_ge(s["y_ps"], of("ec2", "y_ps", B - 1, NEG))
            for e in range(E):
                sp.dma_start(w1[:, e, :], a["L3_ffn_W1"][e]).then_inc(ld_moe3, 16)
                sp.dma_start(w2[:, e, :, :], a["L3_ffn_W2"][e].rearrange("(c p) d -> p c d", p=P)).then_inc(ld_moe3, 16)
            for b in range(B):
                sp.wait_ge(s["x"], of("moe3", "x", b))
                sp.dma_start(out[b], x_res[:, b, :]).then_inc(stored, 16)
            sp.wait_ge(stored, 16 * B)

        SMALL = 16 * n_small[0]

        @block.gpsimd
        def _(pool):
            own = Chain(pool, pool_own)

            def step(ins):
                pool.wait_ge(pool_own, own.mark(ins))

            step(pool.memset(ident[:, :], 0.0))
            step(pool.affine_select(out=ident[:, :], in_=ident[:, :], compare_op=ALU.not_equal, fill=1.0,
                                    base=0, pattern=[[-1, P]], channel_multiplier=1))
            pool.tensor_copy(ident_b[:, :], ident[:, :]).then_inc(const_ready, 1)
            for part in range(NPART):
                step(pool.tensor_copy(id_rep[:, :, part, :], ident[:, :].rearrange("p (g f) -> p g f", g=NG)))
            pool.memset(ones[:, :], 1.0).then_inc(const_ready, 1)
            pool.memset(ones_b[:, :], 1.0).then_inc(const_ready, 1)
            step(pool.memset(before_b[:, :], 1.0))
            pool.affine_select(out=before_b[:, :], in_=before_b[:, :], compare_op=ALU.is_gt, fill=0.0,
                               base=0, pattern=[[1, P]], channel_multiplier=-1).then_inc(const_ready, 1)
            pool.memset(minus_half[:, :], -0.5)
            pool.memset(one[:, :], 1.0)
            pool.memset(v_cur[:, :, :, :], 0.0)
            pool.memset(v_aug[:, :, :, DK:VW], 1.0).then_inc(v_ones, 1)

            def split_keys(i, half, g):
                done = half * NG + (2 * NG * (i - 1) + g)
                raw = k_raw[:, bass.ds(half * NG + g, 1), :].rearrange("p u k -> p (u k)")
                pool.wait_ge(k_evac, done + (2 * NG + 1))
                pool.tensor_copy(k_part[:, g, :], raw).then_inc(k_upper, 1)
                pool.wait_ge(k_upper, done + 1)
                rows = slice(GW, 2 * GW)
                pool.tensor_tensor(k_part[rows, g, :], raw[rows, :], k_part[rows, g, :], ALU.subtract).then_inc(k_lower, 1)
                pool.wait_ge(k_lower, done + 1)
                rows = slice(3 * GW, 4 * GW)
                pool.tensor_tensor(k_part[rows, g, :], raw[rows, :], k_part[rows, g, :], ALU.subtract).then_inc(k_split, 1)

            def scale_of(ph, b, p):
                pool.wait_ge(s["var"], of(ph, "var", b))
                pool.tensor_tensor(rstd[:, p, :], ve[:, p, :], minus_half[:, :], ALU.pow).then_inc(s["rstd"], 1)

            def norms(ph, keys=None):
                with pool.Fori(0, B // U) as it:
                    for u in range(U):
                        scale_of(ph, it * U + u, u % 2)
                        if keys is not None:
                            if u == 0:
                                pool.wait_ge(k_placed, it * (16 * PLACES) + (16 * PLACES * 2 * (keys - 1) + 1))
                            split_keys(keys, it, u)
                            pool.wait_ge(k_split, it * NG + (2 * NG * (keys - 1) + u + 1))

            def split(ph, b, p):
                hold(pool, s["qb"], of(ph, "qb", b))
                if not (isinstance(b, int) and b < 2):
                    hold(pool, s["s_ps"], of(ph, "s_ps", b - 1, 0))
                pool.tensor_tensor(q_st[:, p, :], qb[:, :], one[:, :].to_broadcast([P, 512]), ALU.mult)\
                    .then_inc(s["q_up"], 1)
                pool.wait_ge(s["q_up"], of(ph, "q_up", b))
                pool.tensor_tensor(q_st[P // 2:P, p, :], qb[P // 2:P, :], q_st[P // 2:P, p, :],
                                   ALU.subtract).then_inc(s["qst"], 1)
                pool.wait_ge(s["qst"], of(ph, "qst", b))

            def bring_values(ph, b, p):
                if not (isinstance(b, int) and b < 2):
                    pool.wait_ge(s["pv"], of(ph, "pv", b - 1, 0))
                pool.tensor_copy(v_cur[:, p, :, 0:VW], v_aug[:, bass.ds(b, 1), :, :].rearrange("p b h v -> p (b h) v"))\
                    .then_inc(s["vc"], 1)

            def experts_and_attention(mo, at):
                def add_expert(b, p, e):
                    hold(pool, s["ym"], of(mo, "ym", b, e + 1))
                    hold(pool, s["xm"], of(mo, "xm", b, e + 1))
                    pool.tensor_tensor(xb_of(b), xb_of(b), ys[:, e % 2, :], ALU.add).then_inc(s["xm"], 1)

                def shift(b, g):
                    pool.wait_ge(s["topk"], of(at, "topk", b, g + 1))
                    if not (isinstance(b, int) and b == 0):
                        hold(pool, s["pt_ps"], of(at, "pt_ps", b, g + 1 - 4))
                    pool.tensor_tensor(p_sb[:, g, :, :], ss[:, g % 2, :, :],
                                       v8[:, g % 2, :, 0, 0:1].to_broadcast([P, GH, P]), ALU.subtract).then_inc(s["sd"], 1)
                    pool.tensor_tensor(sel[:, g % 2, :, :], sel[:, g % 2, :, :],
                                       v8[:, g % 2, :, 0, 0:1].to_broadcast([P, GH, P]), ALU.subtract).then_inc(s["sd"], 1)

                def select(b, g):
                    pool.wait_ge(s["ex"], of(at, "ex", b, 2 * g + 2))
                    pool.tensor_tensor(p_sb[:, g, :, :], p_sb[:, g, :, :], sel[:, g % 2, :, :],
                                       ALU.subtract).then_inc(s["psel"], 1)

                def step(b, p, has):
                    for g in range(NG):
                        if g == 1 and has(3):
                            pool.wait_ge(s["m_var"], of(mo, "m_var", b + 3))
                            pool.tensor_tensor(m_rstd[:, :], m_ve[:, :], minus_half[:, :], ALU.pow).then_inc(s["m_rstd"], 1)
                        b1, g1, k1 = slot(b, g, 1)
                        if has(k1):
                            shift(b1, g1)
                        if g == 3 and has(1):
                            split(at, b + 1, 1 - p)
                            bring_values(at, b + 1, 1 - p)
                        if has(k1):
                            select(b1, g1)
                        if g == 0 and has(1):
                            add_expert(b + 1, 1 - p, E - 1)
                        if g == 0 and has(2):
                            hold(pool, s["m_xn"], of(mo, "m_xn", b + 2))
                            pool.tensor_tensor(xb_of(b + 2), xb_of(b + 2), bias_row[:, :], ALU.add).then_inc(s["xm"], 1)
                        if g > 0 and has(2):
                            add_expert(b + 2, p, 2 * g - 1)
                        if has(2):
                            add_expert(b + 2, p, 2 * g)
                        if g == 1 and has(1):
                            scale_of(at, b + 1, 1 - p)
                    if isinstance(b, int) and b < -1:
                        half = b + LEAD
                        pool.wait_ge(k_placed, 16 * PLACES * (2 + half) + 1)
                        for g in range(NG):
                            split_keys(2, half, g)
                            pool.wait_ge(k_split, NG * (2 + half) + g + 1)

                pool.wait_ge(ld_small, SMALL)
                pool.wait_ge(v_ready, 4)
                batches(pool, step, LEAD, 1)

            def attention(ph):
                layer = LAYER.get(ph)

                def step(b, p, has):
                    if has(2):
                        scale_of(ph, b + 2, p)
                        split(ph, b + 2, p)
                    if has(1):
                        bring_values(ph, b + 1, 1 - p)

                if layer is None:
                    pool.wait_ge(v0_ready, 1)
                else:
                    pool.wait_ge(v_ready, 2 * (layer + 1))
                for b in range(LAG):
                    scale_of(ph, b, b)
                    split(ph, b, b)
                bring_values(ph, 0, 0)
                batches(pool, step, LAG, LAG)

            attention("attn0")
            norms("bit0", 1)
            attention("attn1")
            experts_and_attention("moe1", "attn2")
            norms("ecr2", 3)
            attention("attn3")
            norms("moe3")

        @block.tensor
        def _(pe):
            for what, n in FREE.items():
                pe.sem_inc(s[what], n)

            pe.wait_ge(const_ready, 1)
            pe.wait_ge(ld_ctx, 16)
            for half in range(2):
                for i in range(4):
                    ins = pe.transpose(bank[half][:, P * i:P * (i + 1)], ctx_tok[:, 4 * half + i, :], ident[:, :])
                ins.then_inc(tr_ps, 1)
            pe.wait_ge(ld_w, 16 * 13)
            for layer in range(3):
                for i in range(4):
                    ins = pe.transpose(bank[2 + layer][:, P * i:P * (i + 1)], w_raw[:, 4 * layer + i, :], ident[:, :])
                ins.then_inc(tr_ps, 1)

            def project_keys(i):
                if i == 0:
                    pe.wait_ge(ctxT_ready, 2)
                    pe.wait_ge(const_ready, 2)
                else:
                    pe.wait_ge(ctxT_ready, 2)
                    pe.wait_ge(w_ready, 3)
                    pe.wait_ge(s["x"], of(KEY_PHASES[i - 1], "x", B - 1))
                for unit in range(2 * NG):
                    half, g = unit // NG, unit % NG
                    if unit >= 2:
                        pe.wait_ge(k_evac, 2 * NG * i + unit - 1)
                    w = id_rep[:, g, :, :] if i == 0 else wk_rep[:, i - 1, g, :, :]
                    pe.matmul(bank[6 + unit % 2][:, :], w.rearrange("p a f -> p (a f)"),
                              ctxT[:, HALF * half:HALF * (half + 1)], start=True, stop=True).then_inc(k_ps, 1)
                if i > 0:
                    for half in range(2):
                        for j in range(HB):
                            b = HB * half + j
                            ins = pe.matmul(PT_BANK[half][:, P * j:P * (j + 1)], ctxT[:, P * b:P * (b + 1)],
                                            wv_T[:, i - 1, :], start=True, stop=True)
                        ins.then_inc(v_ps, 1)
                    pe.wait_ge(k_evac, 2 * NG * (i + 1))
                    pe.wait_ge(v_ready, 2 * i)

            def attention(ph):
                layer = LAYER.get(ph)

                def front_t(b, p):
                    pe.wait_ge(s["xn"], of(ph, "xn", b))
                    pe.wait_ge(s["qb"], of(ph, "qb", b, 0))
                    pe.transpose(A_BANK[:, 0:P], xn[:, p, :], ident[:, :]).then_inc(s["xnT_ps"], 1)

                def front_q(b, p):
                    pe.wait_ge(s["xnT"], of(ph, "xnT", b))
                    for g in range(NG):
                        w = id_rep[:, g, :, :] if layer is None else wq_rep[:, layer, g, :, :]
                        ins = pe.matmul(A_BANK[:, P * g:P * (g + 1)], w.rearrange("p a f -> p (a f)"),
                                        xnT[:, p, :], start=True, stop=True)
                    ins.then_inc(s["q_ps"], 1)

                def scores(b, p, g):
                    if g == 0:
                        pe.wait_ge(s["qst"], of(ph, "qst", b))
                    pe.wait_ge(s["sx"], of(ph, "sx", b, g + 1 - 2))
                    pe.matmul(S_BANK[g % 2][:, :], q_st[:, p, P * g:P * (g + 1)],
                              k_st[:, :, g, bass.ds(b, 1), :].rearrange("p j b k -> p j (b k)"),
                              start=True, stop=True).then_inc(s["s_ps"], 1)

                def turn_weights(b, g):
                    pe.wait_ge(s["p"], of(ph, "p", b, g + 1))
                    pe.wait_ge(s["pt"], of(ph, "pt", b, g + 1 - 2))
                    for j in range(GH):
                        ins = pe.transpose(PT_BANK[g % 2][:, P * j:P * (j + 1)], p_sb[:, g, j, :], ident[:, :])
                    ins.then_inc(s["pt_ps"], 1)

                def products(b, p, g):
                    pe.wait_ge(s["pt"], of(ph, "pt", b, g + 1))
                    if g == 0:
                        pe.wait_ge(s["vc"], of(ph, "vc", b))
                        pe.wait_ge(s["oT"], of(ph, "oT", b, 0))
                    for j in range(GH):
                        ins = pe.matmul(O_BANK[GW * j:GW * (j + 1), P * g:P * (g + 1)], v_cur[:, p, GH * g + j, :],
                                        pt_sb[:, g % 2, j, :], start=True, stop=True, tile_position=(0, GW * j))
                    ins.then_inc(s["pv"], 1)

                def turn_back(b):
                    pe.wait_ge(s["oT"], of(ph, "oT", b))
                    pe.wait_ge(s["on"], of(ph, "on", b, 0))
                    for g in range(NG):
                        ins = pe.transpose(W_BANK[:, P * g:P * (g + 1)], oT_sb[:, g, :], ident[:, :])
                    ins.then_inc(s["oq_ps"], 1)

                def turn_output(b, p):
                    pe.wait_ge(s["on"], of(ph, "on", b))
                    if not (isinstance(b, int) and b == 0):
                        pe.wait_ge(s["x"], of(ph, "x", b - 1))
                    pe.transpose(R_BANK[:, 0:P], on[:, p, :], ident[:, :]).then_inc(s["onT_ps"], 1)

                def project_output(b, p):
                    pe.wait_ge(s["onT"], of(ph, "onT", b))
                    pe.matmul(R_BANK[:, 0:D], onT[:, p, :], wo_T[:, layer, :], start=True, stop=True).then_inc(s["o_ps"], 1)

                def step(b, p, has):
                    for g in range(NG):
                        if has(0):
                            scores(b, p, g)
                        b2, g2, k2 = slot(b, g, 2)
                        if has(k2):
                            turn_weights(b2, g2)
                        if g == 1 and has(-2) and layer is not None:
                            turn_output(b - 2, p)
                        if g == 2 and has(2):
                            front_t(b + 2, p)
                        if g == 2 and has(-2) and layer is not None:
                            project_output(b - 2, p)
                        if g == 3 and has(2):
                            front_q(b + 2, p)
                        b3, g3, k3 = slot(b, g, 3)
                        if has(k3):
                            products(b3, p if k3 == 0 else 1 - p, g3)
                        if g == 3 and has(-1):
                            turn_back(b - 1)

                if layer is None:
                    pe.wait_ge(k0_masked, 2 * NG)
                    pe.wait_ge(k0_scaled, 2 * NG)
                    pe.sem_inc(k_placed, 1)
                else:
                    pe.wait_ge(k_placed, 16 * PLACES * 2 * (layer + 1) + 1)
                for b in range(LAG):
                    front_t(b, b)
                    front_q(b, b)
                batches(pe, step, LAG, LAG)

            def experts_and_attention(mo, at):
                layer = LAYER[at]

                def inner(b, p, e):
                    pe.wait_ge(s["hT"], of(mo, "hT", b, e + 1 - 2))
                    for c in range(NC):
                        ins = pe.matmul(H2_BANK[e % 2][:, P * c:P * (c + 1)], w1[:, e, P * c:P * (c + 1)],
                                        m_xnT[:, p, :], start=True, stop=True)
                    ins.then_inc(s["h_ps"], 1)

                def outer(b, e):
                    pe.wait_ge(s["hT"], of(mo, "hT", b, e + 1))
                    pe.wait_ge(s["ym"], of(mo, "ym", b, e))
                    for c in range(NC):
                        ins = pe.matmul(Y_BANK[1][:, 0:D], hT[:, e % 2, c, :], w2[:, e, c, :],
                                        start=(c == 0), stop=(c == NC - 1))
                    ins.then_inc(s["y_ps"], 1)

                def step(b, p, has):
                    for g in range(NG):
                        if has(0):
                            if g == 0:
                                pe.wait_ge(s["qst"], of(at, "qst", b))
                            pe.wait_ge(s["ss"], of(at, "ss", b, g))
                            pe.matmul(S_BANK[0][:, :], q_st[:, p, P * g:P * (g + 1)],
                                      k_st[:, :, g, bass.ds(b, 1), :].rearrange("p j b k -> p j (b k)"),
                                      start=True, stop=True).then_inc(s["s_ps"], 1)
                        if g == 3 and has(3):
                            pe.wait_ge(s["lmax"], of(mo, "lmax", b + 3))
                            if has(1):
                                pe.wait_ge(s["qb"], of(at, "qb", b + 1))
                            pe.matmul(A_BANK[:, 64:64 + E], before_b[:, :], mask_b[:, 1 - p, :], start=True, stop=False)
                            pe.matmul(A_BANK[:, 64:64 + E], ones_b[:, :], seen_b[:, 1 - p, :], start=False,
                                      stop=True).then_inc(s["cnt_ps"], 1)
                        if g == 2 and has(-1):
                            pe.wait_ge(s["oT"], of(at, "oT", b - 1))
                            if not (isinstance(b, int) and b == 1):
                                pe.wait_ge(s["x"], of(at, "x", b - 2))
                            for i in range(NG):
                                ins = pe.transpose(W2_BANK[:, P * i:P * (i + 1)], oT_sb[:, i, :], ident[:, :])
                            ins.then_inc(s["oq_ps"], 1)
                        if g == 3 and has(-1):
                            pe.wait_ge(s["on"], of(at, "on", b - 1))
                            pe.transpose(W2_BANK[:, 0:P], on[:, 1 - p, :], ident[:, :]).then_inc(s["onT_ps"], 1)
                        b2, g2, k2 = slot(b, g, 2)
                        if has(k2):
                            pe.wait_ge(s["pt"], of(at, "pt", b2, g2 + 1))
                            if g2 == 0:
                                pe.wait_ge(s["vc"], of(at, "vc", b2))
                                pe.wait_ge(s["oT"], of(at, "oT", b2, 0))
                            for j in range(GH):
                                ins = pe.matmul(O_BANK[GW * j:GW * (j + 1), P * g2:P * (g2 + 1)],
                                                v_cur[:, p if k2 == 0 else 1 - p, GH * g2 + j, :],
                                                pt_sb[:, g2 % 2, j, :], start=True, stop=True, tile_position=(0, GW * j))
                            ins.then_inc(s["pv"], 1)
                        if has(2):
                            inner(b + 2, p, 2 * g)
                        if g == 0 and has(1):
                            outer(b + 1, E - 1)
                        if g > 0 and has(2):
                            outer(b + 2, 2 * g - 1)
                        if g == 1 and has(3):
                            pe.wait_ge(s["m_xn"], of(mo, "m_xn", b + 3))
                            if b is not None and not (isinstance(b, int) and b == -LEAD):
                                pe.wait_ge(s["cnt"], of(mo, "cnt", b + 2))
                            pe.transpose(A_BANK[:, 0:P], m_xn[:, :], ident[:, :]).then_inc(s["m_xnT_ps"], 1)
                        if g == 2 and has(1):
                            pe.wait_ge(s["xn"], of(at, "xn", b + 1))
                            if has(3):
                                pe.wait_ge(s["lg"], of(mo, "lg", b + 3))
                            pe.transpose(A_BANK[:, 0:P], xn[:, 1 - p, :], ident[:, :]).then_inc(s["xnT_ps"], 1)
                        if has(2):
                            inner(b + 2, p, 2 * g + 1)
                            outer(b + 2, 2 * g)
                        if g == 1 and has(3):
                            pe.wait_ge(s["m_xnT"], of(mo, "m_xnT", b + 3))
                            pe.matmul(A_BANK[:, 0:E], m_xnT[:, 1 - p, :], wr[:, 0, :], start=True,
                                      stop=True).then_inc(s["lg_ps"], 1)
                        if g == 2 and has(1):
                            pe.wait_ge(s["xnT"], of(at, "xnT", b + 1))
                            for i in range(NG):
                                ins = pe.matmul(A_BANK[:, P * i:P * (i + 1)],
                                                wq_rep[:, layer, i, :, :].rearrange("p a f -> p (a f)"),
                                                xnT[:, 1 - p, :], start=True, stop=True)
                            ins.then_inc(s["q_ps"], 1)
                        b1, g1, k1 = slot(b, g, 1)
                        if has(k1):
                            pe.wait_ge(s["psel"], of(at, "psel", b1, g1 + 1))
                            pe.wait_ge(s["pt"], of(at, "pt", b1, g1))
                            for j in range(GH):
                                ins = pe.transpose(PT_BANK[0][:, P * j:P * (j + 1)], p_sb[:, g1, j, :], ident[:, :])
                            ins.then_inc(s["pt_ps"], 1)
                        if g == 3 and has(-1):
                            pe.wait_ge(s["onT"], of(at, "onT", b - 1))
                            pe.matmul(W2_BANK[:, 0:D], onT[:, 1 - p, :], wo_T[:, layer, :], start=True,
                                      stop=True).then_inc(s["o_ps"], 1)
                    if isinstance(b, int) and b == -1:
                        pe.wait_ge(k_placed, 16 * PLACES * 2 * (layer + 1) + 1)

                pe.wait_ge(ld_moe1, 32 * E)
                pe.wait_ge(ld_small, SMALL)
                batches(pe, step, LEAD, 1)

            def bitffn(ph):
                def front(b, p):
                    pe.wait_ge(s["xn"], of(ph, "xn", b))
                    pe.transpose(halfword(A_BANK)[:, 0:P], xq[:, p, :], ident_b[:, :]).then_inc(s["xnT_ps"], 1)
                    pe.wait_ge(s["xnT"], of(ph, "xnT", b))
                    for m in range(2):
                        ins = pe.matmul(S_BANK[2 * p + m][:, :], xqT[:, p, :], wbT[:, m, :], start=True, stop=True)
                    ins.then_inc(s["gu_ps"], 1)

                pe.wait_ge(wbT_ready, 1)
                with pe.Fori(0, B // U) as it:
                    front(it * U, 0)
                    for u in range(U):
                        b, p = it * U + u, u % 2
                        if u + 1 < U:
                            if u >= 1:
                                pe.wait_ge(s["h"], of(ph, "h", b - 1))
                            front(b + 1, (u + 1) % 2)
                        pe.wait_ge(s["h"], of(ph, "h", b))
                        for c in range(NC):
                            ins = pe.transpose(halfword(PT_BANK[p])[:, P * c:P * (c + 1)], hq[:, p, P * c:P * (c + 1)],
                                               ident_b[:, :])
                        ins.then_inc(s["hqT_ps"], 1)
                        pe.wait_ge(s["hqT"], of(ph, "hqT", b))
                        if u >= 1:
                            pe.wait_ge(s["x"], of(ph, "x", b - 1))
                        for c in range(NC):
                            ins = pe.matmul(O_BANK[:, 0:D], hqT[:, p, P * c:P * (c + 1)], wbT[:, 2, P * c:P * (c + 1)],
                                            start=(c == 0), stop=(c == NC - 1))
                        ins.then_inc(s["dn_ps"], 1)

            def moe(ph):
                third = ph == "moe3"
                router = 2 if third else 0

                def front_t(b, p):
                    pe.wait_ge(s["xn"], of(ph, "xn", b))
                    pe.transpose(A_BANK[:, 0:P], xn[:, p, :], ident[:, :]).then_inc(s["xnT_ps"], 1)

                def front_l(b, p):
                    pe.wait_ge(s["xnT"], of(ph, "xnT", b))
                    pe.matmul(O_BANK[:, 0:E], xnT[:, p, :], wr[:, router, :], start=True, stop=True).then_inc(s["lg_ps"], 1)

                def front_c(b, p):
                    pe.wait_ge(s["lmax"], of(ph, "lmax", b))
                    pe.matmul(O_BANK[:, 64:64 + E], before_b[:, :], mask_b[:, p, :], start=True, stop=False)
                    pe.matmul(O_BANK[:, 64:64 + E], ones_b[:, :], seen_b[:, p, :], start=False,
                              stop=True).then_inc(s["cnt_ps"], 1)

                def front_g(b, p):
                    pe.wait_ge(s["gates"], of(ph, "gates", b))
                    pe.transpose(A_BANK[0:E, 0:P], gates[:, p, :], ident[:, :]).then_inc(s["gT_ps"], 1)

                def front_b(b, p):
                    pe.wait_ge(s["gT"], of(ph, "gT", b))
                    pe.matmul(O_BANK[:, 0:D], gT[:, p, :], b2_sb[:, 1, :], start=True, stop=True).then_inc(s["b2_ps"], 1)

                pe.wait_ge(ld_small, SMALL)
                pe.wait_ge(*((ld_moe3, 32 * E) if third else (ld_moe1, 32 * E)))
                with pe.Fori(0, B // U) as it:
                    front_t(it * U, 0)
                    front_l(it * U, 0)
                    if third:
                        front_g(it * U, 0)
                        front_b(it * U, 0)
                    else:
                        front_c(it * U, 0)
                    for i in range(E * U + 1):
                        u, e = i // E, i % E
                        b, p = it * U + u, u % 2
                        if u < U:
                            pe.wait_ge(s["hT"], of(ph, "hT", b, e + 1 - 2))
                            for c in range(NC):
                                ins = pe.matmul(H_BANK[e % 2][:, P * c:P * (c + 1)], w1[:, e, P * c:P * (c + 1)],
                                                xnT[:, p, :], start=True, stop=True)
                            ins.then_inc(s["h_ps"], 1)
                        if i >= 1:
                            b1, e1 = it * U + (i - 1) // E, (i - 1) % E
                            pe.wait_ge(s["hT"], of(ph, "hT", b1, e1 + 1))
                            pe.wait_ge(s["acc"], of(ph, "acc", b1, e1 + 1 - 2))
                            for c in range(NC):
                                ins = pe.matmul(Y_BANK[e1 % 2][:, 0:D], hT[:, e1 % 2, c, :], w2[:, e1, c, :],
                                                start=(c == 0), stop=(c == NC - 1))
                            ins.then_inc(s["y_ps"], 1)
                        if u + 1 < U:
                            q = (u + 1) % 2
                            if e == 1:
                                front_t(b + 1, q)
                            if e == 2:
                                front_l(b + 1, q)
                            if e == 4 and not third:
                                front_c(b + 1, q)
                            if e == 6 and third:
                                front_g(b + 1, q)
                            if e == 7 and third:
                                front_b(b + 1, q)

            def choose_tokens(ph):
                with pe.Fori(0, B // 2) as it:
                    for p in range(2):
                        b = it * 2 + p
                        pe.wait_ge(s["xn"], of(ph, "xn", b))
                        pe.transpose(PT_BANK[p][:, 0:P], xn[:, p, :], ident[:, :]).then_inc(s["xnT_ps"], 1)
                        pe.wait_ge(s["xnT"], of(ph, "xnT", b))
                        pe.matmul(bank[0][:, bass.ds(b * E, E)], xnT[:, p, :], wr[:, 1, :],
                                  start=True, stop=True).then_inc(s["lg_ps"], 1)
                pe.wait_ge(prob_ready, 1)
                for b in range(B):
                    ins = pe.transpose(bank[1 + b // HB][0:E, P * (b % HB):P * (b % HB + 1)], prob[:, b, :], ident[:, :])
                ins.then_inc(probT_ps, 1)
                pe.wait_ge(taken_ready, 1)
                for b in range(B):
                    ins = pe.transpose(bank[3][:, E * b:E * (b + 1)], takenT[:, P * b:P * (b + 1)], ident[0:E, 0:E])
                ins.then_inc(taken_ps, 1)

            def expert_choice(ph):
                pe.wait_ge(ld_ec, 16 * (1 + NC2))
                with pe.Fori(0, B // U) as it:
                    for i in range(NEG * U + 1):
                        u, g = i // NEG, i % NEG
                        b, p = it * U + u, u % 2
                        if u < U:
                            if g == 0:
                                pe.wait_ge(s["gT"], of(ph, "gT", b))
                                if u >= 1:
                                    pe.wait_ge(s["acc"], of(ph, "acc", b - 1, 1))
                                pe.matmul(O_BANK[:, 0:D], gT[:, p, :], b2_sb[:, 0, :], start=True,
                                          stop=True).then_inc(s["b2_ps"], 1)
                            pe.wait_ge(s["hT"], of(ph, "hT", b, g + 1 - 2))
                            for c, n in enumerate(FROWS2):
                                ins = pe.matmul(H_BANK[g % 2][0:n, P * c:P * (c + 1)], wu2[:, g, FC2 * c:FC2 * c + n],
                                                xnT_all[:, bass.ds(b, 1), :].rearrange("p b t -> p (b t)"),
                                                start=True, stop=True)
                            ins.then_inc(s["h_ps"], 1)
                        if i >= 1:
                            b1, g1 = it * U + (i - 1) // NEG, (i - 1) % NEG
                            pe.wait_ge(s["hT"], of(ph, "hT", b1, g1 + 1))
                            pe.wait_ge(s["acc"], of(ph, "acc", b1, g1 + 1 - 2))
                            for c, n in enumerate(FROWS2):
                                ins = pe.matmul(Y_BANK[g1 % 2][:, 0:EGRP * D], hT[0:n, g1 % 2, c, :],
                                                wd2[0:n, c, EGRP * g1:EGRP * (g1 + 1), :],
                                                start=(c == 0), stop=(c == NC2 - 1))
                            ins.then_inc(s["y_ps"], 1)

            project_keys(0)
            pe.wait_ge(wsum_ready, 3)
            pe.wait_ge(const_ready, 4)
            pe.matmul(bank[5][:, 0:3], ones[:, :], wstat[:, 0, :], start=True, stop=True).then_inc(wtot_ps, 1)
            pe.wait_ge(wb_ready, 1)
            pe.wait_ge(ctxT_ready, 2)
            pe.wait_ge(w_ready, 3)
            for m in range(3):
                for c in range(NC):
                    ins = pe.transpose(halfword(bank[m])[:, P * c:P * (c + 1)], wb_q[:, m, P * c:P * (c + 1)], ident_b[:, :])
            ins.then_inc(wbT_ps, 1)
            pe.wait_ge(wbT_ready, 1)
            pe.wait_ge(k_evac, 2 * NG)
            attention("attn0")
            project_keys(1)
            bitffn("bit0")
            attention("attn1")
            project_keys(2)
            experts_and_attention("moe1", "attn2")
            project_keys(3)
            choose_tokens("ecr2")
            expert_choice("ec2")
            attention("attn3")
            moe("moe3")

        @block.scalar
        def _(act):
            own = Chain(act, act_own)
            act.wait_ge(tr_ps, 1)
            act.copy(ctxT[:, 0:HALF], bank[0][:, :]).then_inc(ctxT_ready, 1)
            act.wait_ge(tr_ps, 2)
            act.copy(ctxT[:, HALF:T], bank[1][:, :]).then_inc(ctxT_ready, 1)

            def scale_keys(unit):
                half, g = unit // NG, unit % NG
                act.wait_ge(k0_split, unit + 1)
                for j in range(GH // 2, GH):
                    ins = act.activation(k_st[:, j, g, HB * half:HB * (half + 1), :].rearrange("p b k -> p (b k)"),
                                         k_part[:, g, :], ACT.Copy, scale=head_mask[:, j:j + 1])
                ins.then_inc(k0_scaled, 1)

            def evacuate_keys(i):
                for unit in range(2 * NG):
                    act.wait_ge(k_ps, 2 * NG * i + unit + 1)
                    if i > 0 and unit == 0:
                        if i == 1:
                            act.wait_ge(k0_split, 2 * NG)
                        else:
                            act.wait_ge(k_split, 2 * NG * (i - 1))
                        act.wait_ge(ld_small, SMALL)
                    if i == 0:
                        act.copy(k_raw[:, unit, :], bank[6 + unit % 2][:, :]).then_inc(k_evac, 1)
                        if unit >= 1:
                            scale_keys(unit - 1)
                    else:
                        act.activation(k_raw[:, unit, :], bank[6 + unit % 2][:, :], ACT.Identity,
                                       bias=bk_rep[:, i - 1, unit % NG:unit % NG + 1]).then_inc(k_evac, 1)

            evacuate_keys(0)
            scale_keys(2 * NG - 1)
            act.wait_ge(ld_bit, 48)
            for m in range(3):
                act.activation(shared[:, m, :], wb_raw[:, m, :], ACT.Abs, accum_out=wstat[:, 0, m:m + 1]).then_inc(wsum_ready, 1)
            act.wait_ge(wbT_ps, 1)
            for m in range(3):
                ins = act.copy(wbT[:, m, :], halfword(bank[m]))
            ins.then_inc(wbT_ready, 1)

            def attention(ph):
                layer = LAYER.get(ph)

                def front_t(b, p):
                    act.wait_ge(s["xnT_ps"], of(ph, "xnT_ps", b))
                    act.copy(xnT[:, p, :], A_BANK[:, 0:P]).then_inc(s["xnT"], 1)

                def front_q(b, p):
                    act.wait_ge(s["q_ps"], of(ph, "q_ps", b))
                    hold(act, s["qst"], of(ph, "qst", b, 0))
                    if layer is None:
                        act.copy(qb[:, :], A_BANK[:, :]).then_inc(s["qb"], 1)
                    else:
                        for g in range(NG):
                            ins = act.activation(qb[:, P * g:P * (g + 1)], A_BANK[:, P * g:P * (g + 1)], ACT.Identity,
                                                 bias=bq_rep[:, layer, g:g + 1])
                        ins.then_inc(s["qb"], 1)

                def weights(b, g):
                    act.wait_ge(s["sx"], of(ph, "sx", b, g + 1))
                    flat = p_sb[:, g, :, :].rearrange("p j k -> p (j k)")
                    act.activation(flat, flat, ACT.Exp, scale=C).then_inc(s["p"], 1)

                def copy_weights(b, g):
                    act.wait_ge(s["pt_ps"], of(ph, "pt_ps", b, g + 1))
                    hold(act, s["pv"], of(ph, "pv", b, g + 1 - 2))
                    act.copy(pt_sb[:, g % 2, :, :].rearrange("p j k -> p (j k)"), PT_BANK[g % 2][:, :]).then_inc(s["pt"], 1)

                def copy_products(b):
                    act.wait_ge(s["pv"], of(ph, "pv", b, NG))
                    hold(act, s["oq_ps"], of(ph, "oq_ps", b, 0))
                    act.copy(oT_sb[:, :, :].rearrange("p g q -> p (g q)"), O_BANK[:, :]).then_inc(s["oT"], 1)

                def step(b, p, has):
                    for g in range(NG):
                        if g == 3 and has(-1):
                            copy_products(b - 1)
                        b2, g2, k2 = slot(b, g, 2)
                        if has(k2):
                            copy_weights(b2, g2)
                        if has(0):
                            weights(b, g)
                        if g == 1 and has(-2) and layer is not None:
                            act.wait_ge(s["onT_ps"], of(ph, "onT_ps", b - 2))
                            act.copy(onT[:, p, :], R_BANK[:, 0:P]).then_inc(s["onT"], 1)
                        if g == 2 and has(2):
                            front_t(b + 2, p)
                        if g == 3 and has(2):
                            front_q(b + 2, p)

                for b in range(LAG):
                    front_t(b, b)
                    front_q(b, b)
                batches(act, step, LAG, LAG)

            def experts_and_attention(mo, at):
                layer = LAYER[at]

                def gelu(b, e):
                    act.wait_ge(s["h_ps"], of(mo, "h_ps", b, e + 1))
                    hold(act, s["y_ps"], of(mo, "y_ps", b, e + 1 - 2))
                    act.activation(hT[:, e % 2, :, :].rearrange("p c k -> p (c k)"), H2_BANK[e % 2][:, :],
                                   ACT.Gelu_apprx_tanh).then_inc(s["hT"], 1)

                def weigh(b, p, e):
                    if e == 0:
                        hold(act, s["gates"], of(mo, "gates", b))
                    hold(act, s["xm"], of(mo, "xm", b, e))
                    hold(act, s["y_ps"], of(mo, "y_ps", b, e + 1))
                    act.activation(ys[:, e % 2, :], Y_BANK[1][:, 0:D], ACT.Copy, scale=gates[:, p, e:e + 1]).then_inc(s["ym"], 1)

                def step(b, p, has):
                    for g in range(NG):
                        if has(0):
                            act.wait_ge(s["s_ps"], of(at, "s_ps", b, g + 1))
                            hold(act, s["psel"], of(at, "psel", b, g + 1 - 2))
                            act.copy(ss[:, g % 2, :, :].rearrange("p j k -> p (j k)"), S_BANK[0][:, :]).then_inc(s["ss"], 1)
                        if g == 3 and has(3):
                            hold(act, s["cnt_ps"], of(mo, "cnt_ps", b + 3))
                            act.copy(cnt_sb[:, :], A_BANK[:, 64:64 + E]).then_inc(s["cnt"], 1)
                            hold(act, s["lmax"], of(mo, "lmax", b + 3))
                            act.activation(el[:, 1 - p, :], lrow[:, 1 - p, 0:E], ACT.Exp, bias=nlm[:, 1 - p, :],
                                           accum_out=esum[:, 1 - p, :]).then_inc(s["lexp"], 1)
                        b1, g1, k1 = slot(b, g, 1)
                        if has(k1):
                            flat = p_sb[:, g1, :, :].rearrange("p j k -> p (j k)")
                            act.wait_ge(s["sd"], of(at, "sd", b1, 2 * g1 + 1))
                            act.activation(flat, flat, ACT.Exp, scale=C).then_inc(s["ex"], 1)
                            flat = sel[:, g1 % 2, :, :].rearrange("p j k -> p (j k)")
                            act.wait_ge(s["sd"], of(at, "sd", b1, 2 * g1 + 2))
                            act.activation(flat, flat, ACT.Exp, scale=C).then_inc(s["ex"], 1)
                        if has(2):
                            gelu(b + 2, 2 * g)
                        if g == 0 and has(1):
                            weigh(b + 1, 1 - p, E - 1)
                        if g > 0 and has(2):
                            weigh(b + 2, p, 2 * g - 1)
                        if g == 1 and has(3):
                            act.wait_ge(s["m_xnT_ps"], of(mo, "m_xnT_ps", b + 3))
                            act.copy(m_xnT[:, 1 - p, :], A_BANK[:, 0:P]).then_inc(s["m_xnT"], 1)
                        if g == 2 and has(1):
                            act.wait_ge(s["xnT_ps"], of(at, "xnT_ps", b + 1))
                            act.copy(xnT[:, 1 - p, :], A_BANK[:, 0:P]).then_inc(s["xnT"], 1)
                        if g == 3 and has(-1):
                            act.wait_ge(s["onT_ps"], of(at, "onT_ps", b - 1))
                            act.copy(onT[:, 1 - p, :], W2_BANK[:, 0:P]).then_inc(s["onT"], 1)
                        if has(2):
                            gelu(b + 2, 2 * g + 1)
                            weigh(b + 2, p, 2 * g)
                        if g == 1 and has(3):
                            hold(act, s["lg_ps"], of(mo, "lg_ps", b + 3))
                            act.copy(lrow[:, 1 - p, 0:E], A_BANK[:, 0:E]).then_inc(s["lg"], 1)
                        if g == 2 and has(1):
                            act.wait_ge(s["q_ps"], of(at, "q_ps", b + 1))
                            hold(act, s["qst"], of(at, "qst", b + 1, 0))
                            for i in range(NG):
                                ins = act.activation(qb[:, P * i:P * (i + 1)], A_BANK[:, P * i:P * (i + 1)], ACT.Identity,
                                                     bias=bq_rep[:, layer, i:i + 1])
                            ins.then_inc(s["qb"], 1)
                        if has(k1):
                            act.wait_ge(s["pt_ps"], of(at, "pt_ps", b1, g1 + 1))
                            hold(act, s["pv"], of(at, "pv", b1, g1 + 1 - 2))
                            act.copy(pt_sb[:, g1 % 2, :, :].rearrange("p j k -> p (j k)"), PT_BANK[0][:, :])\
                               .then_inc(s["pt"], 1)
                        if g == 1 and has(-1):
                            act.wait_ge(s["pv"], of(at, "pv", b - 1, NG))
                            hold(act, s["oq_ps"], of(at, "oq_ps", b - 1, 0))
                            act.copy(oT_sb[:, :, :].rearrange("p g q -> p (g q)"), O_BANK[:, :]).then_inc(s["oT"], 1)

                batches(act, step, LEAD, 1)

            def bitffn(ph):
                def front(b, p):
                    act.wait_ge(s["xnT_ps"], of(ph, "xnT_ps", b))
                    act.copy(xqT[:, p, :], halfword(A_BANK)[:, 0:P]).then_inc(s["xnT"], 1)
                    act.wait_ge(s["gu_ps"], of(ph, "gu_ps", b))
                    act.activation(gate[:, p, :], S_BANK[2 * p][:, :], ACT.Silu, scale=deq[:, p, 0:1]).then_inc(s["gate"], 1)

                with act.Fori(0, B // U) as it:
                    front(it * U, 0)
                    for u in range(U):
                        b, p = it * U + u, u % 2
                        if u + 1 < U:
                            front(b + 1, (u + 1) % 2)
                        act.wait_ge(s["hqT_ps"], of(ph, "hqT_ps", b))
                        act.copy(hqT[:, p, :], halfword(PT_BANK[p])).then_inc(s["hqT"], 1)

            def moe(ph):
                third = ph == "moe3"

                def front_t(b, p):
                    act.wait_ge(s["xnT_ps"], of(ph, "xnT_ps", b))
                    act.copy(xnT[:, p, :], A_BANK[:, 0:P]).then_inc(s["xnT"], 1)

                def front_e(b, p):
                    act.wait_ge(s["lmax"], of(ph, "lmax", b))
                    act.activation(el[:, p, :], lrow[:, p, 0:E], ACT.Exp, bias=nlm[:, p, :],
                                   accum_out=esum[:, p, :]).then_inc(s["lexp"], 1)

                def front_g(b, p):
                    act.wait_ge(s["gT_ps"], of(ph, "gT_ps", b))
                    act.copy(gT[:, p, :], A_BANK[0:E, 0:P]).then_inc(s["gT"], 1)

                with act.Fori(0, B // U) as it:
                    front_t(it * U, 0)
                    front_e(it * U, 0)
                    if third:
                        front_g(it * U, 0)
                    for i in range(E * U):
                        u, e = i // E, i % E
                        b = it * U + u
                        act.wait_ge(s["h_ps"], of(ph, "h_ps", b, e + 1))
                        hold(act, s["y_ps"], of(ph, "y_ps", b, e + 1 - 2))
                        if third:
                            for c in range(NC):
                                ins = act.activation(hT[:, e % 2, c, :], H_BANK[e % 2][:, P * c:P * (c + 1)], ACT.Gelu,
                                                     bias=b1_col[:, e, c:c + 1])
                        else:
                            ins = act.activation(hT[:, e % 2, :, :].rearrange("p c k -> p (c k)"), H_BANK[e % 2][:, :],
                                                 ACT.Gelu_apprx_tanh)
                        ins.then_inc(s["hT"], 1)
                        if u + 1 < U:
                            q = (u + 1) % 2
                            if e == 1:
                                front_t(b + 1, q)
                            if e == 4:
                                front_e(b + 1, q)
                            if e == 6 and third:
                                front_g(b + 1, q)

            def choose_tokens(ph):
                with act.Fori(0, B // 2) as it:
                    for p in range(2):
                        b = it * 2 + p
                        act.wait_ge(s["xnT_ps"], of(ph, "xnT_ps", b))
                        hold(act, s["lg_ps"], of(ph, "lg_ps", b, -1))
                        act.copy(xnT[:, p, :], PT_BANK[p][:, 0:P]).then_inc(xnT_two, 1)
                        act.copy(xnT_all[:, bass.ds(b, 1), :].rearrange("p b t -> p (b t)"),
                                 PT_BANK[p][:, 0:P]).then_inc(s["xnT"], 1)
                act.wait_ge(lg_all_ready, 1)
                act.activation(prob[:, :, :], lg_all[:, :, :], ACT.Exp).then_inc(lexp_all, 1)
                act.wait_ge(probT_ps, 1)
                for half in range(2):
                    ins = act.copy(probT[:, HALF * half:HALF * (half + 1)], bank[1 + half][0:E, :])
                ins.then_inc(probT_ready, 1)

            def expert_choice(ph):
                act.wait_ge(gT_all_ready, 1)
                with act.Fori(0, B // U) as it:
                    for i in range(NEG * U):
                        u, g = i // NEG, i % NEG
                        b, p = it * U + u, u % 2
                        if g == 0:
                            if u >= 2:
                                hold(act, s["b2_ps"], of(ph, "b2_ps", b - 2))
                            act.copy(gT[:, p, :], probT[:, bass.ds(b * P, P)]).then_inc(s["gT"], 1)
                        act.wait_ge(s["h_ps"], of(ph, "h_ps", b, g + 1))
                        hold(act, s["y_ps"], of(ph, "y_ps", b, g + 1 - 2))
                        for c, n in enumerate(FROWS2):
                            ins = act.activation(hT[0:n, g % 2, c, :], H_BANK[g % 2][0:n, P * c:P * (c + 1)], ACT.Silu,
                                                 bias=bu2[0:n, g, c:c + 1])
                        ins.then_inc(s["hT"], 1)

            attention("attn0")
            evacuate_keys(1)
            bitffn("bit0")
            attention("attn1")
            evacuate_keys(2)
            experts_and_attention("moe1", "attn2")
            evacuate_keys(3)
            choose_tokens("ecr2")
            expert_choice("ec2")
            attention("attn3")
            moe("moe3")

        @block.vector
        def _(dve):
            own = Chain(dve, dve_own)

            def need(n):
                dve.wait_ge(dve_own, own.value(n))

            def need_alone(n):
                hold(dve, dve_own, own.value(n))

            def moments(ph, b, p, x_ready=None):
                if x_ready is not None:
                    hold(dve, *x_ready)
                n = own.mark(dve.bn_stats(stats[:, p, :], xb_of(b)))
                need_alone(n)
                n = own.mark(dve.bn_aggr(mv[:, p, :], stats[:, p, :]))
                need(n)
                dve.tensor_scalar(ve[:, p, :], mv[:, p, 1:2], LN_EPS, None, ALU.add).then_inc(s["var"], 1)

            def scaled(ph, b, p):
                dve.wait_ge(s["rstd"], of(ph, "rstd", b))
                return dve.tensor_scalar(xn[:, p, :], xb_of(b), mv[:, p, 0:1], rstd[:, p, :], ALU.subtract, ALU.mult)

            def layernorm(ph, b, p, x_ready=None):
                moments(ph, b, p, x_ready)
                return scaled(ph, b, p)

            dve.wait_ge(ld_ctx, 16)
            dve.wait_ge(v_ones, 1)
            dve.tensor_copy(v_aug[:, :, :, 0:DK], ctx_tok[:, :, :].rearrange("p b (h d) -> p b h d", h=NH))\
               .then_inc(v0_ready, 1)
            dve.wait_ge(const_ready, 1)
            n = own.mark(dve.tensor_reduce(head_mask[:, :], ident[:, :].rearrange("p (a j d) -> p j a d", a=NPART, j=GH),
                                           mybir.AxisListType.XY, ALU.add))
            for unit in range(2 * NG):
                half, g = unit // NG, unit % NG
                dve.wait_ge(k_evac, unit + 1)
                if half > 0:
                    dve.wait_ge(k0_masked, unit + 1 - NG)
                    dve.wait_ge(k0_scaled, unit + 1 - NG)
                n = own.mark(dve.tensor_copy(k_part[:, g, :], k_raw[:, unit, :]))
                need(n)
                for part in (1, 3):
                    rows = slice(GW * part, GW * (part + 1))
                    ins = dve.tensor_tensor(k_part[rows, g, :], k_raw[rows, unit, :], k_part[rows, g, :], ALU.subtract)
                    if part == 1:
                        n = own.mark(ins)
                ins.then_inc(k0_split, 1)
                need(n)
                dve.wait_ge(k0_split, unit + 1)
                for j in range(GH // 2):
                    ins = dve.tensor_scalar(k_st[:, j, g, HB * half:HB * (half + 1), :].rearrange("p b k -> p (b k)"),
                                            k_part[:, g, :], head_mask[:, j:j + 1], None, ALU.mult)
                ins.then_inc(k0_masked, 1)
            dve.wait_ge(ld_w, 16 * 13)
            n = own.mark(dve.reciprocal(itemp_row[:, :], temp_row[:, :]))
            need(n)
            for layer in range(3):
                dve.wait_ge(tr_ps, 3 + layer)
                wt = bank[2 + layer][:, :].rearrange("p (m g f) -> p m g f", m=4, g=NG)
                for part in range(NPART):
                    if layer == 2:
                        scale = itemp_row[:, :].rearrange("p (g j o) -> p g j o", g=NG, o=1).to_broadcast([P, NG, GH, DK])
                        dve.tensor_tensor(wq_rep[:, layer, :, part, :].rearrange("p g (j d) -> p g j d", d=DK),
                                          wt[:, 0, :, :].rearrange("p g (j d) -> p g j d", d=DK), scale, ALU.mult)
                    else:
                        dve.tensor_copy(wq_rep[:, layer, :, part, :], wt[:, 0, :, :])
                    dve.tensor_copy(wk_rep[:, layer, :, part, :], wt[:, 1, :, :])
                dve.tensor_copy(wv_T[:, layer, :], bank[2 + layer][:, 2 * D:3 * D])
                dve.tensor_copy(wo_T[:, layer, :], bank[2 + layer][:, 3 * D:4 * D]).then_inc(w_ready, 1)
            dve.wait_ge(wtot_ps, 1)
            n = own.mark(dve.tensor_scalar(wstat[:, 1, :], bank[5][:, 0:3], 1.0 / (F * D), QMIN, ALU.mult, ALU.max))
            need(n)
            n = own.mark(dve.reciprocal(wstat[:, 2, :], wstat[:, 1, :]))
            need(n)
            for m in range(3):
                n = own.mark(dve.tensor_scalar(wb_raw[:, m, :], wb_raw[:, m, :], wstat[:, 2, m:m + 1], ROUND,
                                               ALU.mult, ALU.add))
            need(n)
            for m in range(3):
                n = own.mark(dve.tensor_scalar(wb_raw[:, m, :], wb_raw[:, m, :], ROUND, 1.0, ALU.subtract, ALU.min))
            need(n)
            for m in range(3):
                ins = dve.tensor_scalar(wb_q[:, m, :], wb_raw[:, m, :], -1.0, None, ALU.max)
            ins.then_inc(wb_ready, 1)

            def values(i):
                for half in range(2):
                    dve.wait_ge(v_ps, 2 * (i - 1) + half + 1)
                    bias = bv_row[:, i - 1, :].rearrange("p (o h d) -> p o h d", o=1, h=NH)
                    for j in range(HB):
                        ins = dve.tensor_tensor(v_aug[:, HB * half + j, :, 0:DK],
                                                PT_BANK[half][:, P * j:P * (j + 1)].rearrange("p (h d) -> p h d", h=NH),
                                                bias[:, 0, :, :], ALU.add)
                    ins.then_inc(v_ready, 1)

            def normalize(ph, b, p, bank_w):
                dve.wait_ge(s["oq_ps"], of(ph, "oq_ps", b))
                o = bank_w[:, :].rearrange("p (h v) -> p h v", h=NH)
                n = own.mark(dve.reciprocal(rden[:, p, :], o[:, :, DK]))
                need(n)
                dve.tensor_tensor(on[:, p, :].rearrange("p (h d) -> p h d", h=NH), o[:, :, 0:DK],
                                  rden[:, p, :].unsqueeze(2).to_broadcast([P, NH, DK]), ALU.mult).then_inc(s["on"], 1)

            def add(ph, b, p, bank_o):
                layer = LAYER.get(ph)
                if layer is None:
                    dve.wait_ge(s["on"], of(ph, "on", b))
                    dve.tensor_tensor(xb_of(b), xb_of(b), on[:, p, :], ALU.add).then_inc(s["x"], 1)
                else:
                    dve.wait_ge(s["o_ps"], of(ph, "o_ps", b))
                    n = own.mark(dve.tensor_tensor(t_row[:, p, :], bank_o[:, 0:D], bo_row[:, layer, :], ALU.add))
                    need(n)
                    dve.tensor_tensor(xb_of(b), xb_of(b), t_row[:, p, :], ALU.add).then_inc(s["x"], 1)

            def attention(ph, before, marks):
                layer = LAYER.get(ph)

                def shift(b, g):
                    dve.wait_ge(s["s_ps"], of(ph, "s_ps", b, g + 1))
                    scores = S_BANK[g % 2][:, :].rearrange("p (j k) -> p j k", j=GH)
                    n = own.mark(dve.tensor_reduce(mx[:, g, :], scores, AX, ALU.max))
                    hold(dve, s["pt_ps"], of(ph, "pt_ps", b, g + 1 - 4))
                    need(n)
                    dve.tensor_tensor(p_sb[:, g, :, :], scores, mx[:, g, :].unsqueeze(2).to_broadcast([P, GH, P]),
                                      ALU.subtract).then_inc(s["sx"], 1)

                def step(b, p, has):
                    for g in range(NG):
                        if has(0):
                            shift(b, g)
                        if g == 0 and has(-2):
                            normalize(ph, b - 2, p, W_BANK)
                            if layer is None:
                                add(ph, b - 2, p, R_BANK)
                        if g == 0 and has(2):
                            moments(ph, b + 2, p, (s["x"], of(before, "x", b + 2)) if before else None)
                        if g == 1 and has(2):
                            scaled(ph, b + 2, p).then_inc(s["xn"], 1)
                        if g == 3 and has(-2) and layer is not None:
                            add(ph, b - 2, p, R_BANK)

                for b in range(LAG):
                    moments(ph, b, b, (s["x"], of(before, "x", b)) if before else None)
                    scaled(ph, b, b).then_inc(s["xn"], 1)
                batches(dve, step, LAG, LAG, own, marks)

            def experts_and_attention(mo, at, before, marks):
                layer = LAYER[at]

                def search(b, g, between):
                    r = g % 2
                    if b is not None:
                        hold(dve, s["ss"], of(at, "ss", b, g + 1))
                    taken = [None] * GH
                    for rnd in range(ROUNDS):
                        if b is not None:
                            src = ss if rnd == 0 else sel
                            found = [None] * GH
                            for j in range(GH):
                                if rnd > 0 and j % 2 == 0:
                                    need_alone(taken[j + 1])
                                found[j] = own.mark(dve.max(v8[:, r, j, rnd, :], src[:, r, j, :]))
                            for j in range(GH):
                                if j % 2 == 0:
                                    need_alone(found[j + 1])
                                taken[j] = own.mark(dve.match_replace(sel[:, r, j, :], v8[:, r, j, rnd, :], src[:, r, j, :],
                                                                      TAKEN))
                        between(g, rnd)
                    if b is not None:
                        need(taken[-1])
                        dve.sem_inc(s["topk"], 1)

                def step(b, p, has):
                    q = 1 - p

                    def between(g, rnd):
                        if has(3):
                            x3 = x_res[:, bass.ds(b + 3, 1), :].rearrange("p b d -> p (b d)")
                            if (g, rnd) == (0, 0):
                                hold(dve, s["x"], of(before, "x", b + 3))
                                marked["m"] = own.mark(dve.bn_stats(m_stats[:, :], x3))
                            if (g, rnd) == (0, 1):
                                need_alone(marked["m"])
                                marked["m"] = own.mark(dve.bn_aggr(m_mv[:, :], m_stats[:, :]))
                            if (g, rnd) == (0, 2):
                                need(marked["m"])
                                dve.tensor_scalar(m_ve[:, :], m_mv[:, 1:2], LN_EPS, None, ALU.add).then_inc(s["m_var"], 1)
                            if (g, rnd) == (1, 0):
                                dve.wait_ge(s["m_rstd"], of(mo, "m_rstd", b + 3))
                                dve.tensor_scalar(m_xn[:, :], x3, m_mv[:, 0:1], m_rstd[:, :], ALU.subtract,
                                                  ALU.mult).then_inc(s["m_xn"], 1)
                            if (g, rnd) == (2, 0):
                                hold(dve, s["lg"], of(mo, "lg", b + 3))
                                marked["m"] = own.mark(dve.max(top8[:, q, :], lrow[:, q, :]))
                            if (g, rnd) == (2, 1):
                                need(marked["m"])
                                marked["m"] = own.mark(dve.tensor_copy(pick8[:, q, 0:TOPK_E], top8[:, q, 0:TOPK_E]))
                                own.mark(dve.tensor_scalar(nlm[:, q, :], top8[:, q, 0:1], -1.0, None, ALU.mult))
                                need_alone(marked["m"])
                                marked["m"] = own.mark(dve.match_replace(lmark[:, q, :], pick8[:, q, :], lrow[:, q, :], TAKEN))
                            if (g, rnd) == (2, 2):
                                need(marked["m"])
                                marked["m"] = own.mark(dve.tensor_scalar(maskf[:, q, :], lmark[:, q, 0:E], TAKEN, None,
                                                                         ALU.is_equal))
                            if (g, rnd) == (2, 3):
                                own.mark(dve.tensor_copy(seen_b[:, q, :], seen[:, :]))
                                need(marked["m"])
                                own.mark(dve.tensor_copy(mask_b[:, q, :], maskf[:, q, :]))
                                need(own.n)
                                dve.tensor_tensor(seen[:, :], seen[:, :], maskf[:, q, :], ALU.add).then_inc(s["lmax"], 1)
                            if (g, rnd) == (3, 1):
                                dve.wait_ge(s["lexp"], of(mo, "lexp", b + 3))
                                marked["m"] = own.mark(dve.reciprocal(rsum[:, q, :], esum[:, q, :]))
                            if (g, rnd) == (3, 2):
                                need(marked["m"])
                                marked["m"] = own.mark(dve.scalar_tensor_tensor(pr[:, q, :], el[:, q, :], rsum[:, q, :],
                                                                                maskf[:, q, :], ALU.mult, ALU.mult))
                            if (g, rnd) == (3, 3):
                                hold(dve, s["cnt"], of(mo, "cnt", b + 3))
                                need(marked["m"])
                                dve.scalar_tensor_tensor(gates[:, q, :], cnt_sb[:, :], float(CAPACITY), pr[:, q, :],
                                                         ALU.is_lt, ALU.mult).then_inc(s["gates"], 1)
                        if has(1):
                            if (g, rnd) == (1, 0):
                                hold(dve, s["xm"], of(mo, "xm", b + 1, E + 1))
                                marked["a"] = own.mark(dve.bn_stats(stats[:, q, :], xb_of(b + 1)))
                            if (g, rnd) == (1, 1):
                                need_alone(marked["a"])
                                marked["a"] = own.mark(dve.bn_aggr(mv[:, q, :], stats[:, q, :]))
                            if (g, rnd) == (1, 2):
                                need(marked["a"])
                                dve.tensor_scalar(ve[:, q, :], mv[:, q, 1:2], LN_EPS, None, ALU.add).then_inc(s["var"], 1)
                            if (g, rnd) == (2, 0):
                                scaled(at, b + 1, q).then_inc(s["xn"], 1)

                    marked = {}
                    for g in range(NG):
                        search(b if has(0) else None, g, between)
                        if g == 2 and has(-1):
                            normalize(at, b - 1, q, W2_BANK)
                        if g == 3 and has(-1):
                            add(at, b - 1, q, W2_BANK)

                own.mark(dve.memset(lrow[:, :, E:E + 6], PAD))
                own.mark(dve.memset(pick8[:, :, TOPK_E:8], PAD))
                n = own.mark(dve.memset(seen[:, :], 0.0))
                need(n)
                batches(dve, step, LEAD, 1, own, marks)

            def bitffn(ph, before, marks):
                def quantize(src, p, which, width, tmp, dst):
                    n = own.mark(dve.tensor_reduce(amax[:, p, which:which + 1], src, AX, ALU.max, apply_absolute_value=True))
                    need(n)
                    n = own.mark(dve.tensor_scalar(aclip[:, p, which:which + 1], amax[:, p, which:which + 1], QMIN,
                                                   1.0 / 127.0, ALU.max, ALU.mult))
                    need(n)
                    n = own.mark(dve.reciprocal(qscale[:, p, which:which + 1], aclip[:, p, which:which + 1]))
                    need(n)
                    n = own.mark(dve.tensor_scalar(tmp, src, qscale[:, p, which:which + 1], ROUND, ALU.mult, ALU.add))
                    if which == 0:
                        for m in range(2):
                            own.mark(dve.tensor_scalar(deq[:, p, m:m + 1], aclip[:, p, 0:1], wstat[:, 1, m:m + 1],
                                                       None, ALU.mult))
                    else:
                        own.mark(dve.tensor_scalar(deq[:, p, 2:3], aclip[:, p, 1:2], wstat[:, 1, 2:3],
                                                   None, ALU.mult))
                    need(n)
                    return dve.tensor_scalar(dst, tmp, ROUND, None, ALU.subtract)

                def front(b, p):
                    n = own.mark(layernorm(ph, b, p, (s["x"], of(before, "x", b))))
                    need(n)
                    quantize(xn[:, p, :], p, 0, D, xr[:, p, :], xq[:, p, :]).then_inc(s["xn"], 1)

                def inner(b, p):
                    dve.wait_ge(s["gate"], of(ph, "gate", b))
                    n = own.mark(dve.scalar_tensor_tensor(h0[:, p, :], S_BANK[2 * p + 1][:, :], deq[:, p, 1:2],
                                                          gate[:, p, :], ALU.mult, ALU.mult))
                    need(n)
                    quantize(h0[:, p, :], p, 1, F, gate[:, p, :], hq[:, p, :]).then_inc(s["h"], 1)

                def add(b, p):
                    dve.wait_ge(s["dn_ps"], of(ph, "dn_ps", b))
                    dve.scalar_tensor_tensor(xb_of(b), O_BANK[:, 0:D], deq[:, p, 2:3], xb_of(b), ALU.mult,
                                             ALU.add).then_inc(s["x"], 1)

                with dve.Fori(0, B // U) as it:
                    own.turn(it, marks)
                    front(it * U, 0)
                    for u in range(U):
                        b, p = it * U + u, u % 2
                        inner(b, p)
                        if u >= 1:
                            add(b - 1, 1 - p)
                        if u + 1 < U:
                            front(b + 1, 1 - p)
                    add(it * U + (U - 1), (U - 1) % 2)
                own.done(B // U)

            def moe(ph, before, marks):
                third = ph == "moe3"

                def front_x(b, p):
                    layernorm(ph, b, p, (s["x"], of(before, "x", b))).then_inc(s["xn"], 1)

                def front_m(b, p):
                    dve.wait_ge(s["lg_ps"], of(ph, "lg_ps", b))
                    n = own.mark(dve.tensor_copy(lrow[:, p, 0:E], O_BANK[:, 0:E]))
                    need_alone(n)
                    n = own.mark(dve.max(top8[:, p, :], lrow[:, p, :]))
                    need(n)
                    n1 = own.mark(dve.tensor_copy(pick8[:, p, 0:TOPK_E], top8[:, p, 0:TOPK_E]))
                    own.mark(dve.tensor_scalar(nlm[:, p, :], top8[:, p, 0:1], -1.0, None, ALU.mult))
                    need_alone(n1)
                    n = own.mark(dve.match_replace(lmark[:, p, :], pick8[:, p, :], lrow[:, p, :], TAKEN))
                    need(n)
                    n = own.mark(dve.tensor_scalar(maskf[:, p, :], lmark[:, p, 0:E], TAKEN, None, ALU.is_equal))
                    need(n)
                    if not third:
                        own.mark(dve.tensor_copy(seen_b[:, p, :], seen[:, :]))
                        own.mark(dve.tensor_copy(mask_b[:, p, :], maskf[:, p, :]))
                        n = own.mark(dve.tensor_tensor(seen[:, :], seen[:, :], maskf[:, p, :], ALU.add))
                    need(own.n)
                    dve.sem_inc(s["lmax"], 1)

                def front_g(b, p):
                    dve.wait_ge(s["lexp"], of(ph, "lexp", b))
                    n = own.mark(dve.reciprocal(rsum[:, p, :], esum[:, p, :]))
                    need(n)
                    n = own.mark(dve.scalar_tensor_tensor(pr[:, p, :], el[:, p, :], rsum[:, p, :], maskf[:, p, :],
                                                          ALU.mult, ALU.mult))
                    if third:
                        need(n)
                        n = own.mark(dve.tensor_reduce(gsum[:, p, 0:1], pr[:, p, :], AX, ALU.add))
                        need(n)
                        n = own.mark(dve.tensor_scalar(gsum[:, p, 1:2], gsum[:, p, 0:1], NORM_EPS, None, ALU.add))
                        need(n)
                        n = own.mark(dve.reciprocal(gsum[:, p, 2:3], gsum[:, p, 1:2]))
                        need(n)
                        n = own.mark(dve.tensor_scalar(gates[:, p, :], pr[:, p, :], gsum[:, p, 2:3], None, ALU.mult))
                    else:
                        hold(dve, s["cnt_ps"], of(ph, "cnt_ps", b))
                        need(n)
                        n = own.mark(dve.scalar_tensor_tensor(gates[:, p, :], O_BANK[:, 64:64 + E], float(CAPACITY),
                                                              pr[:, p, :], ALU.is_lt, ALU.mult))
                    need(n)
                    dve.sem_inc(s["gates"], 1)

                def front_b(b, p):
                    if third:
                        dve.wait_ge(s["b2_ps"], of(ph, "b2_ps", b))
                        return own.mark(dve.tensor_tensor(xb_of(b), xb_of(b), O_BANK[:, 0:D], ALU.add))
                    return own.mark(dve.tensor_tensor(xb_of(b), xb_of(b), bias_row[:, :], ALU.add))

                n = own.mark(dve.memset(lrow[:, :, E:E + 6], PAD))
                n = own.mark(dve.memset(pick8[:, :, TOPK_E:8], PAD))
                n = own.mark(dve.memset(seen[:, :], 0.0))
                need(n)
                with dve.Fori(0, B // U) as it:
                    own.turn(it, marks)
                    front_x(it * U, 0)
                    front_m(it * U, 0)
                    front_g(it * U, 0)
                    n = front_b(it * U, 0)
                    for i in range(E * U):
                        u, e = i // E, i % E
                        b, p = it * U + u, u % 2
                        dve.wait_ge(s["y_ps"], of(ph, "y_ps", b, e + 1))
                        if e == 0:
                            need_alone(n)
                        else:
                            hold(dve, s["acc"], of(ph, "acc", b, e))
                        dve.scalar_tensor_tensor(xb_of(b), Y_BANK[e % 2][:, 0:D], gates[:, p, e:e + 1], xb_of(b),
                                                 ALU.mult, ALU.add).then_inc(s["acc"], 1)
                        if e == E - 1:
                            dve.wait_ge(s["acc"], of(ph, "acc", b, E))
                            dve.sem_inc(s["x"], 1)
                        if u + 1 < U:
                            if e == 0:
                                front_x(b + 1, 1 - p)
                            if e == 3:
                                front_m(b + 1, 1 - p)
                            if e == 5:
                                front_g(b + 1, 1 - p)
                            if e == 7:
                                n = front_b(b + 1, 1 - p)
                own.done(B // U)

            def choose_tokens(ph, before, marks):
                with dve.Fori(0, B // 2) as it:
                    own.turn(it, marks)
                    for p in range(2):
                        b = it * 2 + p
                        hold(dve, s["xnT_ps"], of(ph, "xnT_ps", b, -1))
                        layernorm(ph, b, p, (s["x"], of(before, "x", b))).then_inc(s["xn"], 1)
                own.done(B // 2)
                dve.wait_ge(s["lg_ps"], of(ph, "lg_ps", B - 1))
                n = own.mark(dve.tensor_tensor(lg_all[:, :, :], bank[0][:, 0:B * E].rearrange("p (b e) -> p b e", e=E),
                                               br_row[:, :].unsqueeze(1).to_broadcast([P, B, E]), ALU.add))
                need(n)
                n = own.mark(dve.tensor_reduce(lmax_all[:, :], lg_all[:, :, :], AX, ALU.max))
                need(n)
                dve.tensor_tensor(lg_all[:, :, :], lg_all[:, :, :], lmax_all[:, :].unsqueeze(2).to_broadcast([P, B, E]),
                                  ALU.subtract).then_inc(lg_all_ready, 1)
                dve.wait_ge(lexp_all, 1)
                n = own.mark(dve.tensor_reduce(lsum_all[:, :], prob[:, :, :], AX, ALU.add))
                need(n)
                n = own.mark(dve.reciprocal(rsum_all[:, :], lsum_all[:, :]))
                need(n)
                dve.tensor_tensor(prob[:, :, :], prob[:, :, :], rsum_all[:, :].unsqueeze(2).to_broadcast([P, B, E]),
                                  ALU.mult).then_inc(prob_ready, 1)
                dve.wait_ge(probT_ready, 1)
                for rnd in range(EC_K // 8):
                    src = probT if rnd == 0 else takenT
                    n = own.mark(dve.max(ec8[:, rnd % 2, :], src))
                    need(n)
                    n = own.mark(dve.match_replace(takenT, ec8[:, rnd % 2, :], src, TAKEN))
                    need(n)
                n = own.mark(dve.tensor_scalar(takenT, takenT, TAKEN, None, ALU.is_equal))
                need(n)
                dve.sem_inc(taken_ready, 1)
                dve.wait_ge(taken_ready, 1)
                dve.tensor_tensor(probT, probT, takenT, ALU.mult).then_inc(gT_all_ready, 1)
                dve.wait_ge(taken_ps, 1)
                dve.tensor_tensor(gates_all[:, :, :], prob[:, :, :], bank[3][:, 0:B * E].rearrange("p (b e) -> p b e", e=E),
                                  ALU.mult).then_inc(ec_gates, 1)

            def expert_choice(ph):
                dve.wait_ge(ec_gates, 1)
                with dve.Fori(0, B // U) as it:
                    own.turn(it, U * (1 + NEG))
                    for i in range(NEG * U):
                        u, g = i // NEG, i % NEG
                        b, p = it * U + u, u % 2
                        if g == 0:
                            dve.wait_ge(s["b2_ps"], of(ph, "b2_ps", b))
                            n = own.mark(dve.tensor_tensor(xb_of(b), xb_of(b), O_BANK[:, 0:D], ALU.add))
                        dve.wait_ge(s["y_ps"], of(ph, "y_ps", b, g + 1))
                        for e in range(EGRP):
                            if e == 0 and g > 0:
                                hold(dve, s["acc"], of(ph, "acc", b, g))
                            else:
                                need_alone(n)
                            gcol = gates_all[:, bass.ds(b, 1), EGRP * g + e:EGRP * g + e + 1].rearrange("p b e -> p (b e)")
                            ins = dve.scalar_tensor_tensor(xb_of(b), Y_BANK[g % 2][:, D * e:D * (e + 1)], gcol, xb_of(b),
                                                           ALU.mult, ALU.add)
                            if e == 0:
                                n = own.mark(ins)
                            else:
                                ins.then_inc(s["acc"], 1)
                        if g == NEG - 1:
                            dve.wait_ge(s["acc"], of(ph, "acc", b, NEG))
                            dve.sem_inc(s["x"], 1)
                own.done(B // U)

            dve.wait_ge(ld_x, 16)
            attention("attn0", None, MARKS["attn0"])
            dve.wait_ge(ld_small, SMALL)
            n = own.mark(dve.reciprocal(itemp_rep[:, :], temp_rep[:, :]))
            need(n)
            n = own.mark(dve.tensor_tensor(bq_rep[:, 2, :], bq_rep[:, 2, :], itemp_rep[:, :], ALU.mult))
            values(1)
            bitffn("bit0", "attn0", MARKS["bit0"])
            attention("attn1", "bit0", MARKS["attn1"])
            values(2)
            experts_and_attention("moe1", "attn2", "attn1", MARKS["attn2"])
            values(3)
            choose_tokens("ecr2", "attn2", 2 * NORM)
            expert_choice("ec2")
            attention("attn3", "ec2", MARKS["attn3"])
            moe("moe3", "attn3", MARKS["moe3"])


NORM, SPLIT, SHIFT, ROWS = 2, 1, NG, 1
MARKS = {
    "attn0": 2 * (NORM + SHIFT + ROWS),
    "attn1": 2 * (NORM + SHIFT + ROWS + 1),
    "attn3": 2 * (NORM + SHIFT + ROWS + 1),
    "attn2": 2 * (2 * NORM + 9 + ROWS + 1 + NG * ROUNDS * GH * 2),
    "bit0": U * (NORM + 1 + 4 + 2 + 1 + 4 + 1),
    "moe3": U * (NORM + 6 + 6 + 1),
}

_OUT_SHAPE = (B, P, D)


def kernel(**inputs):
    import numpy as _np
    import concourse.bacc as _bacc
    from concourse import mybir as _mybir
    from concourse.bass_utils import run_bass_kernel_spmd as _run

    nc = _bacc.Bacc("TRN2", target_bir_lowering=False, num_devices=1)
    arrays, aps = {}, {}
    for name, value in inputs.items():
        arr = _np.ascontiguousarray(value)
        arrays["in_" + name] = arr
        aps[name] = nc.dram_tensor("in_" + name, arr.shape, _mybir.dt.from_np(arr.dtype), kind="ExternalInput").ap()
    out = nc.dram_tensor("out_0", _OUT_SHAPE, _mybir.dt.float32, kind="ExternalOutput").ap()
    build(nc, aps, out)
    r = _run(nc, [arrays], core_ids=[0])
    return r.results[0]["out_0"]
```

```python
from contextlib import ExitStack

import concourse.bass as bass
from concourse import mybir

B = 8
P = 128
D = 128
NH = 16
DK = D // NH
NG = 4
GH = NH // NG
GW = GH * DK
NPART = P // GW
VW = DK + 1
F = 512
NC = F // P
E = 8
TOPK_E = 2
T = B * P
CAPACITY = TOPK_E * T // E
EC_K = T // E
EGRP = 2
NEG = E // EGRP
F2 = int(D * 4 * (2.0 / 3.0))
NC2 = -(-F2 // P)
FC2 = -(-F2 // NC2)
FROWS2 = [min(FC2, F2 - c * FC2) for c in range(NC2)]
TOP_ATTN = 32
ROUNDS = TOP_ATTN // 8
U = 4
LAG = 2
LEAD = 3
HALF = T // 2
HB = B // 2
LN_EPS = 1e-5
QMIN = 1e-5
NORM_EPS = 1e-9
ROUND = 12582912.0
TAKEN = -3.0e38
PAD = -2.0e38
C = DK ** -0.5

F32 = mybir.dt.float32
F32R = mybir.dt.float32r
BF16 = mybir.dt.bfloat16
ALU = mybir.AluOpType
ACT = mybir.ActivationFunctionType
AX = mybir.AxisListType.X

ATTN = dict(var=1, rstd=1, xn=1, xnT_ps=1, xnT=1, q_ps=1, qb=1, q_up=1, qst=1, vc=1, s_ps=NG, sx=NG, p=NG, pt_ps=NG,
            pt=NG, pv=NG, oT=1, oq_ps=1, on=1, onT_ps=1, onT=1, o_ps=1, x=1)
ATTN0 = {k: n for k, n in ATTN.items() if k not in ("onT_ps", "onT", "o_ps")}
TOPK = {**{k: n for k, n in ATTN.items() if k not in ("sx", "p")}, "ss": NG, "topk": NG, "sd": 2 * NG, "ex": 2 * NG, "psel": NG}
BIT = dict(h0=1, var=1, rstd=1, xn=1, xnT_ps=1, xnT=1, gu_ps=1, gate=1, h=1, hqT_ps=1, hqT=1, dn_ps=1, x=1)
MOE = dict(var=1, rstd=1, xn=1, xnT_ps=1, xnT=1, lg_ps=1, lmax=1, lexp=1, gates=1, h_ps=E, hT=E, y_ps=E, acc=E, x=1)
MOE1 = dict(m_var=1, m_rstd=1, m_xn=1, m_xnT_ps=1, m_xnT=1, lg_ps=1, lg=1, lmax=1, lexp=1, cnt_ps=1, cnt=1, gates=1,
            h_ps=E, hT=E, y_ps=E, ym=E, xm=E + 1)
MOE3 = dict({k: n for k, n in MOE.items() if k != "hT"}, bias=1, hT3=E, gT_ps=1, gT=1, b2_ps=1)
ECR = dict(xn=1)
EC = dict(h_ps=NEG, hT=NEG, y_ps=NEG, acc=NEG, gT=1, b2_ps=1, x=1)
PHASES = [("attn0", ATTN0), ("bit0", BIT), ("attn1", ATTN), ("moe1", MOE1), ("attn2", TOPK),
          ("ecr2", ECR), ("ec2", EC), ("attn3", ATTN), ("moe3", MOE3)]
FREE = dict(hT3=4, oT=1, oq_ps=1, qb=1, sx=2, ss=1, pt_ps=4, pt=2, pv=2, on=1, psel=2, qst=1, hT=2, y_ps=2, acc=2, ym=1, xm=2)
LAYER = {"attn1": 0, "attn2": 1, "attn3": 2}


class Counts:

    def __init__(self):
        self.before, self.each, total = {}, {}, {}
        for _, each in PHASES:
            for what in each:
                total.setdefault(what, FREE.get(what, 0))
        for name, each in PHASES:
            self.before[name] = dict(total)
            self.each[name] = each
            for what, n in each.items():
                total[what] += n * B
        self.names = list(total)

    def of(self, phase, what, b, n=1):
        return b * self.each[phase][what] + (self.before[phase][what] + n)


class Chain:

    def __init__(self, eng, sem):
        self.eng, self.sem, self.n, self.it, self.per = eng, sem, 0, None, 0

    def mark(self, ins):
        ins.then_inc(self.sem, 1)
        self.n += 1
        return self.n

    def value(self, n):
        return n if self.it is None else self.it * self.per + n

    def turn(self, it, per):
        self.it, self.per, self.at0 = it, per, self.n

    def done(self, turns):
        assert self.n - self.at0 == self.per, f"{self.n - self.at0} marked in a turn, not {self.per}"
        self.n, self.it = self.at0 + self.per * turns, None


def build(nc, a, out):
    with ExitStack() as ctx:
        def sb(name, shape, dt=F32):
            return ctx.enter_context(nc.sbuf_tensor("sb_" + name, shape, dt))

        def sem(name):
            return ctx.enter_context(nc.semaphore(name))

        bank = [ctx.enter_context(nc.psum_tensor(f"bank{i}", [P, 512], F32)) for i in range(8)]
        S_BANK = bank[0:4]
        W_BANK, R_BANK = bank[2], bank[3]
        PT_BANK = bank[4:6]
        A_BANK, O_BANK = bank[6], bank[7]
        Y_BANK = bank[4:6]
        W2_BANK, H2_BANK = bank[1], bank[2:4]

        def halfword(bk):
            return bk[:, 0:256].bitcast(BF16)

        x_res = sb("x_res", [P, B, D])
        ctx_tok = sb("ctx_tok", [P, B, D])
        xnT_all = ctx_tok
        ctxT = sb("ctxT", [P, T])
        k_st = sb("k_st", [P, GH, NG, B, P], F32R)
        k_raw = sb("k_raw", [P, 2, NG, P])
        k_part = sb("k_part", [P, NG, T], F32R)
        v_aug = sb("v_aug", [P, B, NH, VW])
        id_rep = sb("id_rep", [P, NG, NPART, GW])
        wq_rep = sb("wq_rep", [P, 3, NG, NPART, GW])
        wk_rep = sb("wk_rep", [P, 3, NG, NPART, GW])
        wv_T = sb("wv_T", [P, 3, D])
        wo_T = sb("wo_T", [P, 3, D])
        bq_rep = sb("bq_rep", [P, 3, NG])
        bk_rep = sb("bk_rep", [P, 3, NG])
        bv_row = sb("bv_row", [P, 3, D])
        bo_row = sb("bo_row", [P, 3, D])
        temp_row = sb("temp_row", [P, NH])
        itemp_row = sb("itemp_row", [P, NH])
        temp_rep = sb("temp_rep", [P, NG])
        itemp_rep = sb("itemp_rep", [P, NG])
        ident = sb("ident", [P, P])
        head_mask = sb("head_mask", [P, GH])
        ident_b = sb("ident_b", [P, P], BF16)
        ones = sb("ones", [P, P])
        ones_b = sb("ones_b", [P, P], BF16)
        before_b = sb("before_b", [P, P], BF16)
        stats = sb("stats", [P, 2, 6])
        mv = sb("mv", [P, 2, 2])
        ve = sb("ve", [P, 2, 1])
        rstd = sb("rstd", [P, 2, 1])
        minus_half = sb("minus_half", [P, 1])
        one = sb("one", [P, 1])
        xn = sb("xn", [P, 2, D])
        xnT = sb("xnT", [P, 2, D])
        qb = sb("qb", [P, 512])
        m_stats = sb("m_stats", [P, 6])
        m_mv = sb("m_mv", [P, 2])
        m_ve = sb("m_ve", [P, 1])
        m_rstd = sb("m_rstd", [P, 1])
        cnt_sb = sb("cnt_sb", [P, E])
        v_cur = sb("v_cur", [P, 2, NH, GW])
        oT_sb = sb("oT_sb", [P, NG, P])
        q_st = sb("q_st", [P, 2, 512], F32R)
        mx = sb("mx", [P, NG, GH])
        p_sb = sb("p_sb", [P, NG, GH, P])
        pt_sb = sb("pt_sb", [P, 2, GH, P])
        rden = sb("rden", [P, 2, NH])
        on = sb("on", [P, 2, D])
        onT = sb("onT", [P, 2, D])
        t_row = sb("t_row", [P, 2, D])
        xn8 = p_sb[:, :, :, :].rearrange("p g j k -> p (g j) k")
        v8 = sb("v8", [P, 2, GH, ROUNDS, 8])
        shared = sb("shared", [P, 4, 512])
        gate, h0 = shared[:, 0:2, :], shared[:, 2:4, :]
        ss = shared[:, 0:2, :].rearrange("p r (j k) -> p r j k", k=P)
        sel = shared[:, 2:4, :].rearrange("p r (j k) -> p r j k", k=P)
        probT = shared[0:E, 0:2, :].rearrange("p r k -> p (r k)")
        takenT = shared[0:E, 2:4, :].rearrange("p r k -> p (r k)")
        wstat = sb("wstat", [P, 3, 3])
        amax = sb("amax", [P, 2, 2])
        aclip = sb("aclip", [P, 2, 2])
        qscale = sb("qscale", [P, 2, 2])
        deq = sb("deq", [P, 2, 3])
        xr = sb("xr", [P, 2, D])
        xq = sb("xq", [P, 2, D], BF16)
        xqT = sb("xqT", [P, 2, D], BF16)
        idle = pt_sb[:, :, :, :].rearrange("p a j k -> p (a j k)").bitcast(BF16)
        hq = idle[:, 0:2 * F].rearrange("p (a f) -> p a f", a=2)
        hqT = idle[:, 2 * F:4 * F].rearrange("p (a f) -> p a f", a=2)
        m_xn, m_xnT = ones, xr
        ys = id_rep[:, 0:2, :, :].rearrange("p g a f -> p g (a f)")
        w1 = sb("w1", [P, E, F])
        w2 = sb("w2", [P, E, NC, D])
        hT = sb("hT", [P, 2, NC, P])
        hT3 = k_part[:, :, 0:F].bitcast(F32).rearrange("p a (c k) -> p a c k", c=NC)
        wbT = hT[:, :, :, :].rearrange("p a c k -> p (a c k)").bitcast(BF16)[:, 0:3 * 512]\
            .rearrange("p (m n) -> p m n", m=3)
        wb_q = w1[:, 0:2, :].rearrange("p e f -> p (e f)").bitcast(BF16)[:, 0:3 * 512]\
            .rearrange("p (m n) -> p m n", m=3)
        early = w2[:, :, :, :].rearrange("p e c d -> p (e c d)")
        w_raw = early[:, 0:12 * D].rearrange("p (m i) -> p m i", m=12)
        wb_raw = early[:, 12 * D:12 * D + 3 * 512].rearrange("p (m i) -> p m i", m=3)
        wr = sb("wr", [P, 3, E])
        b1_col = sb("b1_col", [P, E, NC])
        b2_sb = sb("b2_sb", [E, 2, D])
        br_row = sb("br_row", [P, E])
        bias_row = sb("bias_row", [P, D])
        lrow = sb("lrow", [P, 2, E + 6])
        top8 = sb("top8", [P, 2, 8])
        pick8 = sb("pick8", [P, 2, 8])
        lmark = sb("lmark", [P, 2, E + 6])
        nlm = sb("nlm", [P, 2, 1])
        el = sb("el", [P, 2, E])
        esum = sb("esum", [P, 2, 1])
        rsum = sb("rsum", [P, 2, 1])
        pr = sb("pr", [P, 2, E])
        maskf = sb("maskf", [P, 2, E])
        mask_b = sb("mask_b", [P, 2, E], BF16)
        seen = sb("seen", [P, E])
        seen_b = sb("seen_b", [P, 2, E], BF16)
        fits = sb("fits", [P, 2, E])
        gates = sb("gates", [P, 2, E])
        gsum = sb("gsum", [P, 2, 3])
        gT = sb("gT", [E, 2, P])
        wu2 = early[:, 0:NEG * F2].rearrange("p (g f) -> p g f", g=NEG)
        wd2 = w1[0:FC2, :, :].rearrange("p e f -> p (e f)")[:, 0:NC2 * E * D]\
            .rearrange("p (c e d) -> p c e d", c=NC2, e=E)
        h_stage = (p_sb[:, :, :, :].rearrange("p g j k -> p (g j) k")[:, 0:NEG * NC2, :],
                   early[:, 2048:2048 + NEG * NC2 * P].rearrange("p (i k) -> p i k", k=P))
        bu2 = sb("bu2", [P, NEG, NC2])
        lg_all = sb("lg_all", [P, B, E])
        lmax_all = sb("lmax_all", [P, B])
        lsum_all = sb("lsum_all", [P, B])
        rsum_all = sb("rsum_all", [P, B])
        prob = sb("prob", [P, B, E])
        gates_all = lg_all
        ec8 = sb("ec8", [E, 2, 8])
        ve_all = sb("ve_all", [P, B])
        rstd_all = sb("rstd_all", [P, B])
        mv_all = sb("mv_all", [P, B, 2])
        stats_all = qb[:, 0:B * 6].rearrange("p (b k) -> p b k", b=B)

        counts = Counts()
        s = {name: sem("s_" + name) for name in counts.names}
        of = counts.of
        ld_x, ld_ctx, ld_w, ld_bit = sem("ld_x"), sem("ld_ctx"), sem("ld_w"), sem("ld_bit")
        ld_small, ld_moe1, ld_moe3, ld_ec = sem("ld_small"), sem("ld_moe1"), sem("ld_moe3"), sem("ld_ec")
        const_ready = sem("const_ready")
        v_ones = sem("v_ones")
        tr_ps = sem("tr_ps")
        ctxT_ready = sem("ctxT_ready")
        w_ready = sem("w_ready")
        v0_ready = sem("v0_ready")
        wsum_ready = sem("wsum_ready")
        wtot_ps = sem("wtot_ps")
        wb_ready = sem("wb_ready")
        wbT_ps = sem("wbT_ps")
        wbT_ready = sem("wbT_ready")
        k0_upper, k0_lower, k0_split = sem("k0_upper"), sem("k0_lower"), sem("k0_split")
        k0_masked = sem("k0_masked")
        k0_scaled = sem("k0_scaled")
        k_masked = sem("k_masked")
        h_moved = sem("h_moved0"), sem("h_moved1")
        k_ps = sem("k_ps")
        k_evac = sem("k_evac")
        k_upper = sem("k_upper")
        k_lower = sem("k_lower")
        k_split = sem("k_split")
        k_placed = sem("k_placed")
        v_ps = sem("v_ps")
        v_ready = sem("v_ready")
        lg_all_ready = sem("lg_all_ready")
        lexp_all = sem("lexp_all")
        prob_ready = sem("prob_ready")
        var_all = sem("var_all")
        rstd_all_ready = sem("rstd_all_ready")
        xn8T_ps, xn8T_ready = sem("xn8T_ps"), sem("xn8T_ready")
        lg_all_ps = sem("lg_all_ps")
        probT_ps = sem("probT_ps")
        probT_ready = sem("probT_ready")
        taken_ready = sem("taken_ready")
        taken_ps = sem("taken_ps")
        gT_all_ready = sem("gT_all_ready")
        ec_gates = sem("ec_gates")
        dve_own, act_own, pool_own = sem("dve_own"), sem("act_own"), sem("pool_own")
        held = sem("held")
        stored = sem("stored")

        def wbT_place(m):
            return halfword(W_BANK) if m == 2 else R_BANK[:, 256 * m:256 * (m + 1)].bitcast(BF16)

        def bit_input(p):
            return PT_BANK[1 - p][:, 256:256 + P // 2].bitcast(BF16)

        def hold(eng, what, value):
            eng.wait_ge(what, value)
            if not isinstance(value, int):
                eng.sem_inc(held, 1)

        def batches(eng, step, lead, lag, own=None, marks=0, first=0):
            middle = (B - lead - lag) // 2
            for b in range(first, lag):
                step(b, b % 2, lambda k: 0 <= b + k < B)
            with eng.Fori(0, middle) as it:
                if own:
                    own.turn(it, marks)
                for u in range(2):
                    step(it * 2 + (lag + u), (lag + u) % 2, lambda k: True)
            if own:
                own.done(middle)
            for b in range(lag + 2 * middle, B + lag):
                step(b, b % 2, lambda k: 0 <= b + k < B)

        def xb_of(b):
            return x_res[:, bass.ds(b, 1), :].rearrange("p b d -> p (b d)")

        def slot(b, g, back):
            k = g - back
            return (b + k // NG if k // NG else b), k % NG, k // NG

        def h_of(b, c):
            return k_st[:, c, :, b, :].bitcast(F32)

        KEY_PHASES = ["attn0", "attn1", "attn2", "attn3"]
        PLACES = NPART * GH
        block = ctx.enter_context(nc.Block())
        n_small = [0]

        @block.sync
        def _(sp):
            sp.dma_start(ctx_tok[:, :, :], a["ctx_1024"].rearrange("b p d -> p b d")).then_inc(ld_ctx, 16)
            sp.dma_start(x_res[:, :, :], a["x"].rearrange("b p d -> p b d")).then_inc(ld_x, 16)
            for i, name in enumerate(("L0_ffn_w_gate", "L0_ffn_w_up")):
                sp.dma_start(wb_raw[:, i, :].rearrange("p (c i) -> p c i", c=NC),
                             a[name].rearrange("(c p) i -> p c i", p=P)).then_inc(ld_bit, 16)
            sp.dma_start(wb_raw[:, 2, :], a["L0_ffn_w_down"]).then_inc(ld_bit, 16)
            mats = ["L1_xattn_wq_w", "L1_xattn_wk_w", "L1_xattn_wv_w", "L1_xattn_proj_w",
                    "L2_xattn_Wq", "L2_xattn_Wk", "L2_xattn_Wv", "L2_xattn_Wo",
                    "L3_xattn_Wq", "L3_xattn_Wk", "L3_xattn_Wv", "L3_xattn_Wo"]
            for i, name in enumerate(mats):
                sp.dma_start(w_raw[:, i, :], a[name]).then_inc(ld_w, 16)
            temp = a["L3_xattn_temperature"].rearrange("h a b -> (h a b)")
            sp.dma_start(temp_row[:, :], temp.partition_broadcast(P)).then_inc(ld_w, 16)

            def small(dst, src):
                sp.dma_start(dst, src, allow_slow_non_contiguous=True).then_inc(ld_small, 16)
                n_small[0] += 1

            names = [("L1_xattn_wq_b", "L1_xattn_wk_b", "L1_xattn_wv_b", "L1_xattn_proj_b"),
                     ("L2_xattn_bq", "L2_xattn_bk", "L2_xattn_bv", "L2_xattn_bo"),
                     ("L3_xattn_bq", "L3_xattn_bk", "L3_xattn_bv", "L3_xattn_bo")]
            for i, (q, k, v, o) in enumerate(names):
                for part in range(NPART):
                    rows = slice(GW * part, GW * (part + 1))
                    small(bq_rep[rows, i, :], a[q].rearrange("(g h) -> h g", h=GW))
                    small(bk_rep[rows, i, :], a[k].rearrange("(g h) -> h g", h=GW))
                small(bv_row[:, i, :], a[v].partition_broadcast(P))
                small(bo_row[:, i, :], a[o].partition_broadcast(P))
            for part in range(NPART):
                for j in range(GH):
                    lo = GW * part + DK * j
                    small(temp_rep[lo:lo + DK, :], temp.rearrange("(g j) -> j g", j=GH)[j].partition_broadcast(DK))
            small(wr[:, 0, :], a["L1_ffn_w_router"])
            small(wr[:, 1, :], a["L2_ffn_Wr"])
            small(wr[:, 2, :], a["L3_ffn_Wg"])
            small(bias_row[:, :], a["L1_ffn_bias"].rearrange("a b d -> (a b d)").partition_broadcast(P))
            small(br_row[:, :], a["L2_ffn_br"].partition_broadcast(P))
            small(b2_sb[:, 0, :], a["L2_ffn_b_down"])
            small(b2_sb[:, 1, :], a["L3_ffn_b2"])
            for e in range(E):
                small(b1_col[:, e, :], a["L3_ffn_b1"][e].rearrange("(c p) -> p c", p=P))
            for g in range(NEG):
                for c, n in enumerate(FROWS2):
                    small(bu2[0:n, g, c:c + 1],
                          a["L2_ffn_b_up"][g, c * FC2:c * FC2 + n].rearrange("(f o) -> f o", o=1))

            def place_keys(i):
                for half in range(2):
                    sp.wait_ge(k_split, B * (i - 1) + HB * (half + 1))
                    sp.wait_ge(s["s_ps"], of(KEY_PHASES[i - 1], "s_ps", B - 1, NG))
                    for part in range(NPART):
                        for j in range(GH):
                            lo = GW * part + DK * j
                            sp.dma_start(
                                k_st[lo:lo + DK, j, :, HB * half:HB * (half + 1), :]
                                .rearrange("p g b k -> p g (b k)").bitcast(F32),
                                k_part[lo:lo + DK, :, HALF * half:HALF * (half + 1)].bitcast(F32)).then_inc(k_placed, 16)

            sp.wait_ge(ctxT_ready, 2)
            sp.wait_ge(w_ready, 4)
            sp.wait_ge(wb_ready, 1)
            for e in range(E):
                if e == 0:
                    sp.wait_ge(wbT_ps, 1)
                sp.dma_start(w1[:, e, :], a["L1_ffn_w1"][e]).then_inc(ld_moe1, 16)
                sp.dma_start(w2[:, e, :, :], a["L1_ffn_w2"][e].rearrange("(c p) d -> p c d", p=P)).then_inc(ld_moe1, 16)
            place_keys(2)
            sp.wait_ge(s["y_ps"], of("moe1", "y_ps", B - 1, E))
            sp.dma_start(wu2, a["L2_ffn_W_up"].rearrange("g d f -> d g f")).then_inc(ld_ec, 16)
            for c, n in enumerate(FROWS2):
                sp.dma_start(wd2[0:n, c, :, :],
                             a["L2_ffn_W_down"][:, c * FC2:c * FC2 + n, :].rearrange("e f d -> f e d")).then_inc(ld_ec, 16)
            for b in range(B):
                sp.wait_ge(s["hT"], of("ec2", "hT", b, NEG))
                for c, n in enumerate(FROWS2):
                    sp.dma_start(h_of(b, c)[0:n], h_stage[b % 2][0:n, NEG * c:NEG * (c + 1), :]).then_inc(h_moved[b % 2], 16)
            sp.wait_ge(s["y_ps"], of("ec2", "y_ps", B - 1, NEG))
            for e in range(E):
                sp.dma_start(w1[:, e, :], a["L3_ffn_W1"][e]).then_inc(ld_moe3, 16)
                sp.dma_start(w2[:, e, :, :], a["L3_ffn_W2"][e].rearrange("(c p) d -> p c d", p=P)).then_inc(ld_moe3, 16)
            for b in range(B):
                sp.wait_ge(s["x"], of("moe3", "x", b))
                sp.dma_start(out[b], x_res[:, b, :]).then_inc(stored, 16)
            sp.wait_ge(stored, 16 * B)

        SMALL = 16 * n_small[0]

        @block.gpsimd
        def _(pool):
            own = Chain(pool, pool_own)

            def step(ins):
                pool.wait_ge(pool_own, own.mark(ins))

            step(pool.memset(ident[:, :], 0.0))
            step(pool.affine_select(out=ident[:, :], in_=ident[:, :], compare_op=ALU.not_equal, fill=1.0,
                                    base=0, pattern=[[-1, P]], channel_multiplier=1))
            pool.tensor_copy(ident_b[:, :], ident[:, :]).then_inc(const_ready, 1)
            for part in range(NPART):
                step(pool.tensor_copy(id_rep[:, :, part, :], ident[:, :].rearrange("p (g f) -> p g f", g=NG)))
            pool.memset(ones[:, :], 1.0).then_inc(const_ready, 1)
            pool.memset(ones_b[:, :], 1.0).then_inc(const_ready, 1)
            step(pool.memset(before_b[:, :], 1.0))
            pool.affine_select(out=before_b[:, :], in_=before_b[:, :], compare_op=ALU.is_gt, fill=0.0,
                               base=0, pattern=[[1, P]], channel_multiplier=-1).then_inc(const_ready, 1)
            pool.memset(minus_half[:, :], -0.5)
            pool.memset(one[:, :], 1.0)
            pool.memset(v_cur[:, :, :, :], 0.0)
            pool.memset(v_aug[:, :, :, DK:VW], 1.0).then_inc(v_ones, 1)

            def split_keys(i, b, p):
                part = k_part[:, :, bass.ds(b * P, P)]
                hold(pool, k_evac, b + (B * i + 1))
                pool.tensor_tensor(part, k_raw[:, p, :, :], one[:, :].unsqueeze(2).to_broadcast([P, NG, P]), ALU.mult)\
                    .then_inc(k_upper, 1)
                pool.wait_ge(k_upper, b + (B * (i - 1) + 1))
                rows = slice(GW, 2 * GW)
                pool.tensor_tensor(part[rows], k_raw[rows, p, :, :], part[rows], ALU.subtract).then_inc(k_lower, 1)
                pool.wait_ge(k_lower, b + (B * (i - 1) + 1))
                rows = slice(3 * GW, 4 * GW)
                pool.tensor_tensor(part[rows], k_raw[rows, p, :, :], part[rows], ALU.subtract).then_inc(k_split, 1)
                pool.wait_ge(k_split, b + (B * (i - 1) + 1))

            def scale_of(ph, b, p):
                pool.wait_ge(s["var"], of(ph, "var", b))
                pool.tensor_tensor(rstd[:, p, :], ve[:, p, :], minus_half[:, :], ALU.pow).then_inc(s["rstd"], 1)

            def bitffn(ph):
                def step(b, p, has):
                    if has(2):
                        scale_of(ph, b + 2, p)
                    if has(0) and not has(1):
                        for k in range(LAG):
                            scale_of("attn1", k, k)
                    if has(-1):
                        split_keys(1, b - 1, 1 - p)

                pool.wait_ge(k_placed, 1)
                for b in range(2):
                    scale_of(ph, b, b)
                batches(pool, step, 2, 2)

            def split(ph, b, p):
                hold(pool, s["qb"], of(ph, "qb", b))
                if not (isinstance(b, int) and b < 2):
                    hold(pool, s["s_ps"], of(ph, "s_ps", b - 1, 0))
                pool.tensor_tensor(q_st[:, p, :], qb[:, :], one[:, :].to_broadcast([P, 512]), ALU.mult)\
                    .then_inc(s["q_up"], 1)
                pool.wait_ge(s["q_up"], of(ph, "q_up", b))
                pool.tensor_tensor(q_st[P // 2:P, p, :], qb[P // 2:P, :], q_st[P // 2:P, p, :],
                                   ALU.subtract).then_inc(s["qst"], 1)
                pool.wait_ge(s["qst"], of(ph, "qst", b))

            def bring_values(ph, b, p):
                if not (isinstance(b, int) and b < 2):
                    pool.wait_ge(s["pv"], of(ph, "pv", b - 1, 0))
                pool.tensor_copy(v_cur[:, p, :, 0:VW], v_aug[:, bass.ds(b, 1), :, :].rearrange("p b h v -> p (b h) v"))\
                    .then_inc(s["vc"], 1)

            def experts_and_attention(mo, at):
                def add_expert(b, p, e):
                    hold(pool, s["ym"], of(mo, "ym", b, e + 1))
                    hold(pool, s["xm"], of(mo, "xm", b, e + 1))
                    pool.tensor_tensor(xb_of(b), xb_of(b), ys[:, e % 2, :], ALU.add).then_inc(s["xm"], 1)

                def shift(b, g):
                    pool.wait_ge(s["topk"], of(at, "topk", b, g + 1))
                    if not (isinstance(b, int) and b == 0):
                        hold(pool, s["pt_ps"], of(at, "pt_ps", b, g + 1 - 4))
                    pool.tensor_tensor(p_sb[:, g, :, :], ss[:, g % 2, :, :],
                                       v8[:, g % 2, :, 0, 0:1].to_broadcast([P, GH, P]), ALU.subtract).then_inc(s["sd"], 1)
                    pool.tensor_tensor(sel[:, g % 2, :, :], sel[:, g % 2, :, :],
                                       v8[:, g % 2, :, 0, 0:1].to_broadcast([P, GH, P]), ALU.subtract).then_inc(s["sd"], 1)

                def select(b, g):
                    pool.wait_ge(s["ex"], of(at, "ex", b, 2 * g + 2))
                    pool.tensor_tensor(p_sb[:, g, :, :], p_sb[:, g, :, :], sel[:, g % 2, :, :],
                                       ALU.subtract).then_inc(s["psel"], 1)

                def step(b, p, has):
                    for g in range(NG):
                        if g == 1 and has(3):
                            pool.wait_ge(s["m_var"], of(mo, "m_var", b + 3))
                            pool.tensor_tensor(m_rstd[:, :], m_ve[:, :], minus_half[:, :], ALU.pow).then_inc(s["m_rstd"], 1)
                        b1, g1, k1 = slot(b, g, 1)
                        if has(k1):
                            shift(b1, g1)
                        if g == 3 and has(1):
                            split(at, b + 1, 1 - p)
                            if isinstance(b, int) and b < 0:
                                pool.wait_ge(v_ready, 4)
                            bring_values(at, b + 1, 1 - p)
                        if has(k1):
                            select(b1, g1)
                        if g == 0 and has(1):
                            add_expert(b + 1, 1 - p, E - 1)
                        if g == 0 and has(2):
                            hold(pool, s["m_xn"], of(mo, "m_xn", b + 2))
                            pool.tensor_tensor(xb_of(b + 2), xb_of(b + 2), bias_row[:, :], ALU.add).then_inc(s["xm"], 1)
                        if g > 0 and has(2):
                            add_expert(b + 2, p, 2 * g - 1)
                        if has(2):
                            add_expert(b + 2, p, 2 * g)
                        if g == 1 and has(1):
                            scale_of(at, b + 1, 1 - p)

                pool.wait_ge(ld_small, SMALL)
                batches(pool, step, LEAD, 1, first=1 - LEAD)

            def attention(ph, next_keys=False, scaled=False):
                layer = LAYER.get(ph)

                def step(b, p, has):
                    if has(2):
                        scale_of(ph, b + 2, p)
                    if ph == "attn1" and isinstance(b, int) and b == B:
                        pool.wait_ge(s["m_var"], of("moe1", "m_var", 0))
                        pool.tensor_tensor(m_rstd[:, :], m_ve[:, :], minus_half[:, :], ALU.pow).then_inc(s["m_rstd"], 1)
                    if next_keys and has(-1):
                        if isinstance(b, int) and b == 1:
                            pool.wait_ge(k_masked, B)
                        split_keys(2, b - 1, 1 - p)
                    if has(1):
                        bring_values(ph, b + 1, 1 - p)
                    if has(2):
                        split(ph, b + 2, p)

                if layer is None:
                    pool.wait_ge(v0_ready, 1)
                else:
                    pool.wait_ge(v_ready, 2 * (layer + 1))
                if not scaled:
                    for b in range(LAG):
                        scale_of(ph, b, b)
                split(ph, 0, 0)
                bring_values(ph, 0, 0)
                split(ph, 1, 1)
                if layer is None:
                    rows = slice(3 * GW, 4 * GW)
                    for b in range(B):
                        part = k_part[rows, :, P * b:P * (b + 1)]
                        pool.wait_ge(k0_upper, b + 1)
                        pool.tensor_tensor(part, k_raw[rows, b % 2, :, :], part, ALU.subtract).then_inc(k0_lower, 1)
                batches(pool, step, LAG, LAG)

            attention("attn0")
            bitffn("bit0")
            attention("attn1", next_keys=True, scaled=True)
            experts_and_attention("moe1", "attn2")
            for i, (b0, b1) in enumerate(((0, B - 1), (B - 1, B))):
                pool.wait_ge(var_all, i + 1)
                pool.tensor_tensor(rstd_all[:, b0:b1], ve_all[:, b0:b1], minus_half[:, :].to_broadcast([P, b1 - b0]),
                                   ALU.pow).then_inc(rstd_all_ready, 1)
            pool.wait_ge(k_placed, 16 * PLACES * 2 + 1)
            with pool.Fori(0, B // 2) as it:
                for u in range(2):
                    split_keys(3, it * 2 + u, u)
            attention("attn3")
            with pool.Fori(0, B // U) as it:
                for u in range(U):
                    scale_of("moe3", it * U + u, u % 2)

        @block.tensor
        def _(pe):
            for what, n in FREE.items():
                pe.sem_inc(s[what], n)
            for p in range(2):
                pe.sem_inc(h_moved[p], 1)

            pe.wait_ge(const_ready, 1)
            pe.wait_ge(ld_ctx, 16)
            for half in range(2):
                for i in range(4):
                    ins = pe.transpose(bank[half][:, P * i:P * (i + 1)], ctx_tok[:, 4 * half + i, :], ident[:, :])
                ins.then_inc(tr_ps, 1)
            def turn_projections(layer):
                pe.wait_ge(ld_w, 16 * 13)
                for i in range(4):
                    ins = pe.transpose(bank[2 + layer][:, P * i:P * (i + 1)], w_raw[:, 4 * layer + i, :], ident[:, :])
                ins.then_inc(tr_ps, 1)

            def project_keys(i, b, to, used=None):
                if used is not None:
                    pe.wait_ge(k_evac, used)
                for g in range(NG):
                    w = id_rep[:, g, :, :] if i == 0 else wk_rep[:, i - 1, g, :, :]
                    ins = pe.matmul(to[:, P * g:P * (g + 1)], w.rearrange("p a f -> p (a f)"),
                                    ctxT[:, bass.ds(b * P, P)], start=True, stop=True)
                ins.then_inc(k_ps, 1)

            def project_values(i, banks):
                for half in range(2):
                    for j in range(HB):
                        b = HB * half + j
                        ins = pe.matmul(banks[half][:, P * j:P * (j + 1)], ctxT[:, P * b:P * (b + 1)],
                                        wv_T[:, i - 1, :], start=True, stop=True)
                    ins.then_inc(v_ps, 1)

            def turn_input(ph, b, p, next_keys=False):
                pe.wait_ge(s["xn"], of(ph, "xn", b))
                if next_keys and not (isinstance(b, int) and b < 3):
                    pe.wait_ge(k_evac, b + (2 * B - 2))
                pe.wait_ge(s["qb"], of(ph, "qb", b, 0))
                pe.transpose(A_BANK[:, 0:P], xn[:, p, :], ident[:, :]).then_inc(s["xnT_ps"], 1)

            def project_queries(ph, b, p):
                layer = LAYER.get(ph)
                pe.wait_ge(s["xnT"], of(ph, "xnT", b))
                for g in range(NG):
                    w = id_rep[:, g, :, :] if layer is None else wq_rep[:, layer, g, :, :]
                    ins = pe.matmul(A_BANK[:, P * g:P * (g + 1)], w.rearrange("p a f -> p (a f)"),
                                    xnT[:, p, :], start=True, stop=True)
                ins.then_inc(s["q_ps"], 1)

            def scores(ph, b, p, g):
                if g == 0:
                    pe.wait_ge(s["qst"], of(ph, "qst", b))
                    if ph in ("attn1", "attn3"):
                        pe.wait_ge(k_masked, b + (1 if ph == "attn1" else B + 1))
                pe.wait_ge(s["sx"], of(ph, "sx", b, g + 1 - 2))
                pe.matmul(S_BANK[g % 2][:, :], q_st[:, p, P * g:P * (g + 1)],
                          k_st[:, :, g, bass.ds(b, 1), :].rearrange("p j b k -> p j (b k)"),
                          start=True, stop=True).then_inc(s["s_ps"], 1)

            def begin_attention(ph, part):
                if part == 0:
                    if ph == "attn1":
                        pe.wait_ge(k_evac, 2 * B)
                    turn_input(ph, 0, 0)
                if part == 1:
                    project_queries(ph, 0, 0)
                if part == 2:
                    turn_input(ph, 1, 1)
                if part == 3:
                    scores(ph, 0, 0, 0)
                    project_queries(ph, 1, 1)

            def moe_input(ph, b, p):
                pe.wait_ge(s["xn"], of(ph, "xn", b))
                if not (isinstance(b, int) and b == 0):
                    pe.wait_ge(s["gT"], of(ph, "gT", b - 1))
                pe.transpose(A_BANK[:, 0:P], xn[:, p, :], ident[:, :]).then_inc(s["xnT_ps"], 1)

            def moe_logits(ph, b, p):
                pe.wait_ge(s["xnT"], of(ph, "xnT", b))
                if not (isinstance(b, int) and b == 0):
                    pe.wait_ge(s["bias"], of(ph, "bias", b - 1))
                pe.matmul(O_BANK[:, 0:E], xnT[:, p, :], wr[:, 2, :], start=True, stop=True).then_inc(s["lg_ps"], 1)

            def bit_turn(ph, b, p):
                pe.wait_ge(s["xn"], of(ph, "xn", b))
                pe.transpose(bit_input(p), xq[:, p, :], ident_b[:, :]).then_inc(s["xnT_ps"], 1)

            def bit_inner(ph, b, p):
                pe.wait_ge(s["xnT"], of(ph, "xnT", b))
                if not (isinstance(b, int) and b < 2):
                    pe.wait_ge(s["h0"], of(ph, "h0", b - 2))
                for m in range(2):
                    ins = pe.matmul(S_BANK[2 * p + m][:, :], xqT[:, p, :], wbT[:, m, :], start=True, stop=True)
                ins.then_inc(s["gu_ps"], 1)

            def attention(ph, next_keys=False, begun=False):
                layer = LAYER.get(ph)

                def turn_weights(b, g):
                    pe.wait_ge(s["p"], of(ph, "p", b, g + 1))
                    pe.wait_ge(s["pt"], of(ph, "pt", b, g + 1 - 2))
                    for j in range(GH):
                        ins = pe.transpose(PT_BANK[g % 2][:, P * j:P * (j + 1)], p_sb[:, g, j, :], ident[:, :])
                    ins.then_inc(s["pt_ps"], 1)

                def products(b, p, g):
                    pe.wait_ge(s["pt"], of(ph, "pt", b, g + 1))
                    if g == 0:
                        pe.wait_ge(s["vc"], of(ph, "vc", b))
                        pe.wait_ge(s["oT"], of(ph, "oT", b, 0))
                    for j in range(GH):
                        ins = pe.matmul(O_BANK[GW * j:GW * (j + 1), P * g:P * (g + 1)], v_cur[:, p, GH * g + j, :],
                                        pt_sb[:, g % 2, j, :], start=True, stop=True, tile_position=(0, GW * j))
                    ins.then_inc(s["pv"], 1)

                def turn_back(b):
                    pe.wait_ge(s["oT"], of(ph, "oT", b))
                    if layer is None and isinstance(b, int) and b == 0:
                        pe.wait_ge(wbT_ready, 1)
                    pe.wait_ge(s["on"], of(ph, "on", b, 0))
                    for g in range(NG):
                        ins = pe.transpose(W_BANK[:, P * g:P * (g + 1)], oT_sb[:, g, :], ident[:, :])
                    ins.then_inc(s["oq_ps"], 1)

                def turn_output(b, p):
                    pe.wait_ge(s["on"], of(ph, "on", b))
                    if not (isinstance(b, int) and b == 0):
                        pe.wait_ge(s["x"], of(ph, "x", b - 1))
                    pe.transpose(R_BANK[:, 0:P], on[:, p, :], ident[:, :]).then_inc(s["onT_ps"], 1)

                def project_output(b, p):
                    pe.wait_ge(s["onT"], of(ph, "onT", b))
                    pe.matmul(R_BANK[:, 0:D], onT[:, p, :], wo_T[:, layer, :], start=True, stop=True).then_inc(s["o_ps"], 1)

                def step(b, p, has):
                    for g in range(NG):
                        if g < NG - 1 and has(0):
                            scores(ph, b, p, g + 1)
                        if g == NG - 1 and has(1):
                            scores(ph, b + 1, 1 - p, 0)
                        b2, g2, k2 = slot(b, g, 2)
                        if has(k2):
                            turn_weights(b2, g2)
                        if g == 3 and has(-1):
                            turn_back(b - 1)
                        if g == 3 and next_keys and has(0):
                            if has(2):
                                pe.wait_ge(s["qb"], of(ph, "qb", b + 2))
                            else:
                                pe.wait_ge(k_evac, 2 * B + b)
                            project_keys(2, b, A_BANK)
                        if ph == "attn1" and isinstance(b, int):
                            if (b, g) == (B, 2):
                                pe.wait_ge(k_evac, 3 * B)
                                pe.wait_ge(ld_small, SMALL)
                                pe.wait_ge(s["m_xn"], of("moe1", "m_xn", 0))
                                pe.transpose(A_BANK[:, 0:P], m_xn[:, :], ident[:, :]).then_inc(s["m_xnT_ps"], 1)
                            if (b, g) == (B + 1, 0):
                                pe.wait_ge(s["m_xnT"], of("moe1", "m_xnT", 0))
                                pe.matmul(A_BANK[:, 0:E], m_xnT[:, 0, :], wr[:, 0, :], start=True,
                                          stop=True).then_inc(s["lg_ps"], 1)
                            if (b, g) == (B + 1, 3):
                                pe.wait_ge(s["lmax"], of("moe1", "lmax", 0))
                                pe.matmul(A_BANK[:, 64:64 + E], before_b[:, :], mask_b[:, 0, :], start=True, stop=False)
                                pe.matmul(A_BANK[:, 64:64 + E], ones_b[:, :], seen_b[:, 0, :], start=False,
                                          stop=True).then_inc(s["cnt_ps"], 1)
                        if ph == "attn0" and isinstance(b, int):
                            if (b, g) == (B, 2):
                                pe.wait_ge(s["qb"], of(ph, "qb", B - 1))
                                project_values(1, (A_BANK, R_BANK))
                            if (b, g) == (B, 3):
                                pe.wait_ge(wbT_ready, 1)
                                bit_turn("bit0", 0, 0)
                            if (b, g) == (B + 1, 0):
                                bit_inner("bit0", 0, 0)
                        if ph == "attn3" and isinstance(b, int):
                            if (b, g) == (B, 2):
                                pe.wait_ge(ld_small, SMALL)
                                moe_input("moe3", 0, 0)
                            if (b, g) == (B + 1, 0):
                                moe_logits("moe3", 0, 0)
                        b3, g3, k3 = slot(b, g, 3)
                        if has(k3):
                            products(b3, p if k3 == 0 else 1 - p, g3)
                        if g == 1 and has(-2) and layer is not None:
                            turn_output(b - 2, p)
                        if g == 2 and has(-2) and layer is not None:
                            project_output(b - 2, p)
                        if g == 2 and has(2):
                            turn_input(ph, b + 2, p, next_keys)
                            project_queries(ph, b + 2, p)

                if not begun:
                    for part in range(4):
                        begin_attention(ph, part)
                batches(pe, step, LAG, LAG)

            def experts_and_attention(mo, at):
                layer = LAYER[at]

                def inner(b, p, e):
                    pe.wait_ge(s["hT"], of(mo, "hT", b, e + 1 - 2))
                    for c in range(NC):
                        ins = pe.matmul(H2_BANK[e % 2][:, P * c:P * (c + 1)], w1[:, e, P * c:P * (c + 1)],
                                        m_xnT[:, p, :], start=True, stop=True)
                    ins.then_inc(s["h_ps"], 1)

                def scores(b, p, g):
                    if g == 0:
                        pe.wait_ge(s["qst"], of(at, "qst", b))
                    pe.wait_ge(s["ss"], of(at, "ss", b, g))
                    pe.matmul(S_BANK[0][:, :], q_st[:, p, P * g:P * (g + 1)],
                              k_st[:, :, g, bass.ds(b, 1), :].rearrange("p j b k -> p j (b k)"),
                              start=True, stop=True).then_inc(s["s_ps"], 1)

                def outer(b, e):
                    pe.wait_ge(s["hT"], of(mo, "hT", b, e + 1))
                    pe.wait_ge(s["ym"], of(mo, "ym", b, e))
                    for c in range(NC):
                        ins = pe.matmul(Y_BANK[1][:, 0:D], hT[:, e % 2, c, :], w2[:, e, c, :],
                                        start=(c == 0), stop=(c == NC - 1))
                    ins.then_inc(s["y_ps"], 1)

                def step(b, p, has):
                    if isinstance(b, int) and b == -1:
                        project_values(2, (bank[4], bank[1]))
                    for g in range(NG):
                        if g == 3 and has(3):
                            pe.wait_ge(s["lmax"], of(mo, "lmax", b + 3))
                            if has(1):
                                pe.wait_ge(s["qb"], of(at, "qb", b + 1))
                            pe.matmul(A_BANK[:, 64:64 + E], before_b[:, :], mask_b[:, 1 - p, :], start=True, stop=False)
                            pe.matmul(A_BANK[:, 64:64 + E], ones_b[:, :], seen_b[:, 1 - p, :], start=False,
                                      stop=True).then_inc(s["cnt_ps"], 1)
                        if g == 2 and has(-1):
                            pe.wait_ge(s["oT"], of(at, "oT", b - 1))
                            if not (isinstance(b, int) and b == 1):
                                pe.wait_ge(s["x"], of(at, "x", b - 2))
                            for i in range(NG):
                                ins = pe.transpose(W2_BANK[:, P * i:P * (i + 1)], oT_sb[:, i, :], ident[:, :])
                            ins.then_inc(s["oq_ps"], 1)
                        if g == 3 and has(-1):
                            pe.wait_ge(s["on"], of(at, "on", b - 1))
                            pe.transpose(W2_BANK[:, 0:P], on[:, 1 - p, :], ident[:, :]).then_inc(s["onT_ps"], 1)
                        b2, g2, k2 = slot(b, g, 2)
                        if has(k2):
                            pe.wait_ge(s["pt"], of(at, "pt", b2, g2 + 1))
                            if g2 == 0:
                                pe.wait_ge(s["vc"], of(at, "vc", b2))
                                pe.wait_ge(s["oT"], of(at, "oT", b2, 0))
                            for j in range(GH):
                                ins = pe.matmul(O_BANK[GW * j:GW * (j + 1), P * g2:P * (g2 + 1)],
                                                v_cur[:, p if k2 == 0 else 1 - p, GH * g2 + j, :],
                                                pt_sb[:, g2 % 2, j, :], start=True, stop=True, tile_position=(0, GW * j))
                            ins.then_inc(s["pv"], 1)
                        if has(2):
                            inner(b + 2, p, 2 * g)
                        if g == 0 and has(1):
                            outer(b + 1, E - 1)
                        if g > 0 and has(2):
                            outer(b + 2, 2 * g - 1)
                        if g == 1 and has(3):
                            pe.wait_ge(s["m_xn"], of(mo, "m_xn", b + 3))
                            if b is not None and not (isinstance(b, int) and b == -LEAD):
                                pe.wait_ge(s["cnt"], of(mo, "cnt", b + 2))
                            pe.transpose(A_BANK[:, 0:P], m_xn[:, :], ident[:, :]).then_inc(s["m_xnT_ps"], 1)
                        if g == 2 and has(1):
                            pe.wait_ge(s["xn"], of(at, "xn", b + 1))
                            if has(3):
                                pe.wait_ge(s["lg"], of(mo, "lg", b + 3))
                            pe.transpose(A_BANK[:, 0:P], xn[:, 1 - p, :], ident[:, :]).then_inc(s["xnT_ps"], 1)
                        if has(2):
                            inner(b + 2, p, 2 * g + 1)
                            outer(b + 2, 2 * g)
                        if g == 1 and has(3):
                            pe.wait_ge(s["m_xnT"], of(mo, "m_xnT", b + 3))
                            pe.matmul(A_BANK[:, 0:E], m_xnT[:, 1 - p, :], wr[:, 0, :], start=True,
                                      stop=True).then_inc(s["lg_ps"], 1)
                        if g == 2 and has(1):
                            pe.wait_ge(s["xnT"], of(at, "xnT", b + 1))
                            for i in range(NG):
                                ins = pe.matmul(A_BANK[:, P * i:P * (i + 1)],
                                                wq_rep[:, layer, i, :, :].rearrange("p a f -> p (a f)"),
                                                xnT[:, 1 - p, :], start=True, stop=True)
                            ins.then_inc(s["q_ps"], 1)
                        if isinstance(b, int) and b == -1 and g == NG - 1:
                            pe.wait_ge(v_ready, 4)
                            pe.wait_ge(k_placed, 16 * PLACES * 2 * layer + 1)
                        if g < NG - 1 and has(0):
                            scores(b, p, g + 1)
                        if g == NG - 1 and has(1):
                            scores(b + 1, 1 - p, 0)
                        b1, g1, k1 = slot(b, g, 1)
                        if has(k1):
                            pe.wait_ge(s["psel"], of(at, "psel", b1, g1 + 1))
                            pe.wait_ge(s["pt"], of(at, "pt", b1, g1))
                            for j in range(GH):
                                ins = pe.transpose(PT_BANK[0][:, P * j:P * (j + 1)], p_sb[:, g1, j, :], ident[:, :])
                            ins.then_inc(s["pt_ps"], 1)
                        if g == 3 and has(-1):
                            pe.wait_ge(s["onT"], of(at, "onT", b - 1))
                            pe.matmul(W2_BANK[:, 0:D], onT[:, 1 - p, :], wo_T[:, layer, :], start=True,
                                      stop=True).then_inc(s["o_ps"], 1)

                pe.wait_ge(ld_moe1, 32 * E)
                pe.wait_ge(ld_small, SMALL)
                pe.wait_ge(k_evac, 3 * B)
                pe.wait_ge(s["x"], of("attn1", "x", B - 1))
                batches(pe, step, LEAD, 1, first=1 - LEAD)

            def bitffn(ph):
                def outer(b, p, has):
                    if has(-2):
                        pe.wait_ge(s["x"], of(ph, "x", b - 1))
                    pe.wait_ge(s["hqT"], of(ph, "hqT", b))
                    for c in range(NC):
                        ins = pe.matmul(O_BANK[:, 0:D], hqT[:, p, P * c:P * (c + 1)], wbT[:, 2, P * c:P * (c + 1)],
                                        start=(c == 0), stop=(c == NC - 1))
                    ins.then_inc(s["dn_ps"], 1)

                def step(b, p, has):
                    if has(1):
                        bit_turn(ph, b + 1, 1 - p)
                    if has(-1):
                        outer(b - 1, 1 - p, has)
                    if has(1):
                        bit_inner(ph, b + 1, 1 - p)
                    if has(0):
                        pe.wait_ge(s["h"], of(ph, "h", b))
                        for c in range(NC):
                            ins = pe.transpose(halfword(PT_BANK[p])[:, P * c:P * (c + 1)], hq[:, p, P * c:P * (c + 1)],
                                               ident_b[:, :])
                        ins.then_inc(s["hqT_ps"], 1)
                        if has(-1):
                            pe.wait_ge(k_evac, b + B)
                        project_keys(1, b, A_BANK)

                pe.wait_ge(v_ready, 2)
                pe.wait_ge(s["x"], of("attn0", "x", B - 1))
                batches(pe, step, 2, 2)

            def moe(ph):
                def turn_gates(b, p):
                    pe.wait_ge(s["gates"], of(ph, "gates", b))
                    pe.transpose(A_BANK[0:E, 0:P], gates[:, p, :], ident[:, :]).then_inc(s["gT_ps"], 1)

                def outer_bias(b, p):
                    pe.wait_ge(s["gT"], of(ph, "gT", b))
                    pe.matmul(O_BANK[:, 0:D], gT[:, p, :], b2_sb[:, 1, :], start=True, stop=True).then_inc(s["b2_ps"], 1)

                def step(b, p, has):
                    for e in range(E):
                        if e == 2 and isinstance(b, int) and b == 0:
                            pe.wait_ge(s["x"], of("attn3", "x", B - 1))
                        if has(0):
                            pe.wait_ge(s["hT3"], of(ph, "hT3", b, e + 1 - 4))
                            for c in range(NC):
                                ins = pe.matmul(S_BANK[e % 4][:, P * c:P * (c + 1)], w1[:, e, P * c:P * (c + 1)],
                                                xnT[:, p, :], start=True, stop=True)
                            ins.then_inc(s["h_ps"], 1)
                        b3, e3 = (b, e - 3) if e >= 3 else (b - 1, e - 3 + E)
                        if has(0 if e >= 3 else -1):
                            pe.wait_ge(s["hT3"], of(ph, "hT3", b3, e3 + 1))
                            pe.wait_ge(s["acc"], of(ph, "acc", b3, e3 + 1 - 2))
                            for c in range(NC):
                                ins = pe.matmul(Y_BANK[e3 % 2][:, 0:D], hT3[:, e3 % 4, c, :], w2[:, e3, c, :],
                                                start=(c == 0), stop=(c == NC - 1))
                            ins.then_inc(s["y_ps"], 1)
                        if e == 1 and has(0):
                            turn_gates(b, p)
                        if e == 2 and has(0):
                            outer_bias(b, p)
                        if e == 3 and has(1):
                            moe_input(ph, b + 1, 1 - p)
                        if e == 4 and has(1):
                            moe_logits(ph, b + 1, 1 - p)

                pe.wait_ge(ld_moe3, 32 * E)
                batches(pe, step, 1, 1)

            def choose_tokens(ph):
                def turn(b0, b1):
                    for b in range(b0, b1):
                        pe.wait_ge(s["xn"], of(ph, "xn", b))
                        ins = pe.transpose(PT_BANK[b // HB][:, P * (b % HB):P * (b % HB + 1)], xn8[:, b, :], ident[:, :])
                    if b1 % HB == 0:
                        ins.then_inc(xn8T_ps, 1)

                def logits(half):
                    pe.wait_ge(xn8T_ready, half + 1)
                    for b in range(HB * half, HB * (half + 1)):
                        ins = pe.matmul(bank[0][:, E * b:E * (b + 1)], xnT_all[:, b, :], wr[:, 1, :], start=True, stop=True)
                    return ins

                turn(0, HB)
                turn(HB, B - 1)
                logits(0)
                turn(B - 1, B)
                ins = logits(1)
                ins.then_inc(lg_all_ps, 1)
                pe.wait_ge(prob_ready, 1)
                for b in range(B):
                    ins = pe.transpose(bank[1 + b // HB][0:E, P * (b % HB):P * (b % HB + 1)], prob[:, b, :], ident[:, :])
                ins.then_inc(probT_ps, 1)
                pe.wait_ge(ld_ec, 16 * (1 + NC2))
                pe.wait_ge(probT_ready, 1)
                with pe.Fori(0, B // 2) as it:
                    for p in range(2):
                        b = it * 2 + p
                        for g in range(NEG):
                            pe.wait_ge(s["hT"], of("ec2", "hT", b, g + 1 - 2))
                            for c, n in enumerate(FROWS2):
                                ins = pe.matmul(bank[g % 2][0:n, P * c:P * (c + 1)], wu2[:, g, FC2 * c:FC2 * c + n],
                                                xnT_all[:, bass.ds(b, 1), :].rearrange("p b t -> p (b t)"),
                                                start=True, stop=True)
                            ins.then_inc(s["h_ps"], 1)
                        project_keys(3, b, bank[6 + p], b + (B * 3 - 1))
                pe.wait_ge(xn8T_ready, 2)
                project_values(3, PT_BANK)
                pe.wait_ge(k_evac, B * 4)
                pe.wait_ge(taken_ready, 1)
                for b in range(B):
                    ins = pe.transpose(bank[3][:, E * b:E * (b + 1)], takenT[:, P * b:P * (b + 1)], ident[0:E, 0:E])
                ins.then_inc(taken_ps, 1)

            def expert_choice(ph):
                for p in range(2):
                    pe.wait_ge(h_moved[p], 16 * NC2 * (B // 2) + 1)
                for b in range(B):
                    pe.wait_ge(s["gT"], of(ph, "gT", b))
                    if b >= 1:
                        pe.wait_ge(s["acc"], of(ph, "acc", b - 1, 1))
                    pe.matmul(O_BANK[:, 0:D], gT[:, b % 2, :], b2_sb[:, 0, :], start=True, stop=True).then_inc(s["b2_ps"], 1)
                    for g in range(NEG):
                        pe.wait_ge(s["acc"], of(ph, "acc", b, g + 1 - 2))
                        for c, n in enumerate(FROWS2):
                            ins = pe.matmul(Y_BANK[g % 2][:, 0:EGRP * D], h_of(b, c)[0:n, g, :],
                                            wd2[0:n, c, EGRP * g:EGRP * (g + 1), :],
                                            start=(c == 0), stop=(c == NC2 - 1))
                        ins.then_inc(s["y_ps"], 1)
                        if b == B - 1:
                            begin_attention("attn3", g)

            pe.wait_ge(const_ready, 2)
            for b in range(LAG):
                turn_input("attn0", b, b)
                project_queries("attn0", b, b)
                turn_projections(b)
            pe.wait_ge(ctxT_ready, 2)
            for b in range(B):
                if b == 1:
                    pe.wait_ge(s["qb"], of("attn0", "qb", 1))
                project_keys(0, b, bank[7 - b % 2], b - 1 if b >= 2 else None)
                if b == 1:
                    turn_projections(2)
                if b == HB - 1:
                    pe.wait_ge(wsum_ready, 3)
                    pe.wait_ge(const_ready, 4)
                    pe.matmul(bank[5][:, 0:3], ones[:, :], wstat[:, 0, :], start=True, stop=True).then_inc(wtot_ps, 1)
            pe.wait_ge(w_ready, 4)
            pe.wait_ge(k_evac, B)
            pe.wait_ge(k0_masked, B)
            pe.wait_ge(k0_scaled, B)
            pe.sem_inc(k_placed, 1)
            scores("attn0", 0, 0, 0)
            pe.wait_ge(wb_ready, 3)
            for m in range(3):
                for c in range(NC):
                    ins = pe.transpose(wbT_place(m)[:, P * c:P * (c + 1)], wb_q[:, m, P * c:P * (c + 1)], ident_b[:, :])
            ins.then_inc(wbT_ps, 1)
            attention("attn0", begun=True)
            bitffn("bit0")
            attention("attn1", next_keys=True)
            experts_and_attention("moe1", "attn2")
            choose_tokens("ecr2")
            expert_choice("ec2")
            attention("attn3", begun=True)
            moe("moe3")

        @block.scalar
        def _(act):
            own = Chain(act, act_own)
            act.wait_ge(tr_ps, 1)
            act.copy(ctxT[:, 0:HALF], bank[0][:, :]).then_inc(ctxT_ready, 1)
            act.wait_ge(tr_ps, 2)
            act.copy(ctxT[:, HALF:T], bank[1][:, :]).then_inc(ctxT_ready, 1)

            def place_keys(i, b, j0=0, j1=GH):
                if j0 == 0:
                    hold(act, k_split, b + (B * (i - 1) + 1))
                for j in range(j0, j1):
                    ins = act.activation(k_st[:, j, :, bass.ds(b, 1), :].rearrange("p g b k -> p (g b) k"),
                                         k_part[:, :, bass.ds(b * P, P)], ACT.Copy, scale=head_mask[:, j:j + 1])
                if j1 == GH:
                    ins.then_inc(k_masked, 1)

            def evacuate_keys(i, b, p, bk):
                hold(act, k_ps, b + (B * i + 1))
                if isinstance(b, int) and b < 2 and i < 2:
                    if i == 1:
                        act.wait_ge(k0_split, B)
                        act.wait_ge(k0_lower, B)
                else:
                    if i == 0:
                        act.wait_ge(k0_lower, b - 1)
                    hold(act, *((k0_split, b - 1) if i == 0 else (k_split, b + (B * (i - 1) - 1))))
                if i == 0:
                    act.copy(k_raw[:, p, :, :].rearrange("p g k -> p (g k)"), bk[:, :]).then_inc(k_evac, 1)
                else:
                    for g in range(NG):
                        ins = act.activation(k_raw[:, p, g, :], bk[:, P * g:P * (g + 1)], ACT.Identity,
                                             bias=bk_rep[:, i - 1, g:g + 1])
                    ins.then_inc(k_evac, 1)

            def copy_input(ph, b, p):
                act.wait_ge(s["xnT_ps"], of(ph, "xnT_ps", b))
                act.copy(xnT[:, p, :], A_BANK[:, 0:P]).then_inc(s["xnT"], 1)

            def copy_queries(ph, b, p):
                layer = LAYER.get(ph)
                act.wait_ge(s["q_ps"], of(ph, "q_ps", b))
                hold(act, s["qst"], of(ph, "qst", b, 0))
                if layer is None:
                    act.copy(qb[:, :], A_BANK[:, :]).then_inc(s["qb"], 1)
                else:
                    for g in range(NG):
                        ins = act.activation(qb[:, P * g:P * (g + 1)], A_BANK[:, P * g:P * (g + 1)], ACT.Identity,
                                             bias=bq_rep[:, layer, g:g + 1])
                    ins.then_inc(s["qb"], 1)

            def begin_attention(ph):
                for b in range(LAG):
                    copy_input(ph, b, b)
                    copy_queries(ph, b, b)

            def moe_copy_input(ph, b, p):
                act.wait_ge(s["xnT_ps"], of(ph, "xnT_ps", b))
                act.copy(xnT[:, p, :], A_BANK[:, 0:P]).then_inc(s["xnT"], 1)

            def moe_exponents(ph, b, p):
                act.wait_ge(s["lmax"], of(ph, "lmax", b))
                act.activation(el[:, p, :], lrow[:, p, 0:E], ACT.Exp, bias=nlm[:, p, :],
                               accum_out=esum[:, p, :]).then_inc(s["lexp"], 1)

            def bit_front(ph, b, p, between=lambda: None):
                act.wait_ge(s["xnT_ps"], of(ph, "xnT_ps", b))
                act.copy(xqT[:, p, :], bit_input(p)).then_inc(s["xnT"], 1)
                between()
                act.wait_ge(s["gu_ps"], of(ph, "gu_ps", b))
                act.activation(gate[:, p, :], S_BANK[2 * p][:, :], ACT.Silu, scale=deq[:, p, 0:1]).then_inc(s["gate"], 1)

            def attention(ph, next_keys=False, begun=False):
                layer = LAYER.get(ph)

                def weights(b, g):
                    act.wait_ge(s["sx"], of(ph, "sx", b, g + 1))
                    flat = p_sb[:, g, :, :].rearrange("p j k -> p (j k)")
                    act.activation(flat, flat, ACT.Exp, scale=C).then_inc(s["p"], 1)

                def copy_weights(b, g):
                    act.wait_ge(s["pt_ps"], of(ph, "pt_ps", b, g + 1))
                    hold(act, s["pv"], of(ph, "pv", b, g + 1 - 2))
                    act.copy(pt_sb[:, g % 2, :, :].rearrange("p j k -> p (j k)"), PT_BANK[g % 2][:, :]).then_inc(s["pt"], 1)

                def copy_products(b):
                    act.wait_ge(s["pv"], of(ph, "pv", b, NG))
                    hold(act, s["oq_ps"], of(ph, "oq_ps", b, 0))
                    act.copy(oT_sb[:, :, :].rearrange("p g q -> p (g q)"), O_BANK[:, :]).then_inc(s["oT"], 1)

                def step(b, p, has):
                    for g in range(NG):
                        if g == 3 and has(-1):
                            copy_products(b - 1)
                        if g == 3 and has(2):
                            copy_queries(ph, b + 2, p)
                        b2, g2, k2 = slot(b, g, 2)
                        if has(k2):
                            copy_weights(b2, g2)
                        if has(0):
                            weights(b, g)
                        if ph == "attn1" and isinstance(b, int):
                            if (b, g) == (B, 2):
                                act.wait_ge(s["m_xnT_ps"], of("moe1", "m_xnT_ps", 0))
                                act.copy(m_xnT[:, 0, :], A_BANK[:, 0:P]).then_inc(s["m_xnT"], 1)
                            if (b, g) == (B + 1, 0):
                                act.wait_ge(s["lg_ps"], of("moe1", "lg_ps", 0))
                                act.copy(lrow[:, 0, 0:E], A_BANK[:, 0:E]).then_inc(s["lg"], 1)
                            if (b, g) == (B + 1, 3):
                                act.wait_ge(s["cnt_ps"], of("moe1", "cnt_ps", 0))
                                act.copy(cnt_sb[:, :], A_BANK[:, 64:64 + E]).then_inc(s["cnt"], 1)
                                act.wait_ge(s["lmax"], of("moe1", "lmax", 0))
                                act.activation(el[:, 0, :], lrow[:, 0, 0:E], ACT.Exp, bias=nlm[:, 0, :],
                                               accum_out=esum[:, 0, :]).then_inc(s["lexp"], 1)
                        if ph == "attn0" and isinstance(b, int) and (b, g) == (B + 1, 0):
                            bit_front("bit0", 0, 0)
                        if ph == "attn3" and isinstance(b, int):
                            if (b, g) == (B, 2):
                                moe_copy_input("moe3", 0, 0)
                        if g == 1 and has(-2) and layer is not None:
                            act.wait_ge(s["onT_ps"], of(ph, "onT_ps", b - 2))
                            act.copy(onT[:, p, :], R_BANK[:, 0:P]).then_inc(s["onT"], 1)
                        if ph == "attn3" and isinstance(b, int) and (b, g) == (B + 1, 1):
                            moe_exponents("moe3", 0, 0)
                        if g == 1 and has(2):
                            copy_input(ph, b + 2, p)
                        if g == 3 and next_keys and has(0):
                            evacuate_keys(2, b, p, A_BANK)
                        if g in (1, 3) and ph == "attn1" and isinstance(b, int) and b == 0:
                            place_keys(1, B - 2 + g // 2)
                        if g == 3 and ph == "attn3" and isinstance(b, int) and b == 0:
                            act.wait_ge(s["y_ps"], of("ec2", "y_ps", B - 1, NEG))
                            place_keys(3, B - 1)

                if not begun:
                    begin_attention(ph)
                batches(act, step, LAG, LAG)

            def experts_and_attention(mo, at):
                layer = LAYER[at]

                def gelu(b, e):
                    act.wait_ge(s["h_ps"], of(mo, "h_ps", b, e + 1))
                    hold(act, s["y_ps"], of(mo, "y_ps", b, e + 1 - 2))
                    act.activation(hT[:, e % 2, :, :].rearrange("p c k -> p (c k)"), H2_BANK[e % 2][:, :],
                                   ACT.Gelu_apprx_tanh).then_inc(s["hT"], 1)

                def copy_scores(b, g):
                    act.wait_ge(s["s_ps"], of(at, "s_ps", b, g + 1))
                    if g >= 2 or not (isinstance(b, int) and b == 0):
                        hold(act, s["sd"], of(at, "sd", b, 2 * (g - 2) + 1))
                    act.copy(ss[:, g % 2, :, :].rearrange("p j k -> p (j k)"), S_BANK[0][:, :]).then_inc(s["ss"], 1)

                def weigh(b, p, e):
                    if e == 0:
                        hold(act, s["gates"], of(mo, "gates", b))
                    hold(act, s["xm"], of(mo, "xm", b, e))
                    hold(act, s["y_ps"], of(mo, "y_ps", b, e + 1))
                    act.activation(ys[:, e % 2, :], Y_BANK[1][:, 0:D], ACT.Copy, scale=gates[:, p, e:e + 1]).then_inc(s["ym"], 1)

                def step(b, p, has):
                    for g in range(NG):
                        if g == 3 and has(3):
                            hold(act, s["cnt_ps"], of(mo, "cnt_ps", b + 3))
                            act.copy(cnt_sb[:, :], A_BANK[:, 64:64 + E]).then_inc(s["cnt"], 1)
                            hold(act, s["lmax"], of(mo, "lmax", b + 3))
                            act.activation(el[:, 1 - p, :], lrow[:, 1 - p, 0:E], ACT.Exp, bias=nlm[:, 1 - p, :],
                                           accum_out=esum[:, 1 - p, :]).then_inc(s["lexp"], 1)
                        b1, g1, k1 = slot(b, g, 1)
                        if has(k1):
                            flat = p_sb[:, g1, :, :].rearrange("p j k -> p (j k)")
                            act.wait_ge(s["sd"], of(at, "sd", b1, 2 * g1 + 1))
                            act.activation(flat, flat, ACT.Exp, scale=C).then_inc(s["ex"], 1)
                            flat = sel[:, g1 % 2, :, :].rearrange("p j k -> p (j k)")
                            act.wait_ge(s["sd"], of(at, "sd", b1, 2 * g1 + 2))
                            act.activation(flat, flat, ACT.Exp, scale=C).then_inc(s["ex"], 1)
                        if has(2):
                            gelu(b + 2, 2 * g)
                        if g == 0 and has(1):
                            weigh(b + 1, 1 - p, E - 1)
                        if g > 0 and has(2):
                            weigh(b + 2, p, 2 * g - 1)
                        if g == 1 and has(3):
                            act.wait_ge(s["m_xnT_ps"], of(mo, "m_xnT_ps", b + 3))
                            act.copy(m_xnT[:, 1 - p, :], A_BANK[:, 0:P]).then_inc(s["m_xnT"], 1)
                        if g == 2 and has(1):
                            act.wait_ge(s["xnT_ps"], of(at, "xnT_ps", b + 1))
                            act.copy(xnT[:, 1 - p, :], A_BANK[:, 0:P]).then_inc(s["xnT"], 1)
                        if g == 3 and has(-1):
                            act.wait_ge(s["onT_ps"], of(at, "onT_ps", b - 1))
                            act.copy(onT[:, 1 - p, :], W2_BANK[:, 0:P]).then_inc(s["onT"], 1)
                        if has(2):
                            gelu(b + 2, 2 * g + 1)
                            weigh(b + 2, p, 2 * g)
                        if g == 1 and has(3):
                            hold(act, s["lg_ps"], of(mo, "lg_ps", b + 3))
                            act.copy(lrow[:, 1 - p, 0:E], A_BANK[:, 0:E]).then_inc(s["lg"], 1)
                        if g == 2 and has(1):
                            act.wait_ge(s["q_ps"], of(at, "q_ps", b + 1))
                            hold(act, s["qst"], of(at, "qst", b + 1, 0))
                            for i in range(NG):
                                ins = act.activation(qb[:, P * i:P * (i + 1)], A_BANK[:, P * i:P * (i + 1)], ACT.Identity,
                                                     bias=bq_rep[:, layer, i:i + 1])
                            ins.then_inc(s["qb"], 1)
                        if g < NG - 1 and has(0):
                            copy_scores(b, g + 1)
                        if g == NG - 1 and has(1):
                            copy_scores(b + 1, 0)
                        if has(k1):
                            act.wait_ge(s["pt_ps"], of(at, "pt_ps", b1, g1 + 1))
                            hold(act, s["pv"], of(at, "pv", b1, g1 + 1 - 2))
                            act.copy(pt_sb[:, g1 % 2, :, :].rearrange("p j k -> p (j k)"), PT_BANK[0][:, :])\
                               .then_inc(s["pt"], 1)
                        if g == 1 and has(-1):
                            act.wait_ge(s["pv"], of(at, "pv", b - 1, NG))
                            hold(act, s["oq_ps"], of(at, "oq_ps", b - 1, 0))
                            act.copy(oT_sb[:, :, :].rearrange("p g q -> p (g q)"), O_BANK[:, :]).then_inc(s["oT"], 1)

                batches(act, step, LEAD, 1, first=1 - LEAD)

            def bitffn(ph):
                def step(b, p, has):
                    def place(j0, j1):
                        if has(-2) and has(0):
                            place_keys(1, b - 2, j0, j1)

                    if has(1):
                        bit_front(ph, b + 1, 1 - p, lambda: place(0, 2))
                    else:
                        place(0, 2)
                    if has(0):
                        act.wait_ge(s["hqT_ps"], of(ph, "hqT_ps", b))
                        act.copy(hqT[:, p, :], halfword(PT_BANK[p])).then_inc(s["hqT"], 1)
                        evacuate_keys(1, b, p, A_BANK)
                    place(2, GH)

                batches(act, step, 2, 2)

            def moe(ph):
                def copy_gates(b, p):
                    act.wait_ge(s["gT_ps"], of(ph, "gT_ps", b))
                    act.copy(gT[:, p, :], A_BANK[0:E, 0:P]).then_inc(s["gT"], 1)

                def step(b, p, has):
                    for e in range(E):
                        if has(0):
                            act.wait_ge(s["h_ps"], of(ph, "h_ps", b, e + 1))
                            if e >= 4 or not (isinstance(b, int) and b == 0):
                                hold(act, s["y_ps"], of(ph, "y_ps", b, e + 1 - 4))
                            for c in range(NC):
                                ins = act.activation(hT3[:, e % 4, c, :], S_BANK[e % 4][:, P * c:P * (c + 1)], ACT.Gelu,
                                                     bias=b1_col[:, e, c:c + 1])
                            ins.then_inc(s["hT3"], 1)
                        if e == 1 and has(0):
                            copy_gates(b, p)
                        if e == 3 and has(1):
                            moe_copy_input(ph, b + 1, 1 - p)
                        if e == 5 and has(1):
                            moe_exponents(ph, b + 1, 1 - p)

                batches(act, step, 1, 1)

            def choose_tokens(ph):
                for half in range(2):
                    act.wait_ge(xn8T_ps, half + 1)
                    act.copy(xnT_all[:, HB * half:HB * (half + 1), :].rearrange("p b t -> p (b t)"),
                             PT_BANK[half][:, :]).then_inc(xn8T_ready, 1)
                act.wait_ge(lg_all_ready, 1)
                act.activation(prob[:, :, :], lg_all[:, :, :], ACT.Exp).then_inc(lexp_all, 1)
                act.wait_ge(probT_ps, 1)
                for half in range(2):
                    ins = act.copy(probT[:, HALF * half:HALF * (half + 1)], bank[1 + half][0:E, :])
                ins.then_inc(probT_ready, 1)
                with act.Fori(0, B // 2) as it:
                    for p in range(2):
                        b = it * 2 + p
                        hold(act, h_moved[p], it * (16 * NC2) + 1)
                        for g in range(NEG):
                            hold(act, s["h_ps"], of("ec2", "h_ps", b, g + 1))
                            for c, n in enumerate(FROWS2):
                                ins = act.activation(h_stage[p][0:n, NEG * c + g, :], bank[g % 2][0:n, P * c:P * (c + 1)],
                                                     ACT.Silu, bias=bu2[0:n, g, c:c + 1])
                            ins.then_inc(s["hT"], 1)
                        evacuate_keys(3, b, p, bank[6 + p])

            def expert_choice(ph):
                act.wait_ge(gT_all_ready, 1)
                for b in range(2):
                    act.copy(gT[:, b, :], probT[:, P * b:P * (b + 1)]).then_inc(s["gT"], 1)
                with act.Fori(0, (B - 2) // 2) as it:
                    for p in range(2):
                        b = it * 2 + p
                        hold(act, s["y_ps"], of(ph, "y_ps", b, NEG))
                        act.copy(gT[:, p, :], probT[:, bass.ds(b * P + 2 * P, P)]).then_inc(s["gT"], 1)
                        place_keys(3, b)
                act.wait_ge(s["y_ps"], of(ph, "y_ps", B - 2, NEG))
                place_keys(3, B - 2)
                begin_attention("attn3")

            begin_attention("attn0")
            def scale_keys(b):
                act.wait_ge(k0_split, b + 1)
                act.wait_ge(k0_lower, b + 1)
                for j in range(GH // 2, GH):
                    ins = act.activation(k_st[:, j, :, b, :], k_part[:, :, P * b:P * (b + 1)], ACT.Copy,
                                         scale=head_mask[:, j:j + 1])
                ins.then_inc(k0_scaled, 1)

            copies = []
            for layer in range(3):
                wt = bank[2 + layer][:, :].rearrange("p (m g f) -> p m g f", m=4, g=NG)
                copies += [(wk_rep[:, layer, :, part, :], wt[:, 1, :, :]) for part in range(NPART)]
                copies += [(wv_T[:, layer, :], bank[2 + layer][:, 2 * D:3 * D]),
                           (wo_T[:, layer, :], bank[2 + layer][:, 3 * D:4 * D])]
            each = -(-len(copies) // (B - 2))
            act.wait_ge(ld_bit, 48)
            for b in range(B):
                evacuate_keys(0, b, b % 2, bank[7 - b % 2])
                if b >= 1:
                    scale_keys(b - 1)
                if b < 3:
                    act.activation(shared[:, b, :], wb_raw[:, b, :], ACT.Abs, accum_out=wstat[:, 0, b:b + 1])\
                       .then_inc(wsum_ready, 1)
                if 1 <= b < B - 1:
                    act.wait_ge(w_ready, (b + 1) // 2)
                    for dst, src in copies[each * (b - 1):each * b]:
                        ins = act.copy(dst, src)
                if b == B - 2:
                    ins.then_inc(w_ready, 1)
            scale_keys(B - 1)
            act.wait_ge(wbT_ps, 1)
            for m in range(3):
                ins = act.copy(wbT[:, m, :], wbT_place(m))
            ins.then_inc(wbT_ready, 1)
            attention("attn0", begun=True)
            act.wait_ge(ld_small, SMALL)
            bitffn("bit0")
            attention("attn1", next_keys=True)
            experts_and_attention("moe1", "attn2")
            choose_tokens("ecr2")
            expert_choice("ec2")
            attention("attn3", begun=True)
            moe("moe3")

        @block.vector
        def _(dve):
            own = Chain(dve, dve_own)

            def need(n):
                dve.wait_ge(dve_own, own.value(n))

            def need_alone(n):
                hold(dve, dve_own, own.value(n))

            def moments(ph, b, p, x_ready=None):
                if x_ready is not None:
                    hold(dve, *x_ready)
                n = own.mark(dve.bn_stats(stats[:, p, :], xb_of(b)))
                need_alone(n)
                n = own.mark(dve.bn_aggr(mv[:, p, :], stats[:, p, :]))
                need(n)
                dve.tensor_scalar(ve[:, p, :], mv[:, p, 1:2], LN_EPS, None, ALU.add).then_inc(s["var"], 1)

            def scaled(ph, b, p):
                dve.wait_ge(s["rstd"], of(ph, "rstd", b))
                return dve.tensor_scalar(xn[:, p, :], xb_of(b), mv[:, p, 0:1], rstd[:, p, :], ALU.subtract, ALU.mult)

            def values(i, banks=PT_BANK):
                for half in range(2):
                    dve.wait_ge(v_ps, 2 * (i - 1) + half + 1)
                    bias = bv_row[:, i - 1, :].rearrange("p (o h d) -> p o h d", o=1, h=NH)
                    for j in range(HB):
                        ins = dve.tensor_tensor(v_aug[:, HB * half + j, :, 0:DK],
                                                banks[half][:, P * j:P * (j + 1)].rearrange("p (h d) -> p h d", h=NH),
                                                bias[:, 0, :, :], ALU.add)
                    ins.then_inc(v_ready, 1)

            def normalize(ph, b, p, bank_w):
                dve.wait_ge(s["oq_ps"], of(ph, "oq_ps", b))
                o = bank_w[:, :].rearrange("p (h v) -> p h v", h=NH)
                n = own.mark(dve.reciprocal(rden[:, p, :], o[:, :, DK]))
                need(n)
                dve.tensor_tensor(on[:, p, :].rearrange("p (h d) -> p h d", h=NH), o[:, :, 0:DK],
                                  rden[:, p, :].unsqueeze(2).to_broadcast([P, NH, DK]), ALU.mult).then_inc(s["on"], 1)

            def add_bias_row(ph, b, p, bank_o):
                dve.wait_ge(s["o_ps"], of(ph, "o_ps", b))
                return own.mark(dve.tensor_tensor(t_row[:, p, :], bank_o[:, 0:D], bo_row[:, LAYER[ph], :], ALU.add))

            def add(ph, b, p, bank_o):
                layer = LAYER.get(ph)
                if layer is None:
                    dve.wait_ge(s["on"], of(ph, "on", b))
                    dve.tensor_tensor(xb_of(b), xb_of(b), on[:, p, :], ALU.add).then_inc(s["x"], 1)
                else:
                    need(add_bias_row(ph, b, p, bank_o))
                    dve.tensor_tensor(xb_of(b), xb_of(b), t_row[:, p, :], ALU.add).then_inc(s["x"], 1)

            def moe_maximum(ph, b, p):
                dve.wait_ge(s["lg_ps"], of(ph, "lg_ps", b))
                n = own.mark(dve.tensor_copy(lrow[:, p, 0:E], O_BANK[:, 0:E]))
                need_alone(n)
                n = own.mark(dve.max(top8[:, p, :], lrow[:, p, :]))
                need(n)
                own.mark(dve.tensor_scalar(nlm[:, p, :], top8[:, p, 0:1], -1.0, None, ALU.mult))
                n1 = own.mark(dve.tensor_copy(pick8[:, p, 0:TOPK_E], top8[:, p, 0:TOPK_E]))
                need_alone(n1)
                dve.sem_inc(s["lmax"], 1)
                n = own.mark(dve.match_replace(lmark[:, p, :], pick8[:, p, :], lrow[:, p, :], TAKEN))
                need(n)
                own.mark(dve.tensor_scalar(maskf[:, p, :], lmark[:, p, 0:E], TAKEN, None, ALU.is_equal))

            def moe_gates(ph, b, p):
                n = own.n
                dve.wait_ge(s["lexp"], of(ph, "lexp", b))
                n1 = own.mark(dve.reciprocal(rsum[:, p, :], esum[:, p, :]))
                need(n1)
                n = own.mark(dve.scalar_tensor_tensor(pr[:, p, :], el[:, p, :], rsum[:, p, :], maskf[:, p, :],
                                                      ALU.mult, ALU.mult))
                need(n)
                n = own.mark(dve.tensor_reduce(gsum[:, p, 0:1], pr[:, p, :], AX, ALU.add))
                need(n)
                n = own.mark(dve.tensor_scalar(gsum[:, p, 1:2], gsum[:, p, 0:1], NORM_EPS, None, ALU.add))
                need(n)
                n = own.mark(dve.reciprocal(gsum[:, p, 2:3], gsum[:, p, 1:2]))
                need(n)
                dve.tensor_scalar(gates[:, p, :], pr[:, p, :], gsum[:, p, 2:3], None, ALU.mult).then_inc(s["gates"], 1)

            def magnitude(src, p, which):
                return own.mark(dve.tensor_reduce(amax[:, p, which:which + 1], src, AX, ALU.max,
                                                  apply_absolute_value=True))

            def clipped(p, which):
                return own.mark(dve.tensor_scalar(aclip[:, p, which:which + 1], amax[:, p, which:which + 1], QMIN,
                                                  1.0 / 127.0, ALU.max, ALU.mult))

            def scales(p, which):
                n = own.mark(dve.reciprocal(qscale[:, p, which:which + 1], aclip[:, p, which:which + 1]))
                for m in ((0, 1), (2,))[which]:
                    own.mark(dve.tensor_scalar(deq[:, p, m:m + 1], aclip[:, p, which:which + 1],
                                               wstat[:, 1, m:m + 1], None, ALU.mult))
                return n

            def rounded(tmp, src, p, which):
                return own.mark(dve.tensor_scalar(tmp, src, qscale[:, p, which:which + 1], ROUND, ALU.mult, ALU.add))

            def quantize_input(ph, b, p):
                n = own.mark(scaled(ph, b, p))
                need(n)
                n = magnitude(xn[:, p, :], p, 0)
                need(n)
                n = clipped(p, 0)
                need(n)
                n = scales(p, 0)
                need(n)
                n = rounded(xr[:, p, :], xn[:, p, :], p, 0)
                need(n)
                dve.tensor_scalar(xq[:, p, :], xr[:, p, :], ROUND, None, ALU.subtract).then_inc(s["xn"], 1)

            marked_m = [0]

            def begin_experts(mo, b, q, g, rnd, before):
                x3 = x_res[:, bass.ds(b, 1), :].rearrange("p b d -> p (b d)")
                if (g, rnd) == (0, 0):
                    hold(dve, s["x"], of(before, "x", b))
                    marked_m[0] = own.mark(dve.bn_stats(m_stats[:, :], x3))
                if (g, rnd) == (0, 1):
                    need_alone(marked_m[0])
                    marked_m[0] = own.mark(dve.bn_aggr(m_mv[:, :], m_stats[:, :]))
                if (g, rnd) == (0, 2):
                    need(marked_m[0])
                    dve.tensor_scalar(m_ve[:, :], m_mv[:, 1:2], LN_EPS, None, ALU.add).then_inc(s["m_var"], 1)
                if (g, rnd) == (1, 0):
                    dve.wait_ge(s["m_rstd"], of(mo, "m_rstd", b))
                    dve.tensor_scalar(m_xn[:, :], x3, m_mv[:, 0:1], m_rstd[:, :], ALU.subtract,
                                      ALU.mult).then_inc(s["m_xn"], 1)
                if (g, rnd) == (2, 0):
                    hold(dve, s["lg"], of(mo, "lg", b))
                    marked_m[0] = own.mark(dve.max(top8[:, q, :], lrow[:, q, :]))
                if (g, rnd) == (2, 1):
                    need(marked_m[0])
                    marked_m[0] = own.mark(dve.tensor_copy(pick8[:, q, 0:TOPK_E], top8[:, q, 0:TOPK_E]))
                    own.mark(dve.tensor_scalar(nlm[:, q, :], top8[:, q, 0:1], -1.0, None, ALU.mult))
                    need_alone(marked_m[0])
                    marked_m[0] = own.mark(dve.match_replace(lmark[:, q, :], pick8[:, q, :], lrow[:, q, :], TAKEN))
                if (g, rnd) == (2, 2):
                    need(marked_m[0])
                    marked_m[0] = own.mark(dve.tensor_scalar(maskf[:, q, :], lmark[:, q, 0:E], TAKEN, None,
                                                             ALU.is_equal))
                if (g, rnd) == (2, 3):
                    own.mark(dve.tensor_copy(seen_b[:, q, :], seen[:, :]))
                    need(marked_m[0])
                    own.mark(dve.tensor_copy(mask_b[:, q, :], maskf[:, q, :]))
                    need(own.n)
                    dve.tensor_tensor(seen[:, :], seen[:, :], maskf[:, q, :], ALU.add).then_inc(s["lmax"], 1)
                if (g, rnd) == (3, 1):
                    dve.wait_ge(s["lexp"], of(mo, "lexp", b))
                    marked_m[0] = own.mark(dve.reciprocal(rsum[:, q, :], esum[:, q, :]))
                if (g, rnd) == (3, 2):
                    need(marked_m[0])
                    marked_m[0] = own.mark(dve.scalar_tensor_tensor(pr[:, q, :], el[:, q, :], rsum[:, q, :],
                                                                    maskf[:, q, :], ALU.mult, ALU.mult))
                if (g, rnd) == (3, 3):
                    hold(dve, s["cnt"], of(mo, "cnt", b))
                    need(marked_m[0])
                    dve.scalar_tensor_tensor(gates[:, q, :], cnt_sb[:, :], float(CAPACITY), pr[:, q, :],
                                             ALU.is_lt, ALU.mult).then_inc(s["gates"], 1)

            def attention(ph, before, marks, begun=False):
                layer = LAYER.get(ph)

                def maximum(b, g):
                    dve.wait_ge(s["s_ps"], of(ph, "s_ps", b, g + 1))
                    scores = S_BANK[g % 2][:, :].rearrange("p (j k) -> p j k", j=GH)
                    return own.mark(dve.tensor_reduce(mx[:, g, :], scores, AX, ALU.max))

                def shift(b, g, n):
                    hold(dve, s["pt_ps"], of(ph, "pt_ps", b, g + 1 - 4))
                    need(n)
                    scores = S_BANK[g % 2][:, :].rearrange("p (j k) -> p j k", j=GH)
                    dve.tensor_tensor(p_sb[:, g, :, :], scores, mx[:, g, :].unsqueeze(2).to_broadcast([P, GH, P]),
                                      ALU.subtract).then_inc(s["sx"], 1)

                def step(b, p, has):
                    for g in range(NG):
                        if has(0):
                            n = maximum(b, g)
                        if g == 0 and has(2):
                            if before:
                                hold(dve, s["x"], of(before, "x", b + 2))
                            m = own.mark(dve.bn_stats(stats[:, p, :], xb_of(b + 2)))
                        if g == 2 and has(2):
                            scaled(ph, b + 2, p).then_inc(s["xn"], 1)
                        if g == 3 and has(-2) and layer is not None:
                            t = add_bias_row(ph, b - 2, p, R_BANK)
                        if has(0):
                            shift(b, g, n)
                        if g == 0 and has(-2):
                            dve.wait_ge(s["oq_ps"], of(ph, "oq_ps", b - 2))
                            o = W_BANK[:, :].rearrange("p (h v) -> p h v", h=NH)
                            r = own.mark(dve.reciprocal(rden[:, p, :], o[:, :, DK]))
                        if g == 0 and has(2):
                            need_alone(m)
                            m = own.mark(dve.bn_aggr(mv[:, p, :], stats[:, p, :]))
                        if g == 0 and has(-2):
                            need(r)
                            dve.tensor_tensor(on[:, p, :].rearrange("p (h d) -> p h d", h=NH), o[:, :, 0:DK],
                                              rden[:, p, :].unsqueeze(2).to_broadcast([P, NH, DK]), ALU.mult)\
                               .then_inc(s["on"], 1)
                        if g == 0 and has(2):
                            need(m)
                            dve.tensor_scalar(ve[:, p, :], mv[:, p, 1:2], LN_EPS, None, ALU.add).then_inc(s["var"], 1)
                        if g == 0 and has(-2) and layer is None:
                            add(ph, b - 2, p, R_BANK)
                        if g == 3 and has(-2) and layer is not None:
                            need(t)
                            dve.tensor_tensor(xb_of(b - 2), xb_of(b - 2), t_row[:, p, :], ALU.add).then_inc(s["x"], 1)
                        if ph == "attn1" and isinstance(b, int):
                            def rounds(g, r0, r1):
                                for rnd in range(r0, r1):
                                    begin_experts("moe1", 0, 0, g, rnd, ph)

                            if (b, g) == (B, 0):
                                own.mark(dve.memset(lrow[:, :, E:E + 6], PAD))
                                own.mark(dve.memset(pick8[:, :, TOPK_E:8], PAD))
                                need(own.mark(dve.memset(seen[:, :], 0.0)))
                                rounds(0, 0, ROUNDS)
                            if (b, g) == (B, 1):
                                rounds(1, 0, 1)
                            if (b, g) == (B + 1, 0):
                                rounds(2, 0, ROUNDS)
                        if ph == "attn0" and isinstance(b, int):
                            if (b, g) == (B, 0):
                                for k in range(2):
                                    moments("bit0", k, k, (s["x"], of(ph, "x", k)))
                            if (b, g) == (B, 1):
                                quantize_input("bit0", 0, 0)
                            if (b, g) == (B, 2):
                                dve.wait_ge(s["vc"], of(ph, "vc", B - 1))
                                dve.wait_ge(ld_small, SMALL)
                                values(1, (A_BANK, R_BANK))
                        if ph == "attn3" and isinstance(b, int):
                            if (b, g) == (B, 0):
                                own.mark(dve.memset(lrow[:, :, E:E + 6], PAD))
                                need(own.mark(dve.memset(pick8[:, :, TOPK_E:8], PAD)))
                                moments("moe3", 0, 0, (s["x"], of(ph, "x", 0)))
                            if (b, g) == (B, 1):
                                scaled("moe3", 0, 0).then_inc(s["xn"], 1)
                            if (b, g) == (B + 1, 0):
                                moe_maximum("moe3", 0, 0)

                if not begun:
                    for b in range(LAG):
                        moments(ph, b, b, (s["x"], of(before, "x", b)) if before else None)
                        scaled(ph, b, b).then_inc(s["xn"], 1)
                batches(dve, step, LAG, LAG, own, marks)
                if ph == "attn1":
                    for rnd in range(1, ROUNDS):
                        begin_experts("moe1", 0, 0, 3, rnd, ph)

            def token_moments(before, b0, b1):
                for b in range(b0, b1):
                    dve.wait_ge(s["x"], of(before, "x", b))
                    n = own.mark(dve.bn_stats(stats_all[:, b, :], x_res[:, b, :]))
                need(n)
                for b in range(b0, b1):
                    n = own.mark(dve.bn_aggr(mv_all[:, b, :], stats_all[:, b, :]))
                need(n)
                dve.tensor_scalar(ve_all[:, b0:b1], mv_all[:, b0:b1, 1], LN_EPS, None, ALU.add).then_inc(var_all, 1)

            def token_norms(before, b0, b1):
                dve.wait_ge(rstd_all_ready, 1 if b0 == 0 else 2)
                if b0 == 0:
                    dve.wait_ge(s["pt_ps"], of(before, "pt_ps", B - 1, B // GH))
                for b in range(b0, b1):
                    dve.tensor_scalar(xn8[:, b, :], x_res[:, b, :], mv_all[:, b, 0:1], rstd_all[:, b:b + 1],
                                      ALU.subtract, ALU.mult).then_inc(s["xn"], 1)

            def experts_and_attention(mo, at, before, marks):
                layer = LAYER[at]

                def search(b, g, between):
                    r = g % 2
                    if b is not None:
                        hold(dve, s["ss"], of(at, "ss", b, g + 1))
                    taken = [None] * GH
                    for rnd in range(ROUNDS):
                        if b is not None:
                            src = ss if rnd == 0 else sel
                            found = [None] * GH
                            for j in range(GH):
                                if rnd > 0 and j % 2 == 0:
                                    need_alone(taken[j + 1])
                                found[j] = own.mark(dve.max(v8[:, r, j, rnd, :], src[:, r, j, :]))
                            if rnd == 0:
                                hold(dve, s["psel"], of(at, "psel", b, g + 1 - 2))
                            for j in range(GH):
                                if j % 2 == 0:
                                    need_alone(found[j + 1])
                                taken[j] = own.mark(dve.match_replace(sel[:, r, j, :], v8[:, r, j, rnd, :], src[:, r, j, :],
                                                                      TAKEN))
                        between(g, rnd)
                    if b is not None:
                        need(taken[-1])
                        dve.sem_inc(s["topk"], 1)

                def step(b, p, has):
                    q = 1 - p

                    def between(g, rnd):
                        if has(3):
                            begin_experts(mo, b + 3, q, g, rnd, before)
                        if has(1):
                            if (g, rnd) == (1, 0):
                                hold(dve, s["xm"], of(mo, "xm", b + 1, E + 1))
                                marked["a"] = own.mark(dve.bn_stats(stats[:, q, :], xb_of(b + 1)))
                            if (g, rnd) == (1, 1):
                                need_alone(marked["a"])
                                marked["a"] = own.mark(dve.bn_aggr(mv[:, q, :], stats[:, q, :]))
                            if (g, rnd) == (1, 2):
                                need(marked["a"])
                                dve.tensor_scalar(ve[:, q, :], mv[:, q, 1:2], LN_EPS, None, ALU.add).then_inc(s["var"], 1)
                            if (g, rnd) == (2, 0):
                                scaled(at, b + 1, q).then_inc(s["xn"], 1)

                    marked = {}
                    if isinstance(b, int) and b == -1:
                        values(2, (bank[4], bank[1]))
                    for g in range(NG):
                        search(b if has(0) else None, g, between)
                        if g == 2 and not has(0) and has(-1):
                            token_moments(at, 0, B - 1)
                            token_norms(at, 0, B - 1)
                        if g == 2 and has(-1):
                            normalize(at, b - 1, q, W2_BANK)
                        if g == 3 and has(-1):
                            add(at, b - 1, q, W2_BANK)

                batches(dve, step, LEAD, 1, own, marks, first=1 - LEAD)

            def bitffn(ph, before, marks):
                def step(b, p, has):
                    q = 1 - p
                    if has(1):
                        quantize_input(ph, b + 1, q)
                    if has(0) and not has(1):
                        for k in range(LAG):
                            moments("attn1", k, k, (s["x"], of(ph, "x", k)))
                    if has(0):
                        dve.wait_ge(s["gate"], of(ph, "gate", b))
                        dve.scalar_tensor_tensor(h0[:, p, :], S_BANK[2 * p + 1][:, :], deq[:, p, 1:2],
                                                 gate[:, p, :], ALU.mult, ALU.mult).then_inc(s["h0"], 1)
                    if has(2):
                        moments(ph, b + 2, p, (s["x"], of(before, "x", b + 2)))
                    if has(0):
                        dve.wait_ge(s["h0"], of(ph, "h0", b))
                        m = magnitude(h0[:, p, :], p, 1)
                    if has(0) and not has(1):
                        for k in range(LAG):
                            scaled("attn1", k, k).then_inc(s["xn"], 1)
                    if has(-1):
                        dve.wait_ge(s["dn_ps"], of(ph, "dn_ps", b - 1))
                        dve.scalar_tensor_tensor(xb_of(b - 1), O_BANK[:, 0:D], deq[:, q, 2:3], xb_of(b - 1), ALU.mult,
                                                 ALU.add).then_inc(s["x"], 1)
                    if has(0):
                        need(m)
                        m = clipped(p, 1)
                        need(m)
                        m = scales(p, 1)
                        need(m)
                        m = rounded(gate[:, p, :], h0[:, p, :], p, 1)
                        need(m)
                        dve.tensor_scalar(hq[:, p, :], gate[:, p, :], ROUND, None, ALU.subtract).then_inc(s["h"], 1)

                batches(dve, step, 2, 2, own, marks)

            def moe(ph, before, marks):
                def add_bias(b):
                    dve.wait_ge(s["b2_ps"], of(ph, "b2_ps", b))
                    dve.tensor_tensor(xb_of(b), xb_of(b), O_BANK[:, 0:D], ALU.add).then_inc(s["bias"], 1)

                def add_expert(b, p, e):
                    hold(dve, s["y_ps"], of(ph, "y_ps", b, e + 1))
                    if e == 0:
                        dve.wait_ge(s["bias"], of(ph, "bias", b))
                    else:
                        dve.wait_ge(s["acc"], of(ph, "acc", b, e))
                    dve.scalar_tensor_tensor(xb_of(b), Y_BANK[e % 2][:, 0:D], gates[:, p, e:e + 1], xb_of(b),
                                             ALU.mult, ALU.add).then_inc(s["acc"], 1)

                def step(b, p, has):
                    for e in range(E):
                        if has(0 if e >= 3 else -1):
                            add_expert(*((b, p, e - 3) if e >= 3 else (b - 1, 1 - p, e - 3 + E)))
                        if e == 2 and has(-1):
                            dve.wait_ge(s["acc"], of(ph, "acc", b - 1, E))
                            dve.sem_inc(s["x"], 1)
                        if e == 2 and has(0):
                            add_bias(b)
                        if e == 1 and has(1):
                            moments(ph, b + 1, 1 - p)
                        if e == 2 and has(1):
                            scaled(ph, b + 1, 1 - p).then_inc(s["xn"], 1)
                        if e == 4 and has(1):
                            moe_maximum(ph, b + 1, 1 - p)
                        if e == 6 and has(1):
                            moe_gates(ph, b + 1, 1 - p)

                for b in range(B):
                    hold(dve, s["x"], of(before, "x", b))
                moe_gates(ph, 0, 0)
                batches(dve, step, 1, 1, own, marks)

            def choose_tokens(ph, before):
                token_moments(before, B - 1, B)
                token_norms(before, B - 1, B)
                dve.wait_ge(lg_all_ps, 1)
                n = own.mark(dve.tensor_tensor(lg_all[:, :, :], bank[0][:, 0:B * E].rearrange("p (b e) -> p b e", e=E),
                                               br_row[:, :].unsqueeze(1).to_broadcast([P, B, E]), ALU.add))
                need(n)
                n = own.mark(dve.tensor_reduce(lmax_all[:, :], lg_all[:, :, :], AX, ALU.max))
                need(n)
                dve.tensor_tensor(lg_all[:, :, :], lg_all[:, :, :], lmax_all[:, :].unsqueeze(2).to_broadcast([P, B, E]),
                                  ALU.subtract).then_inc(lg_all_ready, 1)
                dve.wait_ge(lexp_all, 1)
                n = own.mark(dve.tensor_reduce(lsum_all[:, :], prob[:, :, :], AX, ALU.add))
                need(n)
                n = own.mark(dve.reciprocal(rsum_all[:, :], lsum_all[:, :]))
                need(n)
                dve.tensor_tensor(prob[:, :, :], prob[:, :, :], rsum_all[:, :].unsqueeze(2).to_broadcast([P, B, E]),
                                  ALU.mult).then_inc(prob_ready, 1)
                dve.wait_ge(probT_ready, 1)
                for rnd in range(EC_K // 8):
                    src = probT if rnd == 0 else takenT
                    n = own.mark(dve.max(ec8[:, rnd % 2, :], src))
                    need(n)
                    n = own.mark(dve.match_replace(takenT, ec8[:, rnd % 2, :], src, TAKEN))
                    need(n)
                n = own.mark(dve.tensor_scalar(takenT, takenT, TAKEN, None, ALU.is_equal))
                need(n)
                dve.sem_inc(taken_ready, 1)
                values(3)
                dve.wait_ge(taken_ready, 1)
                dve.tensor_tensor(probT, probT, takenT, ALU.mult).then_inc(gT_all_ready, 1)
                dve.wait_ge(taken_ps, 1)
                dve.tensor_tensor(gates_all[:, :, :], prob[:, :, :], bank[3][:, 0:B * E].rearrange("p (b e) -> p b e", e=E),
                                  ALU.mult).then_inc(ec_gates, 1)

            def expert_choice(ph):
                dve.wait_ge(ec_gates, 1)
                def batch(b, then):
                    dve.wait_ge(s["b2_ps"], of(ph, "b2_ps", b))
                    n = own.mark(dve.tensor_tensor(xb_of(b), xb_of(b), O_BANK[:, 0:D], ALU.add))
                    for g in range(NEG):
                        dve.wait_ge(s["y_ps"], of(ph, "y_ps", b, g + 1))
                        for e in range(EGRP):
                            if e == 0 and g > 0:
                                hold(dve, s["acc"], of(ph, "acc", b, g))
                            else:
                                need_alone(n)
                            gcol = gates_all[:, bass.ds(b, 1), EGRP * g + e:EGRP * g + e + 1].rearrange("p b e -> p (b e)")
                            ins = dve.scalar_tensor_tensor(xb_of(b), Y_BANK[g % 2][:, D * e:D * (e + 1)], gcol, xb_of(b),
                                                           ALU.mult, ALU.add)
                            if e == 0:
                                n = own.mark(ins)
                            else:
                                ins.then_inc(s["acc"], 1)
                        then(b, g)
                    dve.wait_ge(s["acc"], of(ph, "acc", b, NEG))
                    dve.sem_inc(s["x"], 1)

                def begin(b, g):
                    if b == B - 2 and g >= NEG - 2:
                        k = g - (NEG - 2)
                        moments("attn3", k, k, (s["x"], of(ph, "x", k)))
                    if b == B - 1 and g < 2:
                        scaled("attn3", g, g).then_inc(s["xn"], 1)

                with dve.Fori(0, (B - 2) // 2) as it:
                    own.turn(it, 2 * (1 + NEG))
                    for u in range(2):
                        batch(it * 2 + u, lambda b, g: None)
                own.done((B - 2) // 2)
                for b in range(B - 2, B):
                    batch(b, begin)

            dve.wait_ge(ld_ctx, 16)
            dve.wait_ge(v_ones, 1)
            dve.tensor_copy(v_aug[:, :, :, 0:DK], ctx_tok[:, :, :].rearrange("p b (h d) -> p b h d", h=NH))\
               .then_inc(v0_ready, 1)
            dve.wait_ge(const_ready, 1)
            n = own.mark(dve.tensor_reduce(head_mask[:, :], ident[:, :].rearrange("p (a j d) -> p j a d", a=NPART, j=GH),
                                           mybir.AxisListType.XY, ALU.add))
            dve.wait_ge(ld_x, 16)
            for b in range(LAG):
                moments("attn0", b, b)
                scaled("attn0", b, b).then_inc(s["xn"], 1)

            def mask_keys(b):
                dve.wait_ge(k0_split, b + 1)
                dve.wait_ge(k0_lower, b + 1)
                for j in range(GH // 2):
                    ins = dve.tensor_scalar(k_st[:, j, :, b, :], k_part[:, :, P * b:P * (b + 1)], head_mask[:, j:j + 1],
                                            None, ALU.mult)
                ins.then_inc(k0_masked, 1)

            def scale_queries(layer):
                dve.wait_ge(tr_ps, 3 + layer)
                wt = bank[2 + layer][:, 0:P].rearrange("p (g f) -> p g f", g=NG)
                for part in range(NPART):
                    if layer == 2:
                        scale = itemp_row[:, :].rearrange("p (g j o) -> p g j o", g=NG, o=1).to_broadcast([P, NG, GH, DK])
                        ins = dve.tensor_tensor(wq_rep[:, layer, :, part, :].rearrange("p g (j d) -> p g j d", d=DK),
                                                wt.rearrange("p g (j d) -> p g j d", d=DK), scale, ALU.mult)
                    else:
                        ins = dve.tensor_copy(wq_rep[:, layer, :, part, :], wt)
                ins.then_inc(w_ready, 1)

            def scale_weights():
                dve.wait_ge(wtot_ps, 1)
                n = own.mark(dve.tensor_scalar(wstat[:, 1, :], bank[5][:, 0:3], 1.0 / (F * D), QMIN, ALU.mult, ALU.max))
                need(n)
                need(own.mark(dve.reciprocal(wstat[:, 2, :], wstat[:, 1, :])))

            def quantize_weights(m):
                n = own.mark(dve.tensor_scalar(wb_raw[:, m, :], wb_raw[:, m, :], wstat[:, 2, m:m + 1], ROUND,
                                               ALU.mult, ALU.add))
                need(n)
                n = own.mark(dve.tensor_scalar(wb_raw[:, m, :], wb_raw[:, m, :], ROUND, 1.0, ALU.subtract, ALU.min))
                need(n)
                dve.tensor_scalar(wb_q[:, m, :], wb_raw[:, m, :], -1.0, None, ALU.max).then_inc(wb_ready, 1)

            dve.wait_ge(ld_w, 16 * 13)
            need(own.mark(dve.reciprocal(itemp_row[:, :], temp_row[:, :])))
            rows = slice(GW, 2 * GW)
            for b in range(B):
                part = k_part[:, :, P * b:P * (b + 1)]
                dve.wait_ge(k_evac, b + 1)
                dve.tensor_copy(part, k_raw[:, b % 2, :, :]).then_inc(k0_upper, 1)
                dve.wait_ge(k0_upper, b + 1)
                dve.tensor_tensor(part[rows], k_raw[rows, b % 2, :, :], part[rows], ALU.subtract).then_inc(k0_split, 1)
                if b >= 1:
                    mask_keys(b - 1)
                if b < 3:
                    scale_queries(b)
                if b == HB:
                    scale_weights()
                if HB < b < B - 1:
                    quantize_weights(b - HB - 1)
            mask_keys(B - 1)
            quantize_weights(2)
            attention("attn0", None, MARKS["attn0"], begun=True)
            dve.wait_ge(ld_small, SMALL)
            n = own.mark(dve.reciprocal(itemp_rep[:, :], temp_rep[:, :]))
            need(n)
            n = own.mark(dve.tensor_tensor(bq_rep[:, 2, :], bq_rep[:, 2, :], itemp_rep[:, :], ALU.mult))
            bitffn("bit0", "attn0", MARKS["bit0"])
            attention("attn1", "bit0", MARKS["attn1"], begun=True)
            experts_and_attention("moe1", "attn2", "attn1", MARKS["attn2"])
            choose_tokens("ecr2", "attn2")
            expert_choice("ec2")
            attention("attn3", "ec2", MARKS["attn3"], begun=True)
            moe("moe3", "attn3", MARKS["moe3"])


NORM, SHIFT, ROWS = 2, NG, 1
MARKS = {
    "attn0": 2 * (NORM + SHIFT + ROWS),
    "attn1": 2 * (NORM + SHIFT + ROWS + 1),
    "attn3": 2 * (NORM + SHIFT + ROWS + 1),
    "attn2": 2 * (2 * NORM + 9 + ROWS + 1 + NG * ROUNDS * GH * 2),
    "bit0": 2 * (NORM + 5 + 2 + 3 + 1 + 1),
    "moe3": 2 * (NORM + 6 + 5),
}

_OUT_SHAPE = (B, P, D)


def kernel(**inputs):
    import numpy as _np
    import concourse.bacc as _bacc
    from concourse import mybir as _mybir
    from concourse.bass_utils import run_bass_kernel_spmd as _run

    nc = _bacc.Bacc("TRN2", target_bir_lowering=False, num_devices=1)
    arrays, aps = {}, {}
    for name, value in inputs.items():
        arr = _np.ascontiguousarray(value)
        arrays["in_" + name] = arr
        aps[name] = nc.dram_tensor("in_" + name, arr.shape, _mybir.dt.from_np(arr.dtype), kind="ExternalInput").ap()
    out = nc.dram_tensor("out_0", _OUT_SHAPE, _mybir.dt.float32, kind="ExternalOutput").ap()
    build(nc, aps, out)
    r = _run(nc, [arrays], core_ids=[0])
    return r.results[0]["out_0"]
```
